# Optimizing a Trainium2 kernel written in Bass

```python
import numpy as np
import jax
import jax.numpy as jnp

def _softmax(x, axis=-1):
    return jax.nn.softmax(x, axis=axis)

def _gelu(x):
    return jax.nn.gelu(x, approximate=True)

def _silu(x):
    return jax.nn.silu(x)

def _sigmoid(x):
    return jax.nn.sigmoid(x)

def _layernorm(x, axis=-1, eps=1e-05):
    m = jnp.mean(x, axis=axis, keepdims=True)
    v = jnp.var(x, axis=axis, keepdims=True)
    return (x - m) / jnp.sqrt(v + eps)

def _scatter_add(tgt, idx, src, axis=0):
    return tgt.at[idx].add(src)

def _segment_sum(src, seg, n):
    return jax.ops.segment_sum(src, seg, n)
kernel_name = 'mk_xattn_ffn_d1_seqx_r2_7ba9de'

def setup_inputs(seed: int=0):
    np.random.seed(seed)
    _w = jnp.asarray

    def _rec_inputs():
        import jax
        import jax.numpy as jnp
        _rk = jax.random.key(seed)
        x = -0.0003929 + 0.9999 * jax.random.normal(jax.random.fold_in(_rk, 1), (2, 2048, 512), jnp.float32)
        _lenS = 2048 - jax.random.randint(jax.random.fold_in(_rk, 7), (2,), 0, max(1, 2048 // 4) + 1, jnp.int32)
        _lenS2 = 128 - jax.random.randint(jax.random.fold_in(_rk, 8), (2,), 0, max(1, 128 // 4) + 1, jnp.int32)
        _ctx_1024P = jax.random.normal(jax.random.fold_in(_rk, 11), (2, 16, 512), jnp.float32)
        _ctx_1024c = jax.random.dirichlet(jax.random.fold_in(_rk, 511), 0.3 * jnp.ones((16,), jnp.float32), (2, 128))
        _ctx_1024t = jnp.einsum('bsk,bkd->bsd', _ctx_1024c, _ctx_1024P)
        _ctx_1024t = _ctx_1024t * jax.lax.rsqrt(jnp.mean(jnp.square(_ctx_1024t)) + 1e-12) * 0.953939
        ctx_1024 = 2.81802e-05 + 1.00001 * (_ctx_1024t + 0.3 * jax.random.normal(jax.random.fold_in(_rk, 611), (2, 128, 512), jnp.float32))
        return (x, ctx_1024)
    x, ctx_1024 = _rec_inputs()

    def _L0_xattn_setup():
        import jax, jax.numpy as jnp
        import numpy as np
        B, S, E = (8, 1024, 512)
        EPS = 0.001

        def _layer_norm(x, gamma, beta):
            mu = jnp.mean(x, axis=-1, keepdims=True)
            var = jnp.mean(jnp.square(x - mu), axis=-1, keepdims=True)
            return gamma * (x - mu) * jax.lax.rsqrt(var + EPS) + beta

        def _attention(q_in, k_in, v_in, WQ, WK, WV, causal):
            Q = jnp.einsum('bse,ed->bsd', q_in, WQ)
            K = jnp.einsum('bse,ed->bsd', k_in, WK)
            V = jnp.einsum('bse,ed->bsd', v_in, WV)
            d = K.shape[-1]
            scores = jnp.einsum('bqd,bkd->bqk', Q, K) / jnp.sqrt(jnp.float32(d))
            if causal:
                qlen, klen = (scores.shape[-2], scores.shape[-1])
                mask = jnp.triu(jnp.ones((qlen, klen), bool), k=1)
                scores = jnp.where(mask[None], -jnp.inf, scores)
            p = jax.nn.softmax(scores, axis=-1)
            return jnp.einsum('bqk,bkd->bqd', p, V)
        key = jax.random.key(seed)
        ks = jax.random.split(key, 10)
        sc = 1.0 / np.sqrt(E)
        return {'inputs': jax.random.normal(ks[0], (B, S, E), jnp.float32), 'context': jax.random.normal(ks[1], (B, S, E), jnp.float32), 'Wq': jax.random.normal(ks[2], (E, E), jnp.float32) * sc, 'Wk': jax.random.normal(ks[3], (E, E), jnp.float32) * sc, 'Wv': jax.random.normal(ks[4], (E, E), jnp.float32) * sc, 'Wcq': jax.random.normal(ks[5], (E, E), jnp.float32) * sc, 'Wck': jax.random.normal(ks[6], (E, E), jnp.float32) * sc, 'Wcv': jax.random.normal(ks[7], (E, E), jnp.float32) * sc, 'gamma': jnp.ones((E,), jnp.float32), 'beta': jnp.zeros((E,), jnp.float32), 'W1': jax.random.normal(ks[8], (E, E), jnp.float32) * sc, 'b1': jnp.zeros((E,), jnp.float32)}
    _L0_xattn_all = _L0_xattn_setup()
    _L0_xattn_in = {k: v for k, v in _L0_xattn_all.items() if k in ('Wq', 'Wk', 'Wv', 'Wcq', 'Wck', 'Wcv', 'gamma', 'beta', 'W1', 'b1')}
    del _L0_xattn_all

    def _L0_ffn_setup():
        import jax, jax.numpy as jnp
        import numpy as np
        DIM = 512
        INTER = 512
        E = 32
        K = 4
        G = 8
        LG = 4
        ROUTE_SCALE = 1.0
        CAP_FACTOR = 1.25
        B, S = (4, 1024)

        def _gate(xf, wg):
            logits = xf @ wg.T
            scores = jax.nn.softmax(logits, axis=-1)
            sg = scores.reshape(-1, G, E // G)
            group_scores = sg.max(axis=-1)
            _, gtop = jax.lax.top_k(group_scores, LG)
            keep_g = jnp.sum(jax.nn.one_hot(gtop, G, dtype=jnp.float32), axis=1) > 0
            masked = jnp.where(keep_g[:, :, None], sg, -jnp.inf).reshape(-1, E)
            _, idx = jax.lax.top_k(masked, K)
            w = jnp.take_along_axis(scores, idx, axis=1)
            w = w / (w.sum(-1, keepdims=True) + 1e-09) * ROUTE_SCALE
            return (w.astype(xf.dtype), idx)

        def _forward(x, wg, w1, w2, w3, sw1, sw2, sw3):
            shape = x.shape
            xf = x.reshape(-1, DIM)
            N = xf.shape[0]
            cap = max(1, int(CAP_FACTOR * N * K / E))
            w, idx = _gate(xf, wg)
            fe = idx.reshape(-1)
            oh = jax.nn.one_hot(fe, E, dtype=jnp.int32)
            pos = (jnp.cumsum(oh, axis=0) * oh).sum(-1) - 1
            keep = pos < cap
            dest = jnp.where(keep, fe * cap + pos, E * cap)
            tok = jnp.arange(N * K, dtype=jnp.int32) // K
            buf_tok = jnp.full((E * cap + 1,), N, jnp.int32).at[dest].set(tok)[:-1]
            buf_w = jnp.zeros((E * cap + 1,), x.dtype).at[dest].set(w.reshape(-1))[:-1]
            xp = jnp.concatenate([xf, jnp.zeros((1, DIM), x.dtype)], axis=0)
            xe = xp[buf_tok].reshape(E, cap, DIM)
            h = jax.nn.silu(jnp.einsum('ecd,edh->ech', xe, w1)) * jnp.einsum('ecd,edh->ech', xe, w3)
            out = jnp.einsum('ech,ehd->ecd', h, w2) * buf_w.reshape(E, cap, 1)
            y = jnp.zeros((N + 1, DIM), x.dtype).at[buf_tok].add(out.reshape(E * cap, DIM))[:N]
            z = jax.nn.silu(xf @ sw1) * (xf @ sw3) @ sw2
            return (y + z).reshape(shape)
        key = jax.random.key(seed)
        ks = jax.random.split(key, 9)
        sd = DIM ** (-0.5)
        si = INTER ** (-0.5)
        x = jax.random.normal(ks[0], (B, S, DIM), jnp.float32)
        wg = jax.random.normal(ks[1], (E, DIM), jnp.float32) * sd
        w1 = jax.random.normal(ks[2], (E, DIM, INTER), jnp.float32) * sd
        w3 = jax.random.normal(ks[3], (E, DIM, INTER), jnp.float32) * sd
        w2 = jax.random.normal(ks[4], (E, INTER, DIM), jnp.float32) * si
        sw1 = jax.random.normal(ks[5], (DIM, INTER), jnp.float32) * sd
        sw3 = jax.random.normal(ks[6], (DIM, INTER), jnp.float32) * sd
        sw2 = jax.random.normal(ks[7], (INTER, DIM), jnp.float32) * si
        return dict(x=x, wg=wg, w1=w1, w2=w2, w3=w3, sw1=sw1, sw2=sw2, sw3=sw3)
    _L0_ffn_all = _L0_ffn_setup()
    _L0_ffn_in = {k: v for k, v in _L0_ffn_all.items() if k in ('wg', 'w1', 'w2', 'w3', 'sw1', 'sw2', 'sw3')}
    del _L0_ffn_all
    return {'x': x, 'ctx_1024': ctx_1024, 'L0_xattn_Wq': _L0_xattn_in['Wq'], 'L0_xattn_Wk': _L0_xattn_in['Wk'], 'L0_xattn_Wv': _L0_xattn_in['Wv'], 'L0_xattn_Wcq': _L0_xattn_in['Wcq'], 'L0_xattn_Wck': _L0_xattn_in['Wck'], 'L0_xattn_Wcv': _L0_xattn_in['Wcv'], 'L0_xattn_gamma': _L0_xattn_in['gamma'], 'L0_xattn_beta': _L0_xattn_in['beta'], 'L0_xattn_W1': _L0_xattn_in['W1'], 'L0_xattn_b1': _L0_xattn_in['b1'], 'L0_ffn_wg': _L0_ffn_in['wg'], 'L0_ffn_w1': _L0_ffn_in['w1'], 'L0_ffn_w2': _L0_ffn_in['w2'], 'L0_ffn_w3': _L0_ffn_in['w3'], 'L0_ffn_sw1': _L0_ffn_in['sw1'], 'L0_ffn_sw2': _L0_ffn_in['sw2'], 'L0_ffn_sw3': _L0_ffn_in['sw3']}

def reference(x, ctx_1024, L0_xattn_Wq, L0_xattn_Wk, L0_xattn_Wv, L0_xattn_Wcq, L0_xattn_Wck, L0_xattn_Wcv, L0_xattn_gamma, L0_xattn_beta, L0_xattn_W1, L0_xattn_b1, L0_ffn_wg, L0_ffn_w1, L0_ffn_w2, L0_ffn_w3, L0_ffn_sw1, L0_ffn_sw2, L0_ffn_sw3):
    import jax
    import jax.numpy as jnp

    def _L0_xattn_ref(inputs, context, Wq, Wk, Wv, Wcq, Wck, Wcv, gamma, beta, W1, b1):
        import jax, jax.numpy as jnp
        import numpy as np
        B, S, E = (8, 1024, 512)
        EPS = 0.001

        def _layer_norm(x, gamma, beta):
            mu = jnp.mean(x, axis=-1, keepdims=True)
            var = jnp.mean(jnp.square(x - mu), axis=-1, keepdims=True)
            return gamma * (x - mu) * jax.lax.rsqrt(var + EPS) + beta

        def _attention(q_in, k_in, v_in, WQ, WK, WV, causal):
            Q = jnp.einsum('bse,ed->bsd', q_in, WQ)
            K = jnp.einsum('bse,ed->bsd', k_in, WK)
            V = jnp.einsum('bse,ed->bsd', v_in, WV)
            d = K.shape[-1]
            scores = jnp.einsum('bqd,bkd->bqk', Q, K) / jnp.sqrt(jnp.float32(d))
            if causal:
                qlen, klen = (scores.shape[-2], scores.shape[-1])
                mask = jnp.triu(jnp.ones((qlen, klen), bool), k=1)
                scores = jnp.where(mask[None], -jnp.inf, scores)
            p = jax.nn.softmax(scores, axis=-1)
            return jnp.einsum('bqk,bkd->bqd', p, V)
        a = _attention(inputs, inputs, inputs, Wq, Wk, Wv, causal=True) + inputs
        h = _layer_norm(a, gamma, beta)
        c = _attention(h, context, context, Wcq, Wck, Wcv, causal=False) + h
        h = _layer_norm(c, gamma, beta)
        f = jax.nn.relu(jnp.einsum('bse,ed->bsd', h, W1) + b1)
        out = _layer_norm(f + h, gamma, beta)
        return jax.nn.relu(out)

    def _L0_ffn_ref(x, wg, w1, w2, w3, sw1, sw2, sw3):
        import jax, jax.numpy as jnp
        import numpy as np
        DIM = 512
        INTER = 512
        E = 32
        K = 4
        G = 8
        LG = 4
        ROUTE_SCALE = 1.0
        CAP_FACTOR = 1.25
        B, S = (4, 1024)

        def _gate(xf, wg):
            logits = xf @ wg.T
            scores = jax.nn.softmax(logits, axis=-1)
            sg = scores.reshape(-1, G, E // G)
            group_scores = sg.max(axis=-1)
            _, gtop = jax.lax.top_k(group_scores, LG)
            keep_g = jnp.sum(jax.nn.one_hot(gtop, G, dtype=jnp.float32), axis=1) > 0
            masked = jnp.where(keep_g[:, :, None], sg, -jnp.inf).reshape(-1, E)
            _, idx = jax.lax.top_k(masked, K)
            w = jnp.take_along_axis(scores, idx, axis=1)
            w = w / (w.sum(-1, keepdims=True) + 1e-09) * ROUTE_SCALE
            return (w.astype(xf.dtype), idx)

        def _forward(x, wg, w1, w2, w3, sw1, sw2, sw3):
            shape = x.shape
            xf = x.reshape(-1, DIM)
            N = xf.shape[0]
            cap = max(1, int(CAP_FACTOR * N * K / E))
            w, idx = _gate(xf, wg)
            fe = idx.reshape(-1)
            oh = jax.nn.one_hot(fe, E, dtype=jnp.int32)
            pos = (jnp.cumsum(oh, axis=0) * oh).sum(-1) - 1
            keep = pos < cap
            dest = jnp.where(keep, fe * cap + pos, E * cap)
            tok = jnp.arange(N * K, dtype=jnp.int32) // K
            buf_tok = jnp.full((E * cap + 1,), N, jnp.int32).at[dest].set(tok)[:-1]
            buf_w = jnp.zeros((E * cap + 1,), x.dtype).at[dest].set(w.reshape(-1))[:-1]
            xp = jnp.concatenate([xf, jnp.zeros((1, DIM), x.dtype)], axis=0)
            xe = xp[buf_tok].reshape(E, cap, DIM)
            h = jax.nn.silu(jnp.einsum('ecd,edh->ech', xe, w1)) * jnp.einsum('ecd,edh->ech', xe, w3)
            out = jnp.einsum('ech,ehd->ecd', h, w2) * buf_w.reshape(E, cap, 1)
            y = jnp.zeros((N + 1, DIM), x.dtype).at[buf_tok].add(out.reshape(E * cap, DIM))[:N]
            z = jax.nn.silu(xf @ sw1) * (xf @ sw3) @ sw2
            return (y + z).reshape(shape)
        return _forward(x, wg, w1, w2, w3, sw1, sw2, sw3)
    x = x + _L0_xattn_ref(_layernorm(x, axis=-1), ctx_1024, L0_xattn_Wq, L0_xattn_Wk, L0_xattn_Wv, L0_xattn_Wcq, L0_xattn_Wck, L0_xattn_Wcv, L0_xattn_gamma, L0_xattn_beta, L0_xattn_W1, L0_xattn_b1)
    x = x + _L0_ffn_ref(_layernorm(x, axis=-1), L0_ffn_wg, L0_ffn_w1, L0_ffn_w2, L0_ffn_w3, L0_ffn_sw1, L0_ffn_sw2, L0_ffn_sw3)
    return x

_drawn_inputs = setup_inputs


def setup_inputs(seed=0):
    import zlib

    import numpy as np

    out = dict(_drawn_inputs(seed))
    spreads = {'L0_xattn_gamma': (1.0, 0.2), 'L0_xattn_beta': (0.0, 0.1), 'L0_xattn_b1': (0.0, 0.1)}
    factors = {}
    for name, (base, spread) in spreads.items():
        noise = np.random.default_rng([zlib.crc32(name.encode()), seed]).standard_normal(out[name].shape)
        drawn = base * np.exp(spread * noise) if base else spread * noise
        out[name] = jnp.asarray(drawn.astype(out[name].dtype))
    for name, factor in factors.items():
        out[name] = (out[name] * factor).astype(out[name].dtype)
    return out
```

```python
from contextlib import ExitStack

import numpy as np
import concourse.bass as bass
from concourse import mybir

F32 = mybir.dt.float32
F32R = mybir.dt.float32r
I32 = mybir.dt.int32
U32 = mybir.dt.uint32
ALU = mybir.AluOpType
ACT = mybir.ActivationFunctionType
AX = mybir.AxisListType

P = 128
B, S, D = 2, 2048, 512
C = D // P
NT = B * S // P
GT = 4
GN = GT * P
G = S // GN
QT = S // P
KC = 128
E, TOPK, NG, KEEP_G = 32, 4, 8, 4
CAP = int(1.25 * B * S * TOPK / E)
ST = CAP // P
N = B * S
MASKED = -3.0e38
SCALE = float(D) ** -0.5
EPS_X, EPS_H = 1e-5, 1e-3
PASSES = 3


class Tally:

    def __init__(self, sem, base=0):
        self.sem, self.base, self.n = sem, base, 0

    def inc(self, ins, by=1):
        ins.then_inc(self.sem, by)
        self.n += by
        return self.n

    def wait(self, eng, n=None):
        eng.wait_ge(self.sem, self.base + (self.n if n is None else n))


def matmul(pe, out, lhsT, rhs, start, stop):
    if not isinstance(lhsT, tuple):
        return pe.matmul(out, lhsT, rhs, start=start, stop=stop)
    pe.matmul(out, lhsT[0], rhs[0], start=start, stop=False)
    pe.matmul(out, lhsT[0], rhs[1], start=False, stop=False)
    return pe.matmul(out, lhsT[1], rhs[0], start=False, stop=stop)


def kernel_program(nc, x, ctx_1024, Wq, Wk, Wv, Wcq, Wck, Wcv, gamma, beta, W1, b1,
                   wg, w1, w2, w3, sw1, sw2, sw3, out):
    a_dram = nc.dram_tensor("attended", (N, D), F32, kind="Internal").ap()
    xn_dram = nc.dram_tensor("xn2", (N + CAP, D), F32, kind="Internal").ap()
    y_dram = nc.dram_tensor("y0", (N + CAP, D), F32, kind="Internal").ap()
    x1_dram = nc.dram_tensor("x1", (N, D), F32, kind="Internal").ap()
    xnT_dram = nc.dram_tensor("xn2T", (NT // GT, P, C, GN), F32, kind="Internal").ap()
    table = nc.dram_tensor("slot_table", (E * CAP + N * TOPK, 2), I32, kind="Internal").ap()
    with ExitStack() as keep:
        def sb(name, shape, dt=F32, stack=keep):
            return stack.enter_context(nc.sbuf_tensor(name, shape, dt))

        k = {}
        k["ident"] = sb("ident", [P, P])
        k["iota"] = sb("iota_f", [P, E])
        k["score"] = sb("chosen_score", [P, NT, TOPK])
        k["expert"] = sb("chosen_expert", [P, NT, TOPK])
        with ExitStack() as early:
            k["neg_half"] = sb("neg_half", [P, GT], stack=early)
            k["G"] = sb("G_ctx", [P, C, B * KC], stack=early)
            k["Vc"] = sb("V_ctx", [P, B, D], stack=early)
            k["wgT"] = sb("wgT", [P, C, E], stack=early)
            with ExitStack() as att:
                k["causal"] = sb("causal", [P, P], stack=att)
                k["M"] = sb("M_qk", [P, C, D], stack=att)
                k["Wv"] = sb("Wv_sb", [P, C, D], stack=att)
                prepare(nc, k, ctx_1024, Wq, Wk, Wv, Wcq, Wck, Wcv, wg)
                attend(nc, k, x, a_dram)
            tokens(nc, k, x, a_dram, W1, gamma, beta, b1, x1_dram, xn_dram, xnT_dram, y_dram, table)
        dispatch(nc, k, sw1, sw2, sw3, x1_dram, xnT_dram, y_dram, table)
        experts(nc, k, w1, w2, w3, xn_dram, y_dram, table, out)


def prepare(nc, k, ctx_in, Wq, Wk, Wv, Wcq, Wck, Wcv, wg):
    ident, causal, M, Gc, Vc, wgT = (k[n] for n in ("ident", "causal", "M", "G", "Vc", "wgT"))
    with ExitStack() as ctx:
        def sb(name, shape, dt=F32):
            return ctx.enter_context(nc.sbuf_tensor(name, shape, dt))

        def sem(name):
            return ctx.enter_context(nc.semaphore(name))

        raw = {n: sb(f"raw_{n}", [P, C, D]) for n in ("Wq", "Wk", "Wcq", "Wck", "Wcv")}
        WqT, WkT, WcqT = (sb(n, [P, C, D]) for n in ("WqT", "WkT", "WcqT"))
        cx = sb("cx", [P, B, D])
        cxT = sb("cxT", [P, C, B * KC])
        KcT = sb("KcT", [P, C, B * KC])
        wg_sb = sb("wg_sb", [E, D])
        ps = ctx.enter_context(nc.psum_tensor("ps_prep", [P, 8, 512], F32))
        loaded = {n: sem(f"loaded_{n}") for n in ("Wq", "Wk", "Wv", "Wcq", "Wck", "Wcv", "cx", "wg")}
        iota_i = sb("iota_i", [P, E], I32)
        zeroed, const_ready = sem("zeroed"), sem("const_ready")
        filled, copied = sem("prep_filled"), sem("prep_copied")
        block = ctx.enter_context(nc.Block())

        @block.sync
        def _(sp):
            for n, w in (("Wq", Wq), ("Wk", Wk), ("Wcq", Wcq)):
                sp.dma_start(raw[n][:], w.rearrange("(c p) n -> p c n", p=P)).then_inc(loaded[n], 16)
            sp.dma_start(cx[:], ctx_in.rearrange("b p n -> p b n")).then_inc(loaded["cx"], 16)
            for n, w in (("Wck", Wck), ("Wcv", Wcv)):
                sp.dma_start(raw[n][:], w.rearrange("(c p) n -> p c n", p=P)).then_inc(loaded[n], 16)
            sp.dma_start(wg_sb[:], wg).then_inc(loaded["wg"], 16)
            sp.dma_start(k["Wv"][:], Wv.rearrange("(c p) n -> p c n", p=P)).then_inc(loaded["Wv"], 16)
            sp.wait_ge(loaded["Wv"], 16)

        @block.gpsimd
        def _(pool):
            pool.memset(ident[:], 0.0).then_inc(zeroed, 1)
            pool.memset(causal[:], 0.0).then_inc(zeroed, 1)
            pool.memset(k["neg_half"][:], -0.5).then_inc(const_ready, 1)
            pool.iota(iota_i[:], [[1, E]], base=0, channel_multiplier=0).then_inc(const_ready, 1)
            pool.wait_ge(zeroed, 2)
            pool.affine_select(out=ident[:], in_=ident[:], compare_op=ALU.not_equal, fill=1.0, base=0,
                               pattern=[[-1, P]], channel_multiplier=1).then_inc(const_ready, 1)
            pool.affine_select(out=causal[:], in_=causal[:], compare_op=ALU.is_ge, fill=MASKED, base=0,
                               pattern=[[-1, P]], channel_multiplier=1).then_inc(const_ready, 1)

        def bank(step, j):
            return ps[:, 4 * (step % 2) + j, :]

        @block.tensor
        def _(pe):
            pe.wait_ge(const_ready, 4)

            def turn(step, src, tiles):
                for c in range(C):
                    for r in range(tiles):
                        last = pe.transpose(bank(step, c)[:, r * P:(r + 1) * P],
                                            src[:, r, c * P:(c + 1) * P], ident[:])
                last.then_inc(filled, 1)

            pe.wait_ge(loaded["Wq"], 16)
            turn(0, raw["Wq"], C)
            pe.wait_ge(loaded["Wk"], 16)
            turn(1, raw["Wk"], C)
            pe.wait_ge(loaded["Wcq"], 16)
            pe.wait_ge(copied, 1)
            turn(2, raw["Wcq"], C)
            pe.wait_ge(loaded["cx"], 16)
            pe.wait_ge(copied, 2)
            turn(3, cx, B)
            pe.wait_ge(copied, 3)
            for r in range(C):
                for d in range(C):
                    last = pe.matmul(bank(4, r), WqT[:, d, r * P:(r + 1) * P], WkT[:, d, :],
                                     start=(d == 0), stop=(d == C - 1))
            last.then_inc(filled, 1)
            pe.wait_ge(loaded["Wck"], 16)
            pe.wait_ge(copied, 4)
            for r in range(C):
                for e in range(C):
                    last = pe.matmul(bank(5, r)[:, 0:B * KC], raw["Wck"][:, e, r * P:(r + 1) * P], cxT[:, e, :],
                                     start=(e == 0), stop=(e == C - 1))
            last.then_inc(filled, 1)
            pe.wait_ge(copied, 6)
            for r in range(C):
                for d in range(C):
                    last = pe.matmul(bank(6, r)[:, 0:B * KC], WcqT[:, d, r * P:(r + 1) * P], KcT[:, d, :],
                                     start=(d == 0), stop=(d == C - 1))
            last.then_inc(filled, 1)
            pe.wait_ge(loaded["Wcv"], 16)
            pe.wait_ge(loaded["wg"], 16)
            for b in range(B):
                for e in range(C):
                    pe.matmul(bank(7, b), cxT[:, e, b * KC:(b + 1) * KC], raw["Wcv"][:, e, :],
                              start=(e == 0), stop=(e == C - 1))
            for c in range(C):
                last = pe.transpose(bank(7, 2)[:, c * E:(c + 1) * E], wg_sb[:, c * P:(c + 1) * P],
                                    ident[0:E, 0:E])
            last.then_inc(filled, 1)

        @block.vector
        def _(dve):
            dve.wait_ge(const_ready, 4)
            dve.tensor_copy(k["iota"][:], iota_i[:])
            copies = [(WqT[:], 512), (WkT[:], 512), (WcqT[:], 512), (cxT[:], B * KC), (M[:], 512),
                      (KcT[:], B * KC), (Gc[:], B * KC)]
            for step, (dst, n) in enumerate(copies):
                dve.wait_ge(filled, step + 1)
                lo = 4 * (step % 2)
                dve.tensor_copy(dst, ps[:, lo:lo + 4, 0:n]).then_inc(copied, 1)
            dve.wait_ge(filled, 8)
            dve.tensor_copy(Vc[:], ps[:, 4:6, :]).then_inc(copied, 1)
            dve.tensor_copy(wgT[:], ps[:, 6, 0:C * E].rearrange("p (c e) -> p c e", c=C)).then_inc(copied, 1)


def wait_alone(eng, sem, value, passed):
    eng.wait_ge(sem, value)
    eng.sem_inc(passed, 1)


def ln_stats(dve, passed, stats_made, tiles, stats, mv, var_ready):
    for t, tile in enumerate(tiles):
        last = dve.bn_stats(stats[:, t, :], tile)
    wait_alone(dve, stats_made.sem, stats_made.base + stats_made.inc(last), passed)
    for t in range(len(tiles)):
        last = dve.bn_aggr(mv[:, t, :], stats[:, t, :])
    last.then_inc(var_ready, 1)


def ln_rstd(pool, rstd, veps, neg_half, mv, eps, eps_added, rstd_ready):
    pool.tensor_scalar(veps, mv[:, :, 1], eps, None, ALU.add).then_inc(eps_added.sem, 1)
    eps_added.n += 1
    eps_added.wait(pool)
    pool.tensor_tensor(rstd, veps, neg_half, ALU.pow).then_inc(rstd_ready, 1)


def attend(nc, k, x, a_dram):
    ident, causal, M, Wv = (k[n] for n in ("ident", "causal", "M", "Wv"))
    x_v = x.rearrange("b (g t p) d -> b g p t d", p=P, t=GT)
    a_v = a_dram.rearrange("(b q p) d -> b q p d", p=P, q=QT)
    with ExitStack() as ctx:
        def sb(name, shape, dt=F32):
            return ctx.enter_context(nc.sbuf_tensor(name, shape, dt))

        def sem(name):
            return ctx.enter_context(nc.semaphore(name))

        x_in = sb("x_in", [P, 2, GT, D])
        xn = sb("xn", [P, QT, D])
        xnT = sb("xnT", [P, C, S])
        V = sb("V", [P, QT, D])
        QMT = sb("QMT", [P, C, S])
        probs = sb("probs", [P, 2, S])
        probsT = sb("probsT", [P, 2, 512])
        a_sb = sb("a_sb", [P, 2, D])
        stats, mv, rstd, veps = (sb(n, s) for n, s in (
            ("stats", [P, GT, 6]), ("mv", [P, GT, 2]), ("rstd", [P, GT]), ("veps", [P, GT])))
        nmax, rsum, rinv = sb("nmax", [P, QT]), sb("rsum", [P, QT]), sb("rinv", [P, QT])
        ps = ctx.enter_context(nc.psum_tensor("ps_att", [P, 8, 512], F32))

        batch_free = sem("batch_free")
        x_loaded = [sem(f"x_loaded{i}") for i in range(2)]
        eps_added, max_linked, stats_made, var_ready, rstd_ready = (
            sem(n) for n in ("eps_added", "max_linked", "stats_made", "var_ready", "rstd_ready"))
        sp_passed, dve_passed, pool_passed = (sem(f"passed_{n}") for n in ("sp", "dve", "pool"))
        xn_ready, xn_turned, xnT_dve, xnT_act = sem("xn_ready"), sem("xn_turned"), sem("xnT_dve"), sem("xnT_act")
        q_made, q_copied, v_made, v_dve, v_act = (sem(n) for n in ("q_made", "q_copied", "v_made", "v_dve", "v_act"))
        scored, masked_max, exped, p_turned, p_copied, pv_used, pv_done, a_ready = (
            sem(n) for n in ("scored", "masked_max", "exped", "p_turned", "p_copied", "pv_used", "pv_done", "a_ready"))
        a_stored = [sem(f"a_stored{i}") for i in range(2)]
        block = ctx.enter_context(nc.Block())
        groups_of = [(q + GT) // GT for q in range(QT)]
        NPG = sum(groups_of)
        first_group = [sum(groups_of[:q]) for q in range(QT)]

        @block.sync
        def _(sp):
            with sp.Fori(0, B) as b:
                sp.sem_inc(batch_free, 1)
                for g in range(G):
                    if g >= 2:
                        wait_alone(sp, xn_ready, b * G + g - 1, sp_passed)
                    sp.dma_start(x_in[:, g % 2], x_v[bass.ds(b, 1), g].rearrange("b p t d -> (b p) t d")
                                 ).then_inc(x_loaded[g % 2], 16)
                for q in range(QT):
                    wait_alone(sp, a_ready, b * QT + q + 1, sp_passed)
                    sp.dma_start(a_v[bass.ds(b, 1), q].rearrange("b p d -> (b p) d"), a_sb[:, q % 2]
                                 ).then_inc(a_stored[q % 2], 16)
                for i in range(2):
                    wait_alone(sp, a_stored[i], b * (8 * QT) + 8 * QT, sp_passed)

        @block.tensor
        def _(pe):
            with pe.Fori(0, B) as b:
                pe.wait_ge(batch_free, b + 1)

                def turn(g):
                    pe.wait_ge(xn_ready, b * G + g + 1)
                    if g:
                        pe.wait_ge(xnT_dve, b * G + g)
                        pe.wait_ge(xnT_act, b * G + g)
                    for c in range(C):
                        for t in range(GT):
                            last = pe.transpose(ps[:, c, t * P:(t + 1) * P],
                                                xn[:, g * GT + t, c * P:(c + 1) * P], ident[:])
                    last.then_inc(xn_turned, 1)

                turn(0)
                for g in range(G):
                    pe.wait_ge(xnT_dve, b * G + g + 1)
                    pe.wait_ge(xnT_act, b * G + g + 1)
                    if g:
                        pe.wait_ge(v_dve, b * G + g)
                        pe.wait_ge(v_act, b * G + g)
                    for c in range(C):
                        for e in range(C):
                            last = matmul(pe, ps[:, 4 + c, :], M[:, e, c * P:(c + 1) * P],
                                          xnT[:, e, g * GN:(g + 1) * GN], e == 0, e == C - 1)
                    last.then_inc(q_made, 1)
                    if g + 1 < G:
                        turn(g + 1)
                    pe.wait_ge(q_copied, b * G + g + 1)
                    for t in range(GT):
                        for e in range(C):
                            last = matmul(pe, ps[:, 4 + t, :],
                                          xnT[:, e, (g * GT + t) * P:(g * GT + t + 1) * P],
                                          Wv[:, e, :], e == 0, e == C - 1)
                    last.then_inc(v_made, 1)

                def scores(q):
                    if q:
                        pe.wait_ge(exped, b * QT + q)
                    n = (q + 1) * P
                    for j in range(0, n, 512):
                        w = min(512, n - j)
                        for c in range(C):
                            last = matmul(pe, ps[:, j // 512, 0:w], QMT[:, c, q * P:(q + 1) * P],
                                          xnT[:, c, j:j + w], c == 0, c == C - 1)
                    last.then_inc(scored, 1)

                def turn_probs(q, j):
                    i = first_group[q] + j
                    if i >= 2:
                        pe.wait_ge(p_copied, b * NPG + i - 1)
                    for t in range(4 * j, min(4 * j + 4, q + 1)):
                        last = pe.transpose(ps[:, 4 + i % 2, (t % 4) * P:(t % 4 + 1) * P],
                                            probs[:, q % 2, t * P:(t + 1) * P], ident[:])
                    last.then_inc(p_turned, 1)

                def attended(q):
                    pe.wait_ge(exped, b * QT + q + 1)
                    if q >= 2:
                        pe.wait_ge(a_ready, b * QT + q - 1)
                    turn_probs(q, 0)
                    for j in range(groups_of[q]):
                        if j + 1 < groups_of[q]:
                            turn_probs(q, j + 1)
                        i = first_group[q] + j
                        pe.wait_ge(p_copied, b * NPG + i + 1)
                        for t in range(4 * j, min(4 * j + 4, q + 1)):
                            last = matmul(pe, ps[:, 6 + q % 2, :], probsT[:, i % 2, (t % 4) * P:(t % 4 + 1) * P],
                                          V[:, t, :], t == 0, t == q)
                        last.then_inc(pv_used, 1)

                pe.wait_ge(v_dve, b * G + G)
                pe.wait_ge(v_act, b * G + G)
                scores(0)
                for q in range(QT):
                    if q + 1 < QT:
                        scores(q + 1)
                    attended(q)

        @block.gpsimd
        def _(pool):
            with pool.Fori(0, B) as b:
                with_eps = Tally(eps_added, b * G)
                for g in range(G):
                    wait_alone(pool, var_ready, b * G + g + 1, pool_passed)
                    ln_rstd(pool, rstd[:], veps[:], k["neg_half"][:], mv, EPS_X, with_eps, rstd_ready)

        @block.vector
        def _(dve):
            with dve.Fori(0, B) as b:
                chain = Tally(max_linked, b * (2 * QT))
                in_stats = Tally(stats_made, b * G)

                def link(ins):
                    chain.inc(ins)
                    chain.wait(dve)

                dve.wait_ge(batch_free, b + 1)

                def norm(g):
                    dve.wait_ge(x_loaded[g % 2], b * (8 * G) + 16 * (g // 2 + 1))
                    ln_stats(dve, dve_passed, in_stats, [x_in[:, g % 2, t, :] for t in range(GT)],
                             stats, mv, var_ready)
                    dve.wait_ge(rstd_ready, b * G + g + 1)
                    for t in range(GT):
                        last = dve.tensor_scalar(xn[:, g * GT + t, :], x_in[:, g % 2, t, :], mv[:, t, 0:1],
                                                 rstd[:, t:t + 1], ALU.subtract, ALU.mult)
                    last.then_inc(xn_ready, 1)

                norm(0)
                for g in range(G):
                    dve.wait_ge(xn_turned, b * G + g + 1)
                    dve.tensor_copy(xnT[:, 0:2, g * GN:(g + 1) * GN], ps[:, 0:2, :]).then_inc(xnT_dve, 1)
                    if g + 1 < G:
                        norm(g + 1)
                    dve.wait_ge(v_made, b * G + g + 1)
                    dve.tensor_copy(V[:, g * GT:g * GT + 2, :], ps[:, 4:6, :]).then_inc(v_dve, 1)

                def softmax_max(q):
                    dve.wait_ge(scored, b * QT + q + 1)
                    col = q * P
                    diag = ps[:, col // 512, col % 512:col % 512 + P]
                    link(dve.tensor_tensor(diag, diag, causal[:], ALU.add))
                    flat = ps[:, 0:4, :].rearrange("p k n -> p (k n)")[:, 0:(q + 1) * P]
                    link(dve.tensor_reduce(nmax[:, q:q + 1], flat, AX.X, ALU.max))
                    dve.tensor_scalar(nmax[:, q:q + 1], nmax[:, q:q + 1], -SCALE, None,
                                      ALU.mult).then_inc(masked_max, 1)

                softmax_max(0)
                for q in range(QT):
                    if q + 1 < QT:
                        softmax_max(q + 1)
                    for j in range(groups_of[q]):
                        i = first_group[q] + j
                        dve.wait_ge(p_turned, b * NPG + i + 1)
                        if i >= 2:
                            dve.wait_ge(pv_used, b * NPG + i - 1)
                        w = min(512, (q + 1) * P - 512 * j)
                        dve.tensor_copy(probsT[:, i % 2, 0:w], ps[:, 4 + i % 2, 0:w]).then_inc(p_copied, 1)
                    dve.reciprocal(rinv[:, q:q + 1], rsum[:, q:q + 1]).then_inc(pv_done, 1)
                    dve.wait_ge(pv_done, b * QT + q + 1)
                    dve.wait_ge(pv_used, b * NPG + first_group[q] + groups_of[q])
                    if q >= 2:
                        dve.wait_ge(a_stored[q % 2], b * (8 * QT) + 16 * (q // 2))
                    dve.scalar_tensor_tensor(out=a_sb[:, q % 2], in0=ps[:, 6 + q % 2, :], scalar=rinv[:, q:q + 1],
                                             in1=xn[:, q, :], op0=ALU.mult, op1=ALU.add).then_inc(a_ready, 1)
                assert chain.n == 2 * QT and in_stats.n == G

        @block.scalar
        def _(act):
            with act.Fori(0, B) as b:
                act.wait_ge(batch_free, b + 1)
                for g in range(G):
                    act.wait_ge(xn_turned, b * G + g + 1)
                    act.copy(xnT[:, 2:4, g * GN:(g + 1) * GN], ps[:, 2:4, :]).then_inc(xnT_act, 1)
                    act.wait_ge(q_made, b * G + g + 1)
                    act.copy(QMT[:, :, g * GN:(g + 1) * GN], ps[:, 4:8, :]).then_inc(q_copied, 1)
                    act.wait_ge(v_made, b * G + g + 1)
                    act.copy(V[:, g * GT + 2:g * GT + 4, :], ps[:, 6:8, :]).then_inc(v_act, 1)
                for q in range(QT):
                    act.wait_ge(masked_max, b * QT + q + 1)
                    flat = ps[:, 0:4, :].rearrange("p k n -> p (k n)")[:, 0:(q + 1) * P]
                    act.activation(probs[:, q % 2, 0:(q + 1) * P], flat, ACT.Exp, bias=nmax[:, q:q + 1],
                                   scale=SCALE, accum_out=rsum[:, q:q + 1]).then_inc(exped, 1)


def tokens(nc, k, x, a_dram, W1, gamma, beta, b1, x1_dram, xn_dram, xnT_dram, y_dram, table):
    ident, Gc, Vc, wgT = (k[n] for n in ("ident", "G", "Vc", "wgT"))
    x_v = x.rearrange("b (g t p) d -> b g p t d", p=P, t=GT)
    a_v = a_dram.rearrange("(b g t p) d -> b g p t d", p=P, t=GT, g=G)
    x1_v = x1_dram.rearrange("(b g t p) d -> b g p t d", p=P, t=GT, g=G)
    xn_v = xn_dram[0:N, :].rearrange("(b g t p) d -> b g p t d", p=P, t=GT, g=G)
    xnT_v = xnT_dram.rearrange("(b g) p c n -> b g p c n", b=B)
    with ExitStack() as ctx:
        def sb(name, shape, dt=F32):
            return ctx.enter_context(nc.sbuf_tensor(name, shape, dt))

        def sem(name):
            return ctx.enter_context(nc.semaphore(name))

        A = [sb(f"A{u}", [P, GT, D]) for u in range(B)]
        H = [sb(f"H{u}", [P, GT, D]) for u in range(B)]
        X = [sb(f"X{u}", [P, GT, D]) for u in range(B)]
        T = [sb(f"T{u}", [P, C, GN]) for u in range(B)]
        W1_sb = sb("W1_sb", [P, C, D])
        gam, bet, b1_sb = sb("gam", [P, D]), sb("bet", [P, D]), sb("b1_sb", [P, D])
        zero = sb("zero", [P, D])
        spare = sb("spare_slots", [P, ST, 2], I32)
        probs = [sb(f"cprobs{u}", [P, GT, KC]) for u in range(B)]
        probsT = [sb(f"cprobsT{u}", [P, GT, P]) for u in range(B)]
        small = {}
        for n, shape in (("stats", [P, GT, 6]), ("mv", [P, GT, 2]), ("rstd", [P, GT]), ("veps", [P, GT]),
                         ("cmax", [P, GT]), ("csum", [P, GT]), ("cinv", [P, GT]), ("lmax", [P, GT]),
                         ("lsum", [P, GT]), ("linv", [P, GT]), ("lexp", [P, GT, E]), ("score", [P, GT, E]),
                         ("gmax", [P, GT, NG]), ("gtop", [P, GT, 8]), ("gidf", [P, GT, 8]),
                         ("hot", [P, GT, NG, KEEP_G]), ("keep", [P, GT, NG]), ("drop", [P, GT, NG]),
                         ("kept", [P, GT, E]), ("masked", [P, GT, E]), ("etop", [P, GT, 8])):
            small[n] = [sb(f"{n}{u}", shape) for u in range(B)]
        for n in ("gid", "eid"):
            small[n] = [sb(f"{n}{u}", [P, GT, 8], U32) for u in range(B)]
        ps = ctx.enter_context(nc.psum_tensor("ps_tok", [P, 8, 512], F32))

        names = ("turn_free w_loaded zeros_made spare_stored rows_made dve_linked stats_made var_ready "
                 "eps_added rstd_ready h_ready turned T_dve T_act cscored cmax_ready cexped cp_turned "
                 "cp_copied c_made f_made x1_ready xn_ready logits_made lmax_ready lexped chosen "
                 "sp_passed dve_passed pool_passed").split()
        s = {n: sem(n + "_t") for n in names}
        a_loaded, x_loaded, x1_stored, xn_stored, xnT_stored = (
            [sem(f"{n}{u}") for u in range(B)] for n in ("a_load", "x_load", "x1_store", "xn_store", "xnT_store"))
        block = ctx.enter_context(nc.Block())

        def bank(u, j):
            return ps[:, 4 * u + j, :]

        @block.sync
        def _(sp):
            sp.dma_start(W1_sb[:], W1.rearrange("(c p) n -> p c n", p=P)).then_inc(s["w_loaded"], 16)
            for dst, v in ((gam, gamma), (bet, beta), (b1_sb, b1)):
                sp.dma_start(dst[:], v.rearrange("(a n) -> a n", a=1).to_broadcast([P, D])
                             ).then_inc(s["w_loaded"], 16)
            with sp.Fori(0, G) as i:
                sp.sem_inc(s["turn_free"], 1)
                for u in range(B):
                    sp.dma_start(A[u][:], a_v[u, bass.ds(i, 1)].rearrange("g p t d -> (g p) t d")
                                 ).then_inc(a_loaded[u], 16)
                for u in range(B):
                    sp.dma_start(X[u][:], x_v[u, bass.ds(i, 1)].rearrange("g p t d -> (g p) t d")
                                 ).then_inc(x_loaded[u], 16)
                for u in range(B):
                    wait_alone(sp, s["x1_ready"], i * B + u + 1, s["sp_passed"])
                    sp.dma_start(x1_v[u, bass.ds(i, 1)].rearrange("g p t d -> (g p) t d"), X[u][:]
                                 ).then_inc(x1_stored[u], 16)
                for u in range(B):
                    wait_alone(sp, s["xn_ready"], i * B + u + 1, s["sp_passed"])
                    sp.dma_start(xn_v[u, bass.ds(i, 1)].rearrange("g p t d -> (g p) t d"), H[u][:]
                                 ).then_inc(xn_stored[u], 16)
                for u in range(B):
                    wait_alone(sp, s["T_dve"], i * (3 * B) + 2 * B + u + 1, s["sp_passed"])
                    wait_alone(sp, s["T_act"], i * (3 * B) + 2 * B + u + 1, s["sp_passed"])
                    sp.dma_start(xnT_v[u, bass.ds(i, 1)].rearrange("g p c n -> (g p) c n"), T[u][:]
                                 ).then_inc(xnT_stored[u], 16)
                for u in range(B):
                    wait_alone(sp, x1_stored[u], i * 16 + 16, s["sp_passed"])
                    wait_alone(sp, xn_stored[u], i * 16 + 16, s["sp_passed"])
                    wait_alone(sp, xnT_stored[u], i * 16 + 16, s["sp_passed"])
                wait_alone(sp, s["chosen"], i * B + B, s["sp_passed"])

        @block.gpsimd
        def _(pool):
            pool.memset(zero[:], 0.0).then_inc(s["zeros_made"], 1)
            pool.iota(spare[:, :, 0], [[1, ST]], base=N, channel_multiplier=ST).then_inc(s["zeros_made"], 1)
            pool.memset(spare[:, :, 1], 0).then_inc(s["zeros_made"], 1)
            pool.wait_ge(s["zeros_made"], 3)
            for dst in (xn_dram, y_dram):
                for t in range(ST):
                    pool.dma_start(dst[N + t * P:N + (t + 1) * P, :], zero[:]).then_inc(s["spare_stored"], 16)
            for e in range(E):
                pool.dma_start(table[e * CAP:(e + 1) * CAP, :].rearrange("(p t) w -> p (t w)", p=P),
                               spare[:].rearrange("p t w -> p (t w)")).then_inc(s["spare_stored"], 16)
            with pool.Fori(0, G) as i:
                with_eps = Tally(s["eps_added"], i * (4 * B))
                for n, eps in enumerate((EPS_H, EPS_H, EPS_H, EPS_X)):
                    for u in range(B):
                        wait_alone(pool, s["var_ready"], i * (4 * B) + n * B + u + 1, s["pool_passed"])
                        ln_rstd(pool, small["rstd"][u][:], small["veps"][u][:], k["neg_half"][:],
                                small["mv"][u], eps, with_eps, s["rstd_ready"])
            pool.wait_ge(s["spare_stored"], 16 * (2 * ST + E))

        @block.tensor
        def _(pe):
            pe.wait_ge(s["w_loaded"], 64)
            with pe.Fori(0, G) as i:
                pe.wait_ge(s["turn_free"], i + 1)

                def turn(n, u):
                    for c in range(C):
                        for t in range(GT):
                            last = pe.transpose(bank(u, c)[:, t * P:(t + 1) * P],
                                                H[u][:, t, c * P:(c + 1) * P], ident[:])
                    last.then_inc(s["turned"], 1)

                def T_ready(n, u):
                    pe.wait_ge(s["T_dve"], i * (3 * B) + n * B + u + 1)
                    pe.wait_ge(s["T_act"], i * (3 * B) + n * B + u + 1)

                for u in range(B):
                    pe.wait_ge(s["h_ready"], i * (2 * B) + u + 1)
                    turn(0, u)
                for u in range(B):
                    T_ready(0, u)
                    for t in range(GT):
                        for e in range(C):
                            last = pe.matmul(bank(u, 0)[:, t * KC:(t + 1) * KC], T[u][:, e, t * P:(t + 1) * P],
                                             Gc[:, e, u * KC:(u + 1) * KC], start=(e == 0), stop=(e == C - 1))
                    last.then_inc(s["cscored"], 1)
                for u in range(B):
                    pe.wait_ge(s["cexped"], i * B + u + 1)
                    for t in range(GT):
                        last = pe.transpose(bank(u, 1)[:, t * P:(t + 1) * P], probs[u][:, t, :], ident[:])
                    last.then_inc(s["cp_turned"], 1)
                for u in range(B):
                    pe.wait_ge(s["cp_copied"], i * B + u + 1)
                    for t in range(GT):
                        last = pe.matmul(bank(u, t), probsT[u][:, t, :], Vc[:, u, :], start=True, stop=True)
                    last.then_inc(s["c_made"], 1)
                for u in range(B):
                    pe.wait_ge(s["h_ready"], i * (2 * B) + B + u + 1)
                    turn(1, u)
                for u in range(B):
                    T_ready(1, u)
                    for t in range(GT):
                        for e in range(C):
                            last = pe.matmul(bank(u, t), T[u][:, e, t * P:(t + 1) * P], W1_sb[:, e, :],
                                             start=(e == 0), stop=(e == C - 1))
                    last.then_inc(s["f_made"], 1)
                for u in range(B):
                    pe.wait_ge(s["xn_ready"], i * B + u + 1)
                    turn(2, u)
                for u in range(B):
                    T_ready(2, u)
                    for t in range(GT):
                        for e in range(C):
                            last = pe.matmul(bank(u, 0)[:, t * E:(t + 1) * E], T[u][:, e, t * P:(t + 1) * P],
                                             wgT[:, e, :], start=(e == 0), stop=(e == C - 1))
                    last.then_inc(s["logits_made"], 1)

        @block.scalar
        def _(act):
            with act.Fori(0, G) as i:
                act.wait_ge(s["turn_free"], i + 1)

                def T_copy(n, u):
                    act.wait_ge(s["turned"], i * (3 * B) + n * B + u + 1)
                    act.copy(T[u][:, 2:4, :], ps[:, 4 * u + 2:4 * u + 4, :]).then_inc(s["T_act"], 1)

                for u in range(B):
                    T_copy(0, u)
                for u in range(B):
                    act.wait_ge(s["cmax_ready"], i * B + u + 1)
                    for t in range(GT):
                        last = act.activation(probs[u][:, t, :], bank(u, 0)[:, t * KC:(t + 1) * KC], ACT.Exp,
                                              bias=small["cmax"][u][:, t:t + 1], scale=SCALE,
                                              accum_out=small["csum"][u][:, t:t + 1])
                    last.then_inc(s["cexped"], 1)
                for u in range(B):
                    act.wait_ge(s["cp_turned"], i * B + u + 1)
                    act.copy(probsT[u][:].rearrange("p t n -> p (t n)"), bank(u, 1)).then_inc(s["cp_copied"], 1)
                for n in (1, 2):
                    for u in range(B):
                        T_copy(n, u)
                for u in range(B):
                    act.wait_ge(s["lmax_ready"], i * B + u + 1)
                    for t in range(GT):
                        last = act.activation(small["lexp"][u][:, t, :], bank(u, 0)[:, t * E:(t + 1) * E], ACT.Exp,
                                              bias=small["lmax"][u][:, t:t + 1], scale=1.0,
                                              accum_out=small["lsum"][u][:, t:t + 1])
                    last.then_inc(s["lexped"], 1)

        LINKS = 44
        @block.vector
        def _(dve):
            dve.wait_ge(s["w_loaded"], 64)
            with dve.Fori(0, G) as i:
                chain = Tally(s["dve_linked"], i * LINKS)
                in_stats = Tally(s["stats_made"], i * (4 * B))

                def link(ins):
                    chain.inc(ins)
                    chain.wait(dve)

                def link_alone(ins):
                    link(ins)
                    dve.sem_inc(s["dve_passed"], 1)

                def T_copy(n, u):
                    dve.wait_ge(s["turned"], i * (3 * B) + n * B + u + 1)
                    dve.tensor_copy(T[u][:, 0:2, :], ps[:, 4 * u:4 * u + 2, :]).then_inc(s["T_dve"], 1)

                def stats(u, src):
                    ln_stats(dve, s["dve_passed"], in_stats, [src[:, t, :] for t in range(GT)],
                             small["stats"][u], small["mv"][u], s["var_ready"])

                def norm(n, u, src, dst):
                    mv, rstd = small["mv"][u], small["rstd"][u]
                    dve.wait_ge(s["rstd_ready"], i * (4 * B) + n * B + u + 1)
                    for t in range(GT):
                        last = dve.scalar_tensor_tensor(out=dst[:, t, :], in0=src[:, t, :], scalar=mv[:, t, 0:1],
                                                        in1=gam[:], op0=ALU.subtract, op1=ALU.mult)
                    link(last)
                    for t in range(GT):
                        last = dve.scalar_tensor_tensor(out=dst[:, t, :], in0=dst[:, t, :], scalar=rstd[:, t:t + 1],
                                                        in1=bet[:], op0=ALU.mult, op1=ALU.add)
                    return last

                for u in range(B):
                    dve.wait_ge(a_loaded[u], i * 16 + 16)
                    stats(u, A[u])
                for u in range(B):
                    norm(0, u, A[u], H[u]).then_inc(s["h_ready"], 1)
                for u in range(B):
                    T_copy(0, u)
                for u in range(B):
                    dve.wait_ge(s["cscored"], i * B + u + 1)
                    link(dve.tensor_reduce(small["cmax"][u][:], bank(u, 0).rearrange("p (t n) -> p t n", t=GT),
                                           AX.X, ALU.max))
                    dve.tensor_scalar(small["cmax"][u][:], small["cmax"][u][:], -SCALE, None,
                                      ALU.mult).then_inc(s["cmax_ready"], 1)
                for u in range(B):
                    dve.wait_ge(s["cexped"], i * B + u + 1)
                    link(dve.reciprocal(small["cinv"][u][:], small["csum"][u][:]))
                    dve.wait_ge(s["c_made"], i * B + u + 1)
                    for t in range(GT):
                        last = dve.scalar_tensor_tensor(out=A[u][:, t, :], in0=bank(u, t),
                                                        scalar=small["cinv"][u][:, t:t + 1], in1=H[u][:, t, :],
                                                        op0=ALU.mult, op1=ALU.add)
                    link(last)
                    stats(u, A[u])
                for u in range(B):
                    norm(1, u, A[u], H[u]).then_inc(s["h_ready"], 1)
                for u in range(B):
                    T_copy(1, u)
                for u in range(B):
                    dve.wait_ge(s["f_made"], i * B + u + 1)
                    for t in range(GT):
                        last = dve.tensor_tensor(A[u][:, t, :], bank(u, t), b1_sb[:], ALU.add)
                    link(last)
                    for t in range(GT):
                        last = dve.scalar_tensor_tensor(out=A[u][:, t, :], in0=A[u][:, t, :], scalar=0.0,
                                                        in1=H[u][:, t, :], op0=ALU.max, op1=ALU.add)
                    link(last)
                    stats(u, A[u])
                for u in range(B):
                    link(norm(2, u, A[u], A[u]))
                    dve.wait_ge(x_loaded[u], i * 16 + 16)
                    for t in range(GT):
                        last = dve.scalar_tensor_tensor(out=X[u][:, t, :], in0=A[u][:, t, :], scalar=0.0,
                                                        in1=X[u][:, t, :], op0=ALU.max, op1=ALU.add)
                    last.then_inc(s["x1_ready"], 1)
                    dve.wait_ge(s["x1_ready"], i * B + u + 1)
                    stats(u, X[u])
                for u in range(B):
                    dve.wait_ge(s["rstd_ready"], i * (4 * B) + 3 * B + u + 1)
                    for t in range(GT):
                        last = dve.tensor_scalar(H[u][:, t, :], X[u][:, t, :], small["mv"][u][:, t, 0:1],
                                                 small["rstd"][u][:, t:t + 1], ALU.subtract, ALU.mult)
                    last.then_inc(s["xn_ready"], 1)
                for u in range(B):
                    T_copy(2, u)
                for u in range(B):
                    dve.wait_ge(s["logits_made"], i * B + u + 1)
                    lg = bank(u, 0)[:, 0:GT * E].rearrange("p (t e) -> p t e", t=GT)
                    link(dve.tensor_reduce(small["lmax"][u][:], lg, AX.X, ALU.max))
                    dve.tensor_scalar(small["lmax"][u][:], small["lmax"][u][:], -1.0, None,
                                      ALU.mult).then_inc(s["lmax_ready"], 1)
                for u in range(B):
                    m = {n: v[u] for n, v in small.items()}
                    dve.wait_ge(s["lexped"], i * B + u + 1)
                    link(dve.reciprocal(m["linv"][:], m["lsum"][:]))
                    link(dve.tensor_tensor(m["score"][:], m["lexp"][:],
                                           m["linv"][:].rearrange("p (t a) -> p t a", a=1).to_broadcast([P, GT, E]),
                                           ALU.mult))
                    link_alone(dve.tensor_reduce(m["gmax"][:].rearrange("p t g -> p (t g)"),
                                           m["score"][:].rearrange("p t (g a) -> p (t g) a", g=NG), AX.X, ALU.max))
                    for t in range(GT):
                        last = dve.max(m["gtop"][:, t, :], m["gmax"][:, t, :])
                    link_alone(last)
                    for t in range(GT):
                        last = dve.max_index(m["gid"][:, t, :], m["gtop"][:, t, :], m["gmax"][:, t, :])
                    link(last)
                    link(dve.tensor_copy(m["gidf"][:], m["gid"][:]))
                    for t in range(GT):
                        last = dve.tensor_tensor(
                            m["hot"][:, t, :, :],
                            m["gidf"][:, t, 0:KEEP_G].rearrange("p (a j) -> p a j", a=1).to_broadcast([P, NG, KEEP_G]),
                            k["iota"][:, 0:NG].rearrange("p (g a) -> p g a", a=1).to_broadcast([P, NG, KEEP_G]),
                            ALU.is_equal)
                    link(last)
                    link(dve.tensor_reduce(m["keep"][:], m["hot"][:], AX.X, ALU.add))
                    dve.tensor_scalar(m["drop"][:], m["keep"][:], -1.0, None, ALU.add)

                    def of_group(tile):
                        return tile[:].rearrange("p t (g a) -> p (t g) a", a=1).to_broadcast([P, GT * NG, E // NG])

                    link(dve.tensor_tensor(m["kept"][:].rearrange("p t (g a) -> p (t g) a", g=NG),
                                           m["score"][:].rearrange("p t (g a) -> p (t g) a", g=NG),
                                           of_group(m["keep"]), ALU.mult))
                    link_alone(dve.tensor_tensor(m["masked"][:].rearrange("p t (g a) -> p (t g) a", g=NG),
                                           m["kept"][:].rearrange("p t (g a) -> p (t g) a", g=NG),
                                           of_group(m["drop"]), ALU.add))
                    for t in range(GT):
                        last = dve.max(m["etop"][:, t, :], m["masked"][:, t, :])
                    link_alone(last)
                    for t in range(GT):
                        last = dve.max_index(m["eid"][:, t, :], m["etop"][:, t, :], m["masked"][:, t, :])
                    link(last)
                    tile = i * GT + u * (S // P)
                    dve.tensor_copy(k["score"][:, bass.ds(tile, GT), :], m["etop"][:, :, 0:TOPK])
                    dve.tensor_copy(k["expert"][:, bass.ds(tile, GT), :], m["eid"][:, :, 0:TOPK]
                                    ).then_inc(s["chosen"], 1)
                assert chain.n == LINKS and in_stats.n == 4 * B, (chain.n, in_stats.n)


def dispatch(nc, k, sw1, sw2, sw3, x1_dram, xnT_dram, y_dram, table):
    x1_v = x1_dram.rearrange("(g t p) d -> g p t d", p=P, t=GT)
    y_v = y_dram[0:N, :].rearrange("(g t p) d -> g p t d", p=P, t=GT)
    NGR = NT // GT
    with ExitStack() as ctx:
        def sb(name, shape, dt=F32):
            return ctx.enter_context(nc.sbuf_tensor(name, shape, dt))

        def sem(name):
            return ctx.enter_context(nc.semaphore(name))

        wraw = sb("sw_raw", [P, C, D])
        W = [tuple(sb(f"sw{m}_{part}", [P, C, D], F32R) for part in ("hi", "lo")) for m in range(3)]
        xT = [sb(f"xT{i}", [P, C, GN]) for i in range(2)]
        xTs = tuple(sb(f"xTs_{part}", [P, C, GN], F32R) for part in ("hi", "lo"))
        x1t = sb("x1t", [P, GT, D])
        yt = sb("yt", [P, GT, D])
        sil = sb("sil", [P, 2, GN])
        gate = sb("gate", [P, 2, GN])
        gs = tuple(sb(f"gs_{part}", [P, C, GN], F32R) for part in ("hi", "lo"))
        hot = sb("hot_all", [P, NT, TOPK, E])
        mask = sb("mask", [P, NT, E])
        prior = sb("prior", [P, NT, E])
        pos = sb("pos", [P, NT, E])
        prefix, ones = sb("prefix", [P, P]), sb("ones", [P, P])
        r = {n: sb(f"r_{n}", [P, NT, TOPK]) for n in ("pos", "keep", "slot", "away", "spare")}
        wsum, winv = sb("wsum", [P, NT]), sb("winv", [P, NT])
        slot = sb("slot", [P, NT, TOPK], I32)
        spare_i = sb("spare_i", [P, NT, TOPK], I32)
        pair = sb("pair", [P, NT, TOPK, 2], I32)
        ps = ctx.enter_context(nc.psum_tensor("ps_dis", [P, 8, 512], F32))

        names = ("sw_loaded sw_read sw_hi sw_split x_free x1_loaded y_stored tri_zero tri_made iotas_made linked "
                 "counted slots_ready scattered xs_hi xs_split sh_made silu_made gated gate_hi g_split "
                 "z_made y_ready sp_passed pool_passed dve_passed").split()
        s = {n: sem(n + "_d") for n in names}
        xT_loaded = [sem(f"xT_loaded{i}") for i in range(2)]
        block = ctx.enter_context(nc.Block())

        def pairs(eng, body):
            with eng.Fori(0, NGR // 2 - 1) as i:
                for v in range(2):
                    body(i, v, False)
            for v in range(2):
                body(NGR // 2 - 1, v, True)

        @block.sync
        def _(sp):
            def load_x(i, v):
                sp.dma_start(xT[v][:], xnT_dram[bass.ds(i * 2 + v, 1)].rearrange("g p c n -> (g p) c n")
                             ).then_inc(xT_loaded[v], 16)

            for m, w in enumerate((sw1, sw3, sw2)):
                if m:
                    sp.wait_ge(s["sw_split"], m)
                sp.dma_start(wraw[:], w.rearrange("(c p) n -> p c n", p=P)).then_inc(s["sw_loaded"], 16)
            for v in range(2):
                load_x(0, v)

            def body(i, v, last):
                n = i * 2 + v
                wait_alone(sp, s["y_ready"], n + 1, s["sp_passed"])
                sp.dma_start(x1t[:], x1_v[bass.ds(n, 1)].rearrange("g p t d -> (g p) t d")
                             ).then_inc(s["x1_loaded"], 16)
                if not last:
                    wait_alone(sp, s["xs_split"], n + 1, s["sp_passed"])
                    load_x(i + 1, v)

            pairs(sp, body)
            sp.wait_ge(s["y_stored"], 16 * (NGR + 1))

        @block.gpsimd
        def _(pool):
            pool.memset(prefix[:], 1.0).then_inc(s["tri_zero"], 1)
            pool.memset(ones[:], 1.0).then_inc(s["tri_made"], 1)
            pool.wait_ge(s["tri_zero"], 1)
            pool.affine_select(out=prefix[:], in_=prefix[:], compare_op=ALU.is_gt, fill=0.0, base=0,
                               pattern=[[1, P]], channel_multiplier=-1).then_inc(s["tri_made"], 1)
            pool.iota(spare_i[:], [[P * TOPK, NT], [1, TOPK]], base=E * CAP,
                      channel_multiplier=TOPK).then_inc(s["iotas_made"], 1)
            pool.iota(pair[:, :, :, 0], [[P, NT], [0, TOPK]], base=0,
                      channel_multiplier=1).then_inc(s["iotas_made"], 1)
            pool.wait_ge(s["slots_ready"], 2)
            for n in range(NT):
                for j in range(TOPK):
                    pool.indirect_dma_start(
                        out=table, out_offset=bass.IndirectOffsetOnAxis(ap=slot[:, n, j:j + 1], axis=0),
                        in_=pair[:, n, j, :], in_offset=None).then_inc(s["scattered"], 16)
            pool.wait_ge(s["scattered"], 16 * NT * TOPK)

        @block.tensor
        def _(pe):
            pe.wait_ge(s["tri_made"], 2)
            pe.wait_ge(s["linked"], 3)
            flat = mask[:].rearrange("p n e -> p (n e)")
            for j in range(2):
                half = flat[:, j * 512:(j + 1) * 512]
                pe.matmul(ps[:, j, :], prefix[:], half, start=True, stop=True)
                last = pe.matmul(ps[:, 2 + j, :], ones[:], half, start=True, stop=True)
            last.then_inc(s["counted"], 1)
            pe.wait_ge(s["sw_split"], 3)
            pe.wait_ge(s["slots_ready"], 1)

            def body(i, v, last):
                n = i * 2 + v
                pe.wait_ge(s["xs_split"], n + 1)
                for hc in range(C):
                    if hc >= 2:
                        pe.wait_ge(s["g_split"], n * C + hc - 1)
                    for m in range(2):
                        for e in range(C):
                            mm = matmul(pe, ps[:, 4 + 2 * (hc % 2) + m, :],
                                        tuple(w[:, e, hc * P:(hc + 1) * P] for w in W[m]),
                                        tuple(x[:, e, :] for x in xTs), e == 0, e == C - 1)
                    mm.then_inc(s["sh_made"], 1)
                pe.wait_ge(s["g_split"], n * C + C)
                pe.wait_ge(s["y_ready"], n + 1)
                for t in range(GT):
                    for hc in range(C):
                        mm = matmul(pe, ps[:, t, :], tuple(g[:, hc, t * P:(t + 1) * P] for g in gs),
                                    tuple(w[:, hc, :] for w in W[2]), hc == 0, hc == C - 1)
                mm.then_inc(s["z_made"], 1)

            pairs(pe, body)

        @block.scalar
        def _(act):
            for m in range(3):
                act.wait_ge(s["sw_loaded"], 16 * (m + 1))
                act.copy(W[m][0][:], wraw[:]).then_inc(s["sw_hi"], 1)
            act.wait_ge(xT_loaded[0], 16)
            act.copy(xTs[0][:], xT[0][:]).then_inc(s["xs_hi"], 1)

            def body(i, v, last):
                n = i * 2 + v
                for hc in range(C):
                    act.wait_ge(s["sh_made"], n * C + hc + 1)
                    act.activation(sil[:, hc % 2, :], ps[:, 4 + 2 * (hc % 2), :], ACT.Silu
                                   ).then_inc(s["silu_made"], 1)
                    act.wait_ge(s["gated"], n * C + hc + 1)
                    act.copy(gs[0][:, hc, :], gate[:, hc % 2, :]).then_inc(s["gate_hi"], 1)
                if not (last and v):
                    act.wait_ge(xT_loaded[1 - v], (i + v) * 16 + 16)
                    act.copy(xTs[0][:], xT[1 - v][:]).then_inc(s["xs_hi"], 1)
                act.wait_ge(s["y_ready"], n + 2)
                act.dma_start(y_v[bass.ds(n, 1)].rearrange("g p t d -> (g p) t d"), yt[:]
                              ).then_inc(s["y_stored"], 16)

            pairs(act, body)

        @block.vector
        def _(dve):
            chain = Tally(s["linked"])

            def link(ins):
                chain.inc(ins)
                chain.wait(dve)

            def split_weight(m):
                dve.wait_ge(s["sw_hi"], m + 1)
                dve.tensor_tensor(W[m][1][:], wraw[:], W[m][0][:].bitcast(F32), ALU.subtract
                                  ).then_inc(s["sw_split"], 1)

            def spread(tile, n):
                return tile.rearrange("p (a b) -> p a b", b=1).to_broadcast([P, tile.shape[1], n])

            nj = "p n j -> p (n j)"
            link(dve.tensor_tensor(hot[:].rearrange("p n j e -> p (n j) e"), spread(k["expert"][:].rearrange(nj), E),
                                   k["iota"][:].rearrange("p (a e) -> p a e", a=1).to_broadcast([P, NT * TOPK, E]),
                                   ALU.is_equal))
            link(dve.memset(prior[:, 0, :], 0.0))
            link(dve.tensor_reduce(mask[:], hot[:].rearrange("p n j e -> p n e j"), AX.X, ALU.add))
            dve.wait_ge(s["iotas_made"], 2)
            dve.tensor_copy(r["spare"][:], spare_i[:])
            link(dve.tensor_reduce(wsum[:], k["score"][:], AX.X, ALU.add))
            link(dve.tensor_scalar(wsum[:], wsum[:], 1e-9, None, ALU.add))
            link(dve.reciprocal(winv[:], wsum[:]))
            link(dve.tensor_tensor(pair[:, :, :, 1].bitcast(F32), k["score"][:], spread(winv[:], TOPK), ALU.mult))
            split_weight(0)
            dve.wait_ge(s["counted"], 1)
            total = ps[:, 2:4, :].rearrange("p k (n e) -> p (k n) e", e=E)
            for n in range(1, NT):
                link(dve.tensor_tensor(prior[:, n, :], prior[:, n - 1, :], total[:, n - 1, :], ALU.add))
            link(dve.tensor_tensor(pos[:].rearrange("p n e -> p (n e)"),
                                   ps[:, 0:2, :].rearrange("p k m -> p (k m)"),
                                   prior[:].rearrange("p n e -> p (n e)"), ALU.add))
            for j in range(TOPK):
                last = dve.tensor_tensor(hot[:, :, j, :], hot[:, :, j, :], pos[:], ALU.mult)
            link(last)
            link(dve.tensor_reduce(r["pos"][:], hot[:], AX.X, ALU.add))
            dve.tensor_scalar(r["keep"][:], r["pos"][:], float(CAP), None, ALU.is_lt)
            link(dve.scalar_tensor_tensor(out=r["slot"][:], in0=k["expert"][:], scalar=float(CAP), in1=r["pos"][:],
                                          op0=ALU.mult, op1=ALU.add))
            link(dve.tensor_tensor(r["away"][:], r["slot"][:], r["spare"][:], ALU.subtract))
            link(dve.tensor_tensor(r["away"][:], r["away"][:], r["keep"][:], ALU.mult))
            link(dve.tensor_tensor(r["slot"][:], r["away"][:], r["spare"][:], ALU.add))
            dve.tensor_copy(slot[:], r["slot"][:]).then_inc(s["slots_ready"], 2)
            split_weight(1)
            split_weight(2)
            dve.sem_inc(s["y_ready"], 1)
            dve.sem_inc(s["y_stored"], 16)

            def split_x(n, v):
                dve.wait_ge(s["xs_hi"], n + 1)
                dve.tensor_tensor(xTs[1][:], xT[v][:], xTs[0][:].bitcast(F32), ALU.subtract
                                  ).then_inc(s["xs_split"], 1)

            split_x(0, 0)

            def body(i, v, last):
                n = i * 2 + v
                for hc in range(C):
                    dve.wait_ge(s["silu_made"], n * C + hc + 1)
                    dve.tensor_tensor(gate[:, hc % 2, :], ps[:, 5 + 2 * (hc % 2), :], sil[:, hc % 2, :],
                                      ALU.mult).then_inc(s["gated"], 1)
                    dve.wait_ge(s["gate_hi"], n * C + hc + 1)
                    dve.tensor_tensor(gs[1][:, hc, :], gate[:, hc % 2, :], gs[0][:, hc, :].bitcast(F32),
                                      ALU.subtract).then_inc(s["g_split"], 1)
                if not (last and v):
                    split_x(n + 1, 1 - v)
                dve.wait_ge(s["z_made"], n + 1)
                dve.wait_ge(s["x1_loaded"], n * 16 + 16)
                dve.wait_ge(s["y_stored"], n * 16 + 16)
                dve.tensor_tensor(yt[:], ps[:, 0:4, :], x1t[:], ALU.add).then_inc(s["y_ready"], 1)

            pairs(dve, body)


def experts(nc, k, w1, w2, w3, xn_dram, y_dram, table, out):
    ident = k["ident"]
    with ExitStack() as ctx:
        def sb(name, shape, dt=F32):
            return ctx.enter_context(nc.sbuf_tensor(name, shape, dt))

        def sem(name):
            return ctx.enter_context(nc.semaphore(name))

        parts = ("hi", "lo")
        raw = [sb(f"w_raw{m}", [P, C, D]) for m in range(3)]
        W = [[tuple(sb(f"w{m}_{part}{u}", [P, C, D], F32R) for part in parts) for m in range(2)] for u in range(2)]
        W2 = tuple(sb(f"w2_{part}", [P, C, D], F32R) for part in parts)
        slots = sb("slots", [P, E, ST, 2], I32)
        gather_ids = [sb(f"gather_ids{u}", [P, ST], I32) for u in range(2)]
        add_ids, weight = sb("add_ids", [P, ST], I32), sb("weight", [P, ST])
        xe = sb("xe", [P, ST, D])
        xT = tuple(sb(f"xeT_{part}", [P, C, CAP], F32R) for part in parts)
        sil = sb("sil_e", [P, 2, CAP // 2])
        gate = sb("gate_e", [P, 4, CAP // 2])
        gs = tuple(sb(f"ge_{part}", [P, C, CAP], F32R) for part in parts)
        o = sb("o_e", [P, ST, D])
        ps = ctx.enter_context(nc.psum_tensor("ps_exp", [P, 8, 512], F32))
        HALF = CAP // 2

        names = ("slots_loaded raw_hi raw_split ids_ready gathered turned xT_hi xT_split h_made silu_made gated "
                 "gate_hi g_split o_made o_ready added o_free weight_ready sp_passed dve_passed pool_passed out_stored").split()
        s = {n: sem(n + "_e") for n in names}
        raw_loaded = [sem(f"raw_loaded{m}") for m in range(3)]
        block = ctx.enter_context(nc.Block())
        src = (w1, w3, w2)

        def pairs(eng, body):
            with eng.Fori(0, E // 2 - 1) as i:
                for u in range(2):
                    body(i, u, False)
            for u in range(2):
                body(E // 2 - 1, u, True)

        @block.sync
        def _(sp):
            def load(e, m):
                sp.dma_start(raw[m][:], src[m][bass.ds(e, 1)].rearrange("e (c p) n -> (e p) c n", p=P)
                             ).then_inc(raw_loaded[m], 16)

            sp.dma_start(slots[:], table[0:E * CAP, :].rearrange("(e p t) w -> p e (t w)", p=P, t=ST)
                         ).then_inc(s["slots_loaded"], 16)
            for m in range(3):
                load(0, m)
            for m in range(2):
                sp.wait_ge(s["raw_split"], m + 1)
                load(1, m)

            def body(i, u, last):
                e = i * 2 + u
                for m in range(3):
                    ahead = 2 if m < 2 else 1
                    if not (last and u + ahead > 1):
                        wait_alone(sp, s["raw_split"], e * 3 + 2 + m + 1, s["sp_passed"])
                        load(e + ahead, m)

            pairs(sp, body)
            sp.wait_ge(s["added"], 16 * ST * E)
            for g in range(8):
                rows = slice(g * N // 8, (g + 1) * N // 8)
                sp.dma_start(out[rows, :], y_dram[rows, :]).then_inc(s["out_stored"], 16)
            sp.wait_ge(s["out_stored"], 16 * 8)

        @block.gpsimd
        def _(pool):
            pool.sem_inc(s["o_free"], 1)

            def gather(e, u):
                wait_alone(pool, s["ids_ready"], e + 1, s["pool_passed"])
                for t in range(ST):
                    pool.indirect_dma_start(
                        out=xe[:, t, :], out_offset=None, in_=xn_dram,
                        in_offset=bass.IndirectOffsetOnAxis(ap=gather_ids[u][:, t:t + 1], axis=0)
                    ).then_inc(s["gathered"], 16)

            gather(0, 0)

            def body(i, u, last):
                e = i * 2 + u
                if not (last and u):
                    wait_alone(pool, s["turned"], e * C + C, s["pool_passed"])
                    gather(e + 1, 1 - u)
                for t in range(ST):
                    wait_alone(pool, s["o_ready"], e * ST + ST + t + 1, s["pool_passed"])
                    pool.indirect_dma_start(
                        out=y_dram, out_offset=bass.IndirectOffsetOnAxis(ap=add_ids[:, t:t + 1], axis=0),
                        in_=o[:, t, :], in_offset=None, compute_op=ALU.add).then_inc(s["added"], 16)
                    wait_alone(pool, s["added"], e * (16 * ST) + 16 * (t + 1), s["pool_passed"])
                pool.sem_inc(s["o_free"], 1)

            pairs(pool, body)

        @block.tensor
        def _(pe):
            def turn(e):
                pe.wait_ge(s["gathered"], e * (16 * ST) + 16 * ST)
                for c in range(C):
                    for t in range(ST):
                        mm = pe.transpose(ps[:, 2 * c + t // GT, (t % GT) * P:(t % GT + 1) * P],
                                          xe[:, t, c * P:(c + 1) * P], ident[:])
                    mm.then_inc(s["turned"], 1)
                    yield c

            for c in turn(0):
                pass

            def body(i, u, last):
                e = i * 2 + u
                for hc in range(C):
                    if hc == 0:
                        pe.wait_ge(s["raw_split"], e * 3 + 2)
                        pe.wait_ge(s["xT_split"], e * C + C)
                        pe.wait_ge(s["o_ready"], e * ST + GT)
                    elif hc == 1:
                        pe.wait_ge(s["o_ready"], e * ST + ST)
                    else:
                        pe.wait_ge(s["gated"], e * (2 * C) + 2 * (hc - 1))
                    for m in range(2):
                        for h in range(2):
                            for d in range(C):
                                mm = matmul(pe, ps[:, 4 * (hc % 2) + 2 * m + h, 0:HALF],
                                            tuple(w[:, d, hc * P:(hc + 1) * P] for w in W[u][m]),
                                            tuple(x[:, d, h * HALF:(h + 1) * HALF] for x in xT),
                                            d == 0, d == C - 1)
                    mm.then_inc(s["h_made"], 1)
                if not (last and u):
                    steps = turn(e + 1)
                    pe.wait_ge(s["gated"], e * (2 * C) + 2 * C - 2)
                    next(steps)
                    next(steps)
                    pe.wait_ge(s["gated"], e * (2 * C) + 2 * C)
                    for _ in steps:
                        pass
                pe.wait_ge(s["g_split"], e * (2 * C) + 2 * C)
                pe.wait_ge(s["raw_split"], e * 3 + (5 if not (last and u) else 3))
                for t in range(ST):
                    if not (last and u) and t % 2 == 0:
                        pe.wait_ge(s["xT_split"], e * C + C + t // 2 + 1)
                    for hc in range(C):
                        mm = matmul(pe, ps[:, t, :], tuple(g[:, hc, t * P:(t + 1) * P] for g in gs),
                                    tuple(w[:, hc, :] for w in W2), hc == 0, hc == C - 1)
                    mm.then_inc(s["o_made"], 1)

            pairs(pe, body)

        @block.scalar
        def _(act):
            def split_weight(m, dst, value):
                act.wait_ge(raw_loaded[m], value)
                act.copy(dst[0][:], raw[m][:]).then_inc(s["raw_hi"], 1)

            def turn_copy(e):
                for c in range(C):
                    act.wait_ge(s["turned"], e * C + c + 1)
                    act.copy(xT[0][:, c, :], ps[:, 2 * c:2 * c + 2, :].rearrange("p k n -> p (k n)")[:, 0:CAP]
                             ).then_inc(s["xT_hi"], 1)

            for m in range(2):
                split_weight(m, W[0][m], 16)
            turn_copy(0)

            def body(i, u, last):
                e = i * 2 + u
                for hc in range(C):
                    act.wait_ge(s["h_made"], e * C + hc + 1)
                    for h in range(2):
                        act.activation(sil[:, h, :], ps[:, 4 * (hc % 2) + h, 0:HALF], ACT.Silu
                                       ).then_inc(s["silu_made"], 1)
                    for h in range(2):
                        act.wait_ge(s["gated"], e * (2 * C) + 2 * hc + h + 1)
                        act.copy(gs[0][:, hc, h * HALF:(h + 1) * HALF], gate[:, 2 * (hc % 2) + h, :]).then_inc(s["gate_hi"], 1)
                    if hc < 2 and not (last and u):
                        split_weight(hc, W[1 - u][hc], e * 16 + 32)
                    elif hc == 2:
                        split_weight(2, W2, e * 16 + 16)
                if not (last and u):
                    turn_copy(e + 1)

            pairs(act, body)

        @block.vector
        def _(dve):
            def split_weight(m, dst, count):
                dve.wait_ge(s["raw_hi"], count)
                dve.tensor_tensor(dst[1][:], raw[m][:], dst[0][:].bitcast(F32), ALU.subtract
                                  ).then_inc(s["raw_split"], 1)

            def turn_split(e):
                for c in range(C):
                    dve.wait_ge(s["xT_hi"], e * C + c + 1)
                    dve.tensor_tensor(xT[1][:, c, :], ps[:, 2 * c:2 * c + 2, :].rearrange("p k n -> p (k n)")[:, 0:CAP],
                                      xT[0][:, c, :].bitcast(F32), ALU.subtract).then_inc(s["xT_split"], 1)

            def ids(e, u):
                dve.tensor_copy(gather_ids[u][:], slots[:, bass.ds(e, 1), :, 0].rearrange("p e t -> p (e t)")
                                ).then_inc(s["ids_ready"], 1)

            dve.wait_ge(s["slots_loaded"], 16)
            ids(0, 0)
            for m in range(2):
                split_weight(m, W[0][m], m + 1)
            turn_split(0)
            dve.sem_inc(s["o_ready"], ST)

            def body(i, u, last):
                e = i * 2 + u
                if not (last and u):
                    ids(e + 1, 1 - u)
                for hc in range(C):
                    if hc >= 2:
                        dve.wait_ge(s["g_split"], e * (2 * C) + 2 * (hc - 1))
                    for h in range(2):
                        n = e * (2 * C) + 2 * hc + h + 1
                        dve.wait_ge(s["silu_made"], n)
                        dve.tensor_tensor(gate[:, 2 * (hc % 2) + h, :], ps[:, 4 * (hc % 2) + 2 + h, 0:HALF], sil[:, h, :],
                                          ALU.mult).then_inc(s["gated"], 1)
                    for h in range(2):
                        n = e * (2 * C) + 2 * hc + h + 1
                        dve.wait_ge(s["gate_hi"], n)
                        dve.tensor_tensor(gs[1][:, hc, h * HALF:(h + 1) * HALF], gate[:, 2 * (hc % 2) + h, :],
                                          gs[0][:, hc, h * HALF:(h + 1) * HALF].bitcast(F32),
                                          ALU.subtract).then_inc(s["g_split"], 1)
                    if hc < 2 and not (last and u):
                        split_weight(hc, W[1 - u][hc], e * 3 + 2 + hc + 1)
                    elif hc == 2:
                        split_weight(2, W2, e * 3 + (5 if not (last and u) else 3))
                if not (last and u):
                    turn_split(e + 1)
                wait_alone(dve, s["o_free"], e + 1, s["dve_passed"])
                dve.tensor_copy(add_ids[:], slots[:, bass.ds(e, 1), :, 0].rearrange("p e t -> p (e t)"))
                dve.tensor_copy(weight[:], slots[:, bass.ds(e, 1), :, 1].bitcast(F32).rearrange("p e t -> p (e t)")
                                ).then_inc(s["weight_ready"], 1)
                dve.wait_ge(s["weight_ready"], e + 1)
                for t in range(ST):
                    dve.wait_ge(s["o_made"], e * ST + t + 1)
                    dve.tensor_scalar(o[:, t, :], ps[:, t, :], weight[:, t:t + 1], None, ALU.mult
                                      ).then_inc(s["o_ready"], 1)

            pairs(dve, body)


_INS = ["x", "ctx_1024", "L0_xattn_Wq", "L0_xattn_Wk", "L0_xattn_Wv", "L0_xattn_Wcq", "L0_xattn_Wck", "L0_xattn_Wcv",
        "L0_xattn_gamma", "L0_xattn_beta", "L0_xattn_W1", "L0_xattn_b1", "L0_ffn_wg", "L0_ffn_w1", "L0_ffn_w2",
        "L0_ffn_w3", "L0_ffn_sw1", "L0_ffn_sw2", "L0_ffn_sw3"]


def kernel(**inputs):
    import concourse.bacc as bacc
    from concourse.bass_utils import run_bass_kernel_spmd

    nc = bacc.Bacc("TRN2", target_bir_lowering=False, num_devices=1)
    arrays, args = {}, []
    for name in _INS:
        a = np.ascontiguousarray(inputs[name])
        arrays[f"in_{name}"] = a
        args.append(nc.dram_tensor(f"in_{name}", a.shape, mybir.dt.from_np(a.dtype), kind="ExternalInput").ap())
    out = nc.dram_tensor("out_0", (N, D), F32, kind="ExternalOutput").ap()
    kernel_program(nc, *args, out)
    r = run_bass_kernel_spmd(nc, [arrays], core_ids=[0])
    return r.results[0]["out_0"].reshape(B, S, D)
```

```python
from contextlib import ExitStack

import numpy as np
import concourse.bass as bass
from concourse import mybir

F32 = mybir.dt.float32
F32R = mybir.dt.float32r
I32 = mybir.dt.int32
U32 = mybir.dt.uint32
ALU = mybir.AluOpType
ACT = mybir.ActivationFunctionType
AX = mybir.AxisListType

P = 128
B, S, D = 2, 2048, 512
C = D // P
NT = B * S // P
GT = 4
GN = GT * P
G = S // GN
QT = S // P
KC = 128
E, TOPK, NG, KEEP_G = 32, 4, 8, 4
CAP = int(1.25 * B * S * TOPK / E)
ST = CAP // P
N = B * S
MASKED = -3.0e38
SCALE = float(D) ** -0.5
EPS_X, EPS_H = 1e-5, 1e-3
HOP = 2.0
DVE_SHARE = 1.0


class Tally:

    def __init__(self, sem, base=0):
        self.sem, self.base, self.n = sem, base, 0

    def inc(self, ins, by=1):
        ins.then_inc(self.sem, by)
        self.n += by
        return self.n

    def wait(self, eng, n=None):
        eng.wait_ge(self.sem, self.base + (self.n if n is None else n))


def matmul(pe, out, lhsT, rhs, start, stop):
    if not isinstance(lhsT, tuple):
        return pe.matmul(out, lhsT, rhs, start=start, stop=stop)
    pe.matmul(out, lhsT[0], rhs[0], start=start, stop=False)
    pe.matmul(out, lhsT[0], rhs[1], start=False, stop=False)
    return pe.matmul(out, lhsT[1], rhs[0], start=False, stop=stop)


def kernel_program(nc, x, ctx_1024, Wq, Wk, Wv, Wcq, Wck, Wcv, gamma, beta, W1, b1,
                   wg, w1, w2, w3, sw1, sw2, sw3, out):
    xn_dram = nc.dram_tensor("xn2", (N + CAP, D), F32, kind="Internal").ap()
    y_dram = nc.dram_tensor("y0", (N + CAP, D), F32, kind="Internal").ap()
    x1_dram = nc.dram_tensor("x1", (N, D), F32, kind="Internal").ap()
    xnT_dram = nc.dram_tensor("xn2T", (NT // GT, P, C, GN), F32, kind="Internal").ap()
    table = nc.dram_tensor("slot_table", (E * CAP + N * TOPK, 2), I32, kind="Internal").ap()
    with ExitStack() as keep:
        def sb(name, shape, dt=F32, stack=keep):
            return stack.enter_context(nc.sbuf_tensor(name, shape, dt))

        k = {}
        k["ident"] = sb("ident", [P, P])
        k["iota"] = sb("iota_f", [P, E])
        k["score"] = sb("chosen_score", [P, NT, TOPK])
        k["expert"] = sb("chosen_expert", [P, NT, TOPK])
        k["fuller"] = sb("fuller", [P, 2, 2], I32)
        with ExitStack() as early:
            k["neg_half"] = sb("neg_half", [P, GT], stack=early)
            k["G"] = sb("G_ctx", [P, C, B * KC], stack=early)
            k["Vc"] = sb("V_ctx", [P, B, D], stack=early)
            k["wgT"] = sb("wgT", [P, C, E], stack=early)
            k["causal"] = sb("causal", [P, P], stack=early)
            k["M"] = sb("M_qk", [P, C, D], stack=early)
            k["Wv"] = sb("Wv_sb", [P, C, D], stack=early)
            prepare(nc, k, ctx_1024, Wq, Wk, Wv, Wcq, Wck, Wcv, wg)
            attend_and_tokens(nc, k, x, W1, gamma, beta, b1, x1_dram, xn_dram, xnT_dram, y_dram, table)
        dispatch(nc, k, sw1, sw2, sw3, x1_dram, xnT_dram, y_dram, table)
        experts(nc, k, w1, w2, w3, xn_dram, y_dram, table, out)


def prepare(nc, k, ctx_in, Wq, Wk, Wv, Wcq, Wck, Wcv, wg):
    ident, causal, M, Gc, Vc, wgT = (k[n] for n in ("ident", "causal", "M", "G", "Vc", "wgT"))
    with ExitStack() as ctx:
        def sb(name, shape, dt=F32):
            return ctx.enter_context(nc.sbuf_tensor(name, shape, dt))

        def sem(name):
            return ctx.enter_context(nc.semaphore(name))

        raw = {n: sb(f"raw_{n}", [P, C, D]) for n in ("Wq", "Wk", "Wcq", "Wck", "Wcv")}
        WqT, WkT, WcqT = (sb(n, [P, C, D]) for n in ("WqT", "WkT", "WcqT"))
        cx = sb("cx", [P, B, D])
        cxT = sb("cxT", [P, C, B * KC])
        KcT = sb("KcT", [P, C, B * KC])
        wg_sb = sb("wg_sb", [E, D])
        ps = ctx.enter_context(nc.psum_tensor("ps_prep", [P, 8, 512], F32))
        loaded = {n: sem(f"loaded_{n}") for n in ("Wq", "Wk", "Wv", "Wcq", "Wck", "Wcv", "cx", "wg")}
        iota_i = sb("iota_i", [P, E], I32)
        zeroed, const_ready = sem("zeroed"), sem("const_ready")
        filled, copied = sem("prep_filled"), sem("prep_copied")
        block = ctx.enter_context(nc.Block())

        @block.sync
        def _(sp):
            for n, w in (("Wq", Wq), ("Wk", Wk), ("Wcq", Wcq)):
                sp.dma_start(raw[n][:], w.rearrange("(c p) n -> p c n", p=P)).then_inc(loaded[n], 16)
            sp.dma_start(cx[:], ctx_in.rearrange("b p n -> p b n")).then_inc(loaded["cx"], 16)
            for n, w in (("Wck", Wck), ("Wcv", Wcv)):
                sp.dma_start(raw[n][:], w.rearrange("(c p) n -> p c n", p=P)).then_inc(loaded[n], 16)
            sp.dma_start(wg_sb[:], wg).then_inc(loaded["wg"], 16)
            sp.dma_start(k["Wv"][:], Wv.rearrange("(c p) n -> p c n", p=P)).then_inc(loaded["Wv"], 16)
            sp.wait_ge(loaded["Wv"], 16)

        @block.gpsimd
        def _(pool):
            pool.memset(ident[:], 0.0).then_inc(zeroed, 1)
            pool.memset(causal[:], 0.0).then_inc(zeroed, 1)
            pool.memset(k["neg_half"][:], -0.5).then_inc(const_ready, 1)
            pool.iota(iota_i[:], [[1, E]], base=0, channel_multiplier=0).then_inc(const_ready, 1)
            pool.wait_ge(zeroed, 2)
            pool.affine_select(out=ident[:], in_=ident[:], compare_op=ALU.not_equal, fill=1.0, base=0,
                               pattern=[[-1, P]], channel_multiplier=1).then_inc(const_ready, 1)
            pool.affine_select(out=causal[:], in_=causal[:], compare_op=ALU.is_ge, fill=MASKED, base=0,
                               pattern=[[-1, P]], channel_multiplier=1).then_inc(const_ready, 1)

        def bank(step, j):
            return ps[:, 4 * (step % 2) + j, :]

        @block.tensor
        def _(pe):
            pe.wait_ge(const_ready, 4)

            def turn(step, src, tiles):
                for c in range(C):
                    for r in range(tiles):
                        last = pe.transpose(bank(step, c)[:, r * P:(r + 1) * P],
                                            src[:, r, c * P:(c + 1) * P], ident[:])
                last.then_inc(filled, 1)

            pe.wait_ge(loaded["Wq"], 16)
            turn(0, raw["Wq"], C)
            pe.wait_ge(loaded["Wk"], 16)
            turn(1, raw["Wk"], C)
            pe.wait_ge(loaded["Wcq"], 16)
            pe.wait_ge(copied, 1)
            turn(2, raw["Wcq"], C)
            pe.wait_ge(loaded["cx"], 16)
            pe.wait_ge(copied, 2)
            turn(3, cx, B)
            pe.wait_ge(copied, 3)
            for r in range(C):
                for d in range(C):
                    last = pe.matmul(bank(4, r), WqT[:, d, r * P:(r + 1) * P], WkT[:, d, :],
                                     start=(d == 0), stop=(d == C - 1))
            last.then_inc(filled, 1)
            pe.wait_ge(loaded["Wck"], 16)
            pe.wait_ge(copied, 4)
            for r in range(C):
                for e in range(C):
                    last = pe.matmul(bank(5, r)[:, 0:B * KC], raw["Wck"][:, e, r * P:(r + 1) * P], cxT[:, e, :],
                                     start=(e == 0), stop=(e == C - 1))
            last.then_inc(filled, 1)
            pe.wait_ge(copied, 6)
            for r in range(C):
                for d in range(C):
                    last = pe.matmul(bank(6, r)[:, 0:B * KC], WcqT[:, d, r * P:(r + 1) * P], KcT[:, d, :],
                                     start=(d == 0), stop=(d == C - 1))
            last.then_inc(filled, 1)
            pe.wait_ge(loaded["Wcv"], 16)
            pe.wait_ge(loaded["wg"], 16)
            for b in range(B):
                for e in range(C):
                    pe.matmul(bank(7, b), cxT[:, e, b * KC:(b + 1) * KC], raw["Wcv"][:, e, :],
                              start=(e == 0), stop=(e == C - 1))
            for c in range(C):
                last = pe.transpose(bank(7, 2)[:, c * E:(c + 1) * E], wg_sb[:, c * P:(c + 1) * P],
                                    ident[0:E, 0:E])
            last.then_inc(filled, 1)

        @block.vector
        def _(dve):
            dve.wait_ge(const_ready, 4)
            dve.tensor_copy(k["iota"][:], iota_i[:])
            copies = [(WqT[:], 512), (WkT[:], 512), (WcqT[:], 512), (cxT[:], B * KC), (M[:], 512),
                      (KcT[:], B * KC), (Gc[:], B * KC)]
            for step, (dst, n) in enumerate(copies):
                dve.wait_ge(filled, step + 1)
                lo = 4 * (step % 2)
                dve.tensor_copy(dst, ps[:, lo:lo + 4, 0:n]).then_inc(copied, 1)
            dve.wait_ge(filled, 8)
            dve.tensor_copy(Vc[:], ps[:, 4:6, :]).then_inc(copied, 1)
            dve.tensor_copy(wgT[:], ps[:, 6, 0:C * E].rearrange("p (c e) -> p c e", c=C)).then_inc(copied, 1)


def wait_alone(eng, sem, value, passed):
    eng.wait_ge(sem, value)
    eng.sem_inc(passed, 1)


def ln_rstd(pool, rstd, veps, neg_half, mv, eps, eps_added, rstd_ready):
    pool.tensor_scalar(veps, mv[:, :, 1], eps, None, ALU.add).then_inc(eps_added.sem, 1)
    eps_added.n += 1
    eps_added.wait(pool)
    pool.tensor_tensor(rstd, veps, neg_half, ALU.pow).then_inc(rstd_ready, 1)


def ln_stats(dve, made, tiles, stats, mv, var_ready):
    for t, tile in enumerate(tiles):
        last = dve.bn_stats(stats[:, t, :], tile)
    made.inc(last)
    made.wait(dve)
    for t in range(len(tiles)):
        last = dve.bn_aggr(mv[:, t, :], stats[:, t, :])
    last.then_inc(var_ready, 1)


def attention_order():
    order, waiting = [], None

    def products(a):
        return [("p", a, j) for j in range(a % QT // GT + 1)]

    for s in range(B * G):
        if s % G == 0 and waiting is not None:
            order += products(waiting)
            waiting = None
        order += [("x", s)] + [("q", s, c) for c in range(C)] + [("v", s, t) for t in range(GT)]
        for a in range(s * GT, (s + 1) * GT):
            order += [("s", a, j) for j in range(a % QT // GT + 1)]
            if waiting is not None:
                order += products(waiting)
            waiting = a
    return order + products(waiting)


TOKEN_STEPS = [
    ("stats1", "dve", 2.8), ("norm1a", "dve", 2.6), ("norm1b", "dve", 2.6), ("turn1a", "pe", 0), ("turn1b", "pe", 0),
    ("cscore", "pe", 0), ("cmax", "dve", 1.0), ("cturn", "pe", 0), ("cprod0", "pe", 0), ("c0", "dve", 1.4),
    ("cprod1", "pe", 0), ("c1", "dve", 1.4), ("stats2", "dve", 2.8), ("norm2a", "dve", 2.6), ("norm2b", "dve", 2.6),
    ("turn2a", "pe", 0), ("turn2b", "pe", 0), ("f0", "pe", 0), ("g0", "dve", 2.6), ("f1", "pe", 0),
    ("g1", "dve", 2.6), ("stats3", "dve", 2.8), ("norm3a", "dve", 2.6), ("norm3b", "dve", 2.6), ("x1", "dve", 2.6),
    ("stats4", "dve", 2.8), ("xn", "dve", 1.6), ("turn3a", "pe", 0), ("turn3b", "pe", 0), ("logits", "pe", 0),
    ("lmax", "dve", 0.5), ("groups", "dve", 2.5), ("keep", "dve", 2.0), ("choose", "dve", 2.5)]


def token_places(order):
    product = 0.85
    start, now, done_at = [], 0.0, {}
    for kind, a, *j in order:
        start.append(now)
        tiles = min(4, a % QT + 1 - 4 * j[0]) if kind in "sp" else 4
        now += tiles * product
        if kind == "p":
            done_at[a // GT] = now
    start.append(now)
    places = [[] for _ in order]
    free, by_pe, p = 0.0, False, 0
    for s in range(B * G):
        at = max(free, done_at[s] + HOP)
        for name, who, cost in TOKEN_STEPS:
            if who == "pe":
                at += HOP
            elif by_pe:
                at += HOP
            by_pe = who == "pe"
            p = max(p, int(np.searchsorted(start, at, side="right")) - 1)
            while p >= len(places):
                places.append([])
            places[p].append((name, s))
            at += cost * DVE_SHARE
        free = at
    return places


def attend_and_tokens(nc, k, x, W1, gamma, beta, b1, x1_dram, xn_dram, xnT_dram, y_dram, table):
    ident, causal, M, Wv, Gc, Vc, wgT = (k[n] for n in ("ident", "causal", "M", "Wv", "G", "Vc", "wgT"))
    order = attention_order()
    places = token_places(order)
    plan = [(order[p] if p < len(order) else None, places[p]) for p in range(len(places))]
    groups_of = [a % QT // GT + 1 for a in range(B * QT)]
    first_group = [sum(groups_of[:a]) for a in range(B * QT)]
    x_stats_at = {("s", (s - 1) * GT + 1, groups_of[(s - 1) * GT + 1] - 1): s for s in range(1, B * G)}
    x_norm_at = {("s", (s - 1) * GT + 2, groups_of[(s - 1) * GT + 2] - 1): s for s in range(1, B * G)}
    x_v = x.rearrange("b (g t p) d -> (b g) p t d", p=P, t=GT)
    x1_v = x1_dram.rearrange("(g t p) d -> g p t d", p=P, t=GT)
    xn_v = xn_dram[0:N, :].rearrange("(g t p) d -> g p t d", p=P, t=GT)
    with ExitStack() as ctx:
        def sb(name, shape, dt=F32):
            return ctx.enter_context(nc.sbuf_tensor(name, shape, dt))

        def sem(name):
            return ctx.enter_context(nc.semaphore(name))

        XN = [sb(f"XN{i}", [P, GT, D]) for i in range(3)]
        xnT = sb("xnT", [P, C, S])
        V = sb("V", [P, QT, D])
        QM = sb("QM", [P, C, GN])
        probs = sb("probs", [P, 2, S])
        probsT = sb("probsT", [P, 2, 512])
        A = [sb(f"A{u}", [P, GT, D]) for u in range(3)]
        H = sb("H", [P, GT, D])
        T = sb("T", [P, C, GN])
        Tx = T[:]
        W1_sb = sb("W1_sb", [P, C, D])
        gam, bet, b1_sb = sb("gam", [P, D]), sb("bet", [P, D]), sb("b1_sb", [P, D])
        zero = sb("zero", [P, D])
        spare = sb("spare_slots", [P, ST, 2], I32)
        cprobs, cprobsT = sb("cprobs", [P, GT, KC]), sb("cprobsT", [P, GT, P])
        nmax, rsum, rinv = sb("nmax", [P, B * QT]), sb("rsum", [P, B * QT]), sb("rinv", [P, B * QT])
        m = {}
        for n, shape in (("x_stats", [P, GT, 6]), ("x_mv", [P, GT, 2]), ("x_rstd", [P, GT]), ("x_veps", [P, GT]),
                         ("stats", [P, GT, 6]), ("mv", [P, GT, 2]), ("rstd", [P, GT]), ("veps", [P, GT]),
                         ("cmax", [P, GT]), ("csum", [P, GT]), ("cinv", [P, GT]), ("lmax", [P, GT]),
                         ("lsum", [P, GT]), ("linv", [P, GT]), ("lexp", [P, GT, E]), ("score", [P, GT, E]),
                         ("gmax", [P, GT, NG]), ("gtop", [P, GT, 8]), ("gidf", [P, GT, 8]),
                         ("hot", [P, GT, NG, KEEP_G]), ("keep", [P, GT, NG]), ("drop", [P, GT, NG]),
                         ("kept", [P, GT, E]), ("masked", [P, GT, E]), ("etop", [P, GT, 8])):
            m[n] = sb(n, shape)
        for n in ("gid", "eid"):
            m[n] = sb(n, [P, GT, 8], U32)
        ps = ctx.enter_context(nc.psum_tensor("ps_att", [P, 8, 512], F32))
        PT, O, TK = 4, 5, 6

        names = ("w_loaded zeros_made spare_stored x_made x_var x_eps x_rstd_ready xn_ready xn_turned xnT_copied "
                 "q_made q_copied v_made v_copied scored max_linked max_ready exped p_turned p_copied pv_used "
                 "rinv_ready a_ready linked stats_made var_ready eps_added rstd_ready h_ready turned T_copied cscored "
                 "cmax_ready cexped cturned cp_copied c_made c_copied f_made f_copied x1_ready xn2_ready logits_made "
                 "lmax_ready lexped chosen x1_stored xn_stored xnT_stored x_again").split()
        s = {n: sem(n + "_a") for n in names}
        x_loaded = [sem(f"x_loaded{i}") for i in range(3)]
        block = ctx.enter_context(nc.Block())

        @block.sync
        def _(sp):
            def load_x(g):
                sp.dma_start(XN[g % 3][:], x_v[g]).then_inc(x_loaded[g % 3], 16)

            load_x(0)
            load_x(1)
            sp.dma_start(W1_sb[:], W1.rearrange("(c p) n -> p c n", p=P)).then_inc(s["w_loaded"], 16)
            for dst, v in ((gam, gamma), (bet, beta), (b1_sb, b1)):
                sp.dma_start(dst[:], v.rearrange("(a n) -> a n", a=1).to_broadcast([P, D])
                             ).then_inc(s["w_loaded"], 16)
            for step, tokens in plan:
                if step and step[0] == "p" and step[1] % GT == GT - 1 and step[2] == groups_of[step[1]] - 1:
                    g = step[1] // GT + 3
                    if g < B * G:
                        sp.wait_ge(s["a_ready"], step[1] + 1)
                        load_x(g)
                if step == ("x", 0):
                    load_x(2)
                for name, g in tokens:
                    if name == "f1":
                        sp.wait_ge(s["f_made"], 2 * g + 2)
                        sp.dma_start(Tx, x_v[g]).then_inc(s["x_again"], 16)
                    if name == "x1":
                        sp.wait_ge(s["x1_ready"], g + 1)
                        sp.dma_start(x1_v[g], A[g % 3][:]).then_inc(s["x1_stored"], 16)
                    if name == "xn":
                        sp.wait_ge(s["xn2_ready"], g + 1)
                        sp.dma_start(xn_v[g], H[:]).then_inc(s["xn_stored"], 16)
                    if name == "turn3b":
                        sp.wait_ge(s["T_copied"], 6 * g + 6)
                        sp.dma_start(xnT_dram[g], T[:]).then_inc(s["xnT_stored"], 16)
            for n in ("x1_stored", "xn_stored", "xnT_stored"):
                sp.wait_ge(s[n], 16 * B * G)

        @block.gpsimd
        def _(pool):
            pool.memset(zero[:], 0.0).then_inc(s["zeros_made"], 1)
            pool.iota(spare[:, :, 0], [[1, ST]], base=N, channel_multiplier=ST).then_inc(s["zeros_made"], 1)
            pool.memset(spare[:, :, 1], 0).then_inc(s["zeros_made"], 1)

            in_x, in_tok = Tally(s["x_eps"]), Tally(s["eps_added"])

            def x_rstd(g):
                pool.wait_ge(s["x_var"], g + 1)
                ln_rstd(pool, m["x_rstd"][:], m["x_veps"][:], k["neg_half"][:], m["x_mv"], EPS_X, in_x,
                        s["x_rstd_ready"])

            x_rstd(0)
            pool.wait_ge(s["zeros_made"], 3)
            for dst in (xn_dram, y_dram):
                for t in range(ST):
                    pool.dma_start(dst[N + t * P:N + (t + 1) * P, :], zero[:]).then_inc(s["spare_stored"], 16)
            for e in range(E):
                pool.dma_start(table[e * CAP:(e + 1) * CAP, :].rearrange("(p t) w -> p (t w)", p=P),
                               spare[:].rearrange("p t w -> p (t w)")).then_inc(s["spare_stored"], 16)
            for step, tokens in plan:
                if step in x_stats_at:
                    x_rstd(x_stats_at[step])
                for name, g in tokens:
                    if name.startswith("stats"):
                        n = int(name[5]) - 1
                        pool.wait_ge(s["var_ready"], 4 * g + n + 1)
                        ln_rstd(pool, m["rstd"][:], m["veps"][:], k["neg_half"][:], m["mv"],
                                EPS_X if n == 3 else EPS_H, in_tok, s["rstd_ready"])
            pool.wait_ge(s["spare_stored"], 16 * (2 * ST + E))

        @block.tensor
        def _(pe):
            pe.wait_ge(s["w_loaded"], 64)

            def turn_probs(a, j):
                i = first_group[a] + j
                pe.wait_ge(s["exped"], a + 1)
                if i:
                    pe.wait_ge(s["p_copied"], i)
                for t in range(4 * j, min(4 * j + 4, a % QT + 1)):
                    mm = pe.transpose(ps[:, PT, (t % 4) * P:(t % 4 + 1) * P],
                                      probs[:, a % 2, t * P:(t + 1) * P], ident[:])
                mm.then_inc(s["p_turned"], 1)

            def attend(kind, a, j=0):
                if kind == "x":
                    pe.wait_ge(s["xn_ready"], a + 1)
                    if a:
                        pe.wait_ge(s["exped"], a * GT)
                    for c in range(C):
                        for t in range(GT):
                            mm = pe.transpose(ps[:, c, t * P:(t + 1) * P],
                                              XN[a % 3][:, t, c * P:(c + 1) * P], ident[:])
                    mm.then_inc(s["xn_turned"], 1)
                elif kind == "q":
                    pe.wait_ge(s["xnT_copied"], 2 * a + 2)
                    for e in range(C):
                        mm = pe.matmul(ps[:, j, :], M[:, e, j * P:(j + 1) * P],
                                       xnT[:, e, a % G * GN:(a % G + 1) * GN], start=(e == 0), stop=(e == C - 1))
                    mm.then_inc(s["q_made"], 1)
                elif kind == "v":
                    pe.wait_ge(s["q_copied"], a * C + j + 1)
                    at = (a % G * GT + j) * P
                    for e in range(C):
                        mm = pe.matmul(ps[:, j, :], xnT[:, e, at:at + P], Wv[:, e, :],
                                       start=(e == 0), stop=(e == C - 1))
                    mm.then_inc(s["v_made"], 1)
                elif kind == "s":
                    g, n = a // GT, (a % QT + 1) * P
                    if a % GT == 0:
                        pe.wait_ge(s["v_copied"], g * GT + min(j + 1, GT))
                        pe.wait_ge(s["q_copied"], g * C + C)
                    else:
                        pe.wait_ge(s["exped"], a)
                    if j == 0 and a % QT:
                        turn_probs(a - 1, 0)
                    w = min(512, n - 512 * j)
                    for c in range(C):
                        mm = pe.matmul(ps[:, j, 0:w], QM[:, c, a % GT * P:(a % GT + 1) * P],
                                       xnT[:, c, 512 * j:512 * j + w], start=(c == 0), stop=(c == C - 1))
                    if j == groups_of[a] - 1:
                        mm.then_inc(s["scored"], 1)
                else:
                    i = first_group[a] + j
                    if j == 0:
                        if a % QT == QT - 1:
                            turn_probs(a, 0)
                        if a:
                            pe.wait_ge(s["a_ready"], a)
                    pe.wait_ge(s["p_copied"], i + 1)
                    if j + 1 < groups_of[a]:
                        turn_probs(a, j + 1)
                    if j == 0 and a % GT == 0:
                        pe.wait_ge(s["v_copied"], (a // GT + 1) * GT)
                    for t in range(4 * j, min(4 * j + 4, a % QT + 1)):
                        mm = pe.matmul(ps[:, O, :], probsT[:, i % 2, (t % 4) * P:(t % 4 + 1) * P],
                                       V[:, t, :], start=(t == 0), stop=(t == a % QT))
                    mm.then_inc(s["pv_used"], 1)

            def token(name, g):
                if name[:4] == "turn":
                    n, half = int(name[4]) - 1, "ab".index(name[5])
                    if half:
                        pe.wait_ge(s["T_copied"], 6 * g + 2 * n + 1)
                    elif n < 2:
                        pe.wait_ge(s["h_ready"], 2 * g + n + 1)
                    else:
                        pe.wait_ge(s["xn2_ready"], g + 1)
                    if n == 0 and half == 0 and g:
                        pe.wait_ge(s["lexped"], g)
                    for i in range(2):
                        c = 2 * half + i
                        for t in range(GT):
                            mm = pe.transpose(ps[:, TK + i, t * P:(t + 1) * P], H[:, t, c * P:(c + 1) * P], ident[:])
                    mm.then_inc(s["turned"], 1)
                elif name == "cscore":
                    pe.wait_ge(s["T_copied"], 6 * g + 2)
                    for t in range(GT):
                        for e in range(C):
                            mm = pe.matmul(ps[:, TK, t * KC:(t + 1) * KC], T[:, e, t * P:(t + 1) * P],
                                           Gc[:, e, g // G * KC:(g // G + 1) * KC], start=(e == 0), stop=(e == C - 1))
                    mm.then_inc(s["cscored"], 1)
                elif name == "cturn":
                    pe.wait_ge(s["cexped"], g + 1)
                    for t in range(GT):
                        mm = pe.transpose(ps[:, TK + 1, t * P:(t + 1) * P], cprobs[:, t, :], ident[:])
                    mm.then_inc(s["cturned"], 1)
                elif name[:5] == "cprod":
                    half = int(name[5])
                    pe.wait_ge(s["cp_copied"], g + 1)
                    if half:
                        pe.wait_ge(s["c_copied"], 2 * g + 1)
                    for i in range(2):
                        mm = pe.matmul(ps[:, TK + i, :], cprobsT[:, 2 * half + i, :], Vc[:, g // G, :],
                                       start=True, stop=True)
                    mm.then_inc(s["c_made"], 1)
                elif name in ("f0", "f1"):
                    half = int(name[1])
                    pe.wait_ge(s["T_copied"], 6 * g + 4)
                    if half:
                        pe.wait_ge(s["f_copied"], 2 * g + 1)
                    for i in range(2):
                        t = 2 * half + i
                        for e in range(C):
                            mm = pe.matmul(ps[:, TK + i, :], T[:, e, t * P:(t + 1) * P], W1_sb[:, e, :],
                                           start=(e == 0), stop=(e == C - 1))
                    mm.then_inc(s["f_made"], 1)
                elif name == "logits":
                    pe.wait_ge(s["T_copied"], 6 * g + 6)
                    for t in range(GT):
                        for e in range(C):
                            mm = pe.matmul(ps[:, TK, t * E:(t + 1) * E], T[:, e, t * P:(t + 1) * P],
                                           wgT[:, e, :], start=(e == 0), stop=(e == C - 1))
                    mm.then_inc(s["logits_made"], 1)

            for step, tokens in plan:
                if step:
                    attend(*step)
                for name, g in tokens:
                    token(name, g)

        @block.scalar
        def _(act):
            def copy_probs(a, j):
                i = first_group[a] + j
                act.wait_ge(s["p_turned"], i + 1)
                if i >= 2:
                    act.wait_ge(s["pv_used"], i - 1)
                w = min(512, (a % QT + 1) * P - 512 * j)
                act.copy(probsT[:, i % 2, 0:w], ps[:, PT, 0:w]).then_inc(s["p_copied"], 1)

            def attend(kind, a, j=0):
                if kind == "x":
                    act.wait_ge(s["xn_turned"], a + 1)
                    for h in range(2):
                        act.copy(xnT[:, 2 * h:2 * h + 2, a % G * GN:(a % G + 1) * GN], ps[:, 2 * h:2 * h + 2, :]
                                 ).then_inc(s["xnT_copied"], 1)
                elif kind == "q":
                    act.wait_ge(s["q_made"], a * C + j + 1)
                    act.copy(QM[:, j, :], ps[:, j, :]).then_inc(s["q_copied"], 1)
                elif kind == "v":
                    act.wait_ge(s["v_made"], a * GT + j + 1)
                    act.copy(V[:, a % G * GT + j, :], ps[:, j, :]).then_inc(s["v_copied"], 1)
                elif kind == "s":
                    if j == 0 and a % QT:
                        copy_probs(a - 1, 0)
                    if j == groups_of[a] - 1:
                        act.wait_ge(s["max_ready"], a + 1)
                        flat = ps[:, 0:4, :].rearrange("p k n -> p (k n)")[:, 0:(a % QT + 1) * P]
                        act.activation(probs[:, a % 2, 0:(a % QT + 1) * P], flat, ACT.Exp, bias=nmax[:, a:a + 1],
                                       scale=SCALE, accum_out=rsum[:, a:a + 1]).then_inc(s["exped"], 1)
                else:
                    if j == 0 and a % QT == QT - 1:
                        copy_probs(a, 0)
                    if j + 1 < groups_of[a]:
                        copy_probs(a, j + 1)

            def token(name, g):
                if name[:4] == "turn":
                    n, half = int(name[4]) - 1, "ab".index(name[5])
                    act.wait_ge(s["turned"], 6 * g + 2 * n + half + 1)
                    if n == 0 and half == 0 and g:
                        act.wait_ge(s["xnT_stored"], 16 * g)
                    act.copy(T[:, 2 * half:2 * half + 2, :], ps[:, TK:TK + 2, :]).then_inc(s["T_copied"], 1)
                elif name == "cmax":
                    act.wait_ge(s["cmax_ready"], g + 1)
                    for t in range(GT):
                        last = act.activation(cprobs[:, t, :], ps[:, TK, t * KC:(t + 1) * KC], ACT.Exp,
                                              bias=m["cmax"][:, t:t + 1], scale=SCALE,
                                              accum_out=m["csum"][:, t:t + 1])
                    last.then_inc(s["cexped"], 1)
                elif name == "cturn":
                    act.wait_ge(s["cturned"], g + 1)
                    act.copy(cprobsT[:].rearrange("p t n -> p (t n)"), ps[:, TK + 1, :]).then_inc(s["cp_copied"], 1)
                elif name == "lmax":
                    act.wait_ge(s["lmax_ready"], g + 1)
                    for t in range(GT):
                        last = act.activation(m["lexp"][:, t, :], ps[:, TK, t * E:(t + 1) * E], ACT.Exp,
                                              bias=m["lmax"][:, t:t + 1], scale=1.0,
                                              accum_out=m["lsum"][:, t:t + 1])
                    last.then_inc(s["lexped"], 1)

            for step, tokens in plan:
                if step:
                    attend(*step)
                for name, g in tokens:
                    token(name, g)

        @block.vector
        def _(dve):
            chain, in_x, in_tok, in_max = (Tally(s[n]) for n in ("linked", "x_made", "stats_made", "max_linked"))

            def link(ins, tally=chain):
                tally.inc(ins)
                tally.wait(dve)

            def x_stats(g):
                dve.wait_ge(x_loaded[g % 3], 16 * (g // 3 + 1))
                ln_stats(dve, in_x, [XN[g % 3][:, t, :] for t in range(GT)], m["x_stats"], m["x_mv"], s["x_var"])

            def x_norm(g):
                dve.wait_ge(s["x_rstd_ready"], g + 1)
                for t in range(GT):
                    last = dve.tensor_scalar(XN[g % 3][:, t, :], XN[g % 3][:, t, :], m["x_mv"][:, t, 0:1],
                                             m["x_rstd"][:, t:t + 1], ALU.subtract, ALU.mult)
                last.then_inc(s["xn_ready"], 1)

            def attend(kind, a, j=0):
                if kind == "s" and j == groups_of[a] - 1:
                    dve.wait_ge(s["scored"], a + 1)
                    col = a % QT * P
                    diag = ps[:, col // 512, col % 512:col % 512 + P]
                    link(dve.tensor_tensor(diag, diag, causal[:], ALU.add), in_max)
                    flat = ps[:, 0:4, :].rearrange("p k n -> p (k n)")[:, 0:col + P]
                    link(dve.tensor_reduce(nmax[:, a:a + 1], flat, AX.X, ALU.max), in_max)
                    dve.tensor_scalar(nmax[:, a:a + 1], nmax[:, a:a + 1], -SCALE, None,
                                      ALU.mult).then_inc(s["max_ready"], 1)
                if kind == "p" and j == groups_of[a] - 1:
                    dve.wait_ge(s["exped"], a + 1)
                    dve.reciprocal(rinv[:, a:a + 1], rsum[:, a:a + 1]).then_inc(s["rinv_ready"], 1)
                    dve.wait_ge(s["rinv_ready"], a + 1)
                    dve.wait_ge(s["pv_used"], first_group[a] + groups_of[a])
                    g = a // GT
                    if g >= 3 and a % GT == 0:
                        dve.wait_ge(s["x1_stored"], 16 * (g - 2))
                    dve.scalar_tensor_tensor(out=A[g % 3][:, a % GT], in0=ps[:, O, :], scalar=rinv[:, a:a + 1],
                                             in1=XN[g % 3][:, a % GT], op0=ALU.mult, op1=ALU.add
                                             ).then_inc(s["a_ready"], 1)

            def token(name, g):
                At = A[g % 3]
                if name[:5] == "stats":
                    if name == "stats1":
                        dve.wait_ge(s["a_ready"], (g + 1) * GT)
                    ln_stats(dve, in_tok, [At[:, t, :] for t in range(GT)], m["stats"], m["mv"], s["var_ready"])
                elif name[:4] == "norm":
                    n, dst = int(name[4]) - 1, (At if name[4] == "3" else H)
                    if name[5] == "a":
                        dve.wait_ge(s["var_ready"], 4 * g + n + 1)
                        if n == 0 and g:
                            dve.wait_ge(s["xn_stored"], 16 * g)
                        for t in range(GT):
                            last = dve.scalar_tensor_tensor(out=dst[:, t, :], in0=At[:, t, :],
                                                            scalar=m["mv"][:, t, 0:1], in1=gam[:],
                                                            op0=ALU.subtract, op1=ALU.mult)
                        link(last)
                    else:
                        dve.wait_ge(s["rstd_ready"], 4 * g + n + 1)
                        for t in range(GT):
                            last = dve.scalar_tensor_tensor(out=dst[:, t, :], in0=dst[:, t, :],
                                                            scalar=m["rstd"][:, t:t + 1], in1=bet[:],
                                                            op0=ALU.mult, op1=ALU.add)
                        if n < 2:
                            last.then_inc(s["h_ready"], 1)
                        else:
                            link(last)
                elif name == "cmax":
                    dve.wait_ge(s["cscored"], g + 1)
                    link(dve.tensor_reduce(m["cmax"][:], ps[:, TK, :].rearrange("p (t n) -> p t n", t=GT),
                                           AX.X, ALU.max))
                    dve.tensor_scalar(m["cmax"][:], m["cmax"][:], -SCALE, None, ALU.mult).then_inc(s["cmax_ready"], 1)
                elif name in ("c0", "c1"):
                    half = int(name[1])
                    if not half:
                        dve.wait_ge(s["cexped"], g + 1)
                        link(dve.reciprocal(m["cinv"][:], m["csum"][:]))
                    dve.wait_ge(s["c_made"], 2 * g + half + 1)
                    for i in range(2):
                        t = 2 * half + i
                        last = dve.scalar_tensor_tensor(out=At[:, t, :], in0=ps[:, TK + i, :],
                                                        scalar=m["cinv"][:, t:t + 1], in1=H[:, t, :],
                                                        op0=ALU.mult, op1=ALU.add)
                    last.then_inc(s["c_copied"], 1)
                    dve.wait_ge(s["c_copied"], 2 * g + half + 1)
                elif name in ("g0", "g1"):
                    half = int(name[1])
                    dve.wait_ge(s["f_made"], 2 * g + half + 1)
                    for i in range(2):
                        t = 2 * half + i
                        last = dve.tensor_tensor(At[:, t, :], ps[:, TK + i, :], b1_sb[:], ALU.add)
                    last.then_inc(s["f_copied"], 1)
                    dve.wait_ge(s["f_copied"], 2 * g + half + 1)
                    for i in range(2):
                        t = 2 * half + i
                        last = dve.scalar_tensor_tensor(out=At[:, t, :], in0=At[:, t, :], scalar=0.0,
                                                        in1=H[:, t, :], op0=ALU.max, op1=ALU.add)
                    link(last)
                elif name == "x1":
                    dve.wait_ge(s["x_again"], 16 * (g + 1))
                    for t in range(GT):
                        last = dve.scalar_tensor_tensor(out=At[:, t, :], in0=At[:, t, :], scalar=0.0,
                                                        in1=T[:, t, :], op0=ALU.max, op1=ALU.add)
                    last.then_inc(s["x1_ready"], 1)
                    dve.wait_ge(s["x1_ready"], g + 1)
                elif name == "xn":
                    dve.wait_ge(s["rstd_ready"], 4 * g + 4)
                    for t in range(GT):
                        last = dve.tensor_scalar(H[:, t, :], At[:, t, :], m["mv"][:, t, 0:1],
                                                 m["rstd"][:, t:t + 1], ALU.subtract, ALU.mult)
                    last.then_inc(s["xn2_ready"], 1)
                elif name == "lmax":
                    dve.wait_ge(s["logits_made"], g + 1)
                    lg = ps[:, TK, 0:GT * E].rearrange("p (t e) -> p t e", t=GT)
                    link(dve.tensor_reduce(m["lmax"][:], lg, AX.X, ALU.max))
                    dve.tensor_scalar(m["lmax"][:], m["lmax"][:], -1.0, None, ALU.mult).then_inc(s["lmax_ready"], 1)
                elif name == "groups":
                    dve.wait_ge(s["lexped"], g + 1)
                    link(dve.reciprocal(m["linv"][:], m["lsum"][:]))
                    link(dve.tensor_tensor(m["score"][:], m["lexp"][:],
                                           m["linv"][:].rearrange("p (t a) -> p t a", a=1).to_broadcast([P, GT, E]),
                                           ALU.mult))
                    link(dve.tensor_reduce(m["gmax"][:].rearrange("p t g -> p (t g)"),
                                           m["score"][:].rearrange("p t (g a) -> p (t g) a", g=NG), AX.X, ALU.max))
                    for t in range(GT):
                        last = dve.max(m["gtop"][:, t, :], m["gmax"][:, t, :])
                    link(last)
                    for t in range(GT):
                        last = dve.max_index(m["gid"][:, t, :], m["gtop"][:, t, :], m["gmax"][:, t, :])
                    link(last)
                elif name == "keep":
                    link(dve.tensor_copy(m["gidf"][:], m["gid"][:]))
                    for t in range(GT):
                        last = dve.tensor_tensor(
                            m["hot"][:, t, :, :],
                            m["gidf"][:, t, 0:KEEP_G].rearrange("p (a j) -> p a j", a=1).to_broadcast([P, NG, KEEP_G]),
                            k["iota"][:, 0:NG].rearrange("p (g a) -> p g a", a=1).to_broadcast([P, NG, KEEP_G]),
                            ALU.is_equal)
                    link(last)
                    link(dve.tensor_reduce(m["keep"][:], m["hot"][:], AX.X, ALU.add))
                    link(dve.tensor_scalar(m["drop"][:], m["keep"][:], -1.0, None, ALU.add))
                elif name == "choose":
                    def of_group(tile):
                        return tile[:].rearrange("p t (g a) -> p (t g) a", a=1).to_broadcast([P, GT * NG, E // NG])

                    link(dve.tensor_tensor(m["kept"][:].rearrange("p t (g a) -> p (t g) a", g=NG),
                                           m["score"][:].rearrange("p t (g a) -> p (t g) a", g=NG),
                                           of_group(m["keep"]), ALU.mult))
                    link(dve.tensor_tensor(m["masked"][:].rearrange("p t (g a) -> p (t g) a", g=NG),
                                           m["kept"][:].rearrange("p t (g a) -> p (t g) a", g=NG),
                                           of_group(m["drop"]), ALU.add))
                    for t in range(GT):
                        last = dve.max(m["etop"][:, t, :], m["masked"][:, t, :])
                    link(last)
                    for t in range(GT):
                        last = dve.max_index(m["eid"][:, t, :], m["etop"][:, t, :], m["masked"][:, t, :])
                    link(last)
                    dve.tensor_copy(k["score"][:, g * GT:(g + 1) * GT, :], m["etop"][:, :, 0:TOPK])
                    link(dve.tensor_copy(k["expert"][:, g * GT:(g + 1) * GT, :], m["eid"][:, :, 0:TOPK]))

            x_stats(0)
            x_norm(0)
            dve.wait_ge(s["w_loaded"], 64)
            for step, tokens in plan:
                if step:
                    attend(*step)
                    if step in x_stats_at:
                        x_stats(x_stats_at[step])
                    if step in x_norm_at:
                        x_norm(x_norm_at[step])
                for name, g in tokens:
                    token(name, g)


def dispatch(nc, k, sw1, sw2, sw3, x1_dram, xnT_dram, y_dram, table):
    x1_v = x1_dram.rearrange("(g t p) d -> g p t d", p=P, t=GT)
    y_v = y_dram[0:N, :].rearrange("(g t p) d -> g p t d", p=P, t=GT)
    NGR = NT // GT
    with ExitStack() as ctx:
        def sb(name, shape, dt=F32):
            return ctx.enter_context(nc.sbuf_tensor(name, shape, dt))

        def sem(name):
            return ctx.enter_context(nc.semaphore(name))

        wraw = sb("sw_raw", [P, C, D])
        W = [tuple(sb(f"sw{m}_{part}", [P, C, D], F32R) for part in ("hi", "lo")) for m in range(3)]
        xT = [sb(f"xT{i}", [P, C, GN]) for i in range(2)]
        xTs = tuple(sb(f"xTs_{part}", [P, C, GN], F32R) for part in ("hi", "lo"))
        x1t = sb("x1t", [P, GT, D])
        yt = sb("yt", [P, GT, D])
        sil = sb("sil", [P, 2, GN])
        gate = sb("gate", [P, 2, GN])
        gs = tuple(sb(f"gs_{part}", [P, C, GN], F32R) for part in ("hi", "lo"))
        hot = sb("hot_all", [P, NT, TOPK, E])
        mask = sb("mask", [P, NT, E])
        prior = sb("prior", [P, NT, E])
        pos = sb("pos", [P, NT, E])
        prefix, ones = sb("prefix", [P, P]), sb("ones", [P, P])
        r = {n: sb(f"r_{n}", [P, NT, TOPK]) for n in ("pos", "tile", "scaled", "keep", "slot", "away", "spare")}
        count, more, bit = sb("count", [P, E]), sb("more", [P, 2, E]), sb("bit", [P, E])
        words = sb("words", [P, 2, 2])
        wsum, winv = sb("wsum", [P, NT]), sb("winv", [P, NT])
        slot = sb("slot", [P, NT, TOPK], I32)
        spare_i = sb("spare_i", [P, NT, TOPK], I32)
        pair = sb("pair", [P, NT, TOPK, 2], I32)
        ps = ctx.enter_context(nc.psum_tensor("ps_dis", [P, 8, 512], F32))

        names = ("sw_loaded sw_read sw_hi sw_split x_free x1_loaded y_stored tri_zero tri_made iotas_made linked "
                 "counted slots_ready scattered xs_hi xs_split sh_made silu_made gated gate_hi g_split "
                 "z_made y_ready sp_passed bits_made").split()
        s = {n: sem(n + "_d") for n in names}
        xT_loaded = [sem(f"xT_loaded{i}") for i in range(2)]
        block = ctx.enter_context(nc.Block())

        def pairs(eng, body):
            with eng.Fori(0, NGR // 2 - 1) as i:
                for v in range(2):
                    body(i, v, False)
            for v in range(2):
                body(NGR // 2 - 1, v, True)

        @block.sync
        def _(sp):
            def load_x(i, v):
                sp.dma_start(xT[v][:], xnT_dram[bass.ds(i * 2 + v, 1)].rearrange("g p c n -> (g p) c n")
                             ).then_inc(xT_loaded[v], 16)

            for m, w in enumerate((sw1, sw3, sw2)):
                if m:
                    sp.wait_ge(s["sw_split"], m)
                sp.dma_start(wraw[:], w.rearrange("(c p) n -> p c n", p=P)).then_inc(s["sw_loaded"], 16)
            for v in range(2):
                load_x(0, v)

            def body(i, v, last):
                n = i * 2 + v
                wait_alone(sp, s["y_ready"], n + 1, s["sp_passed"])
                sp.dma_start(x1t[:], x1_v[bass.ds(n, 1)].rearrange("g p t d -> (g p) t d")
                             ).then_inc(s["x1_loaded"], 16)
                if not last:
                    wait_alone(sp, s["xs_split"], n + 1, s["sp_passed"])
                    load_x(i + 1, v)

            pairs(sp, body)
            sp.wait_ge(s["y_stored"], 16 * (NGR + 1))

        @block.gpsimd
        def _(pool):
            pool.memset(prefix[:], 1.0).then_inc(s["tri_zero"], 1)
            pool.memset(ones[:], 1.0).then_inc(s["tri_made"], 1)
            pool.wait_ge(s["tri_zero"], 1)
            pool.affine_select(out=prefix[:], in_=prefix[:], compare_op=ALU.is_gt, fill=0.0, base=0,
                               pattern=[[1, P]], channel_multiplier=-1).then_inc(s["tri_made"], 1)
            pool.iota(spare_i[:], [[P * TOPK, NT], [1, TOPK]], base=E * CAP,
                      channel_multiplier=TOPK).then_inc(s["iotas_made"], 1)
            pool.iota(pair[:, :, :, 0], [[P, NT], [0, TOPK]], base=0,
                      channel_multiplier=1).then_inc(s["iotas_made"], 1)
            for i in range(E // 2):
                pool.memset(bit[:, 2 * i:2 * i + 2], float(2 ** i)).then_inc(s["bits_made"], 1)
            pool.wait_ge(s["slots_ready"], 2)
            for n in range(NT):
                for j in range(TOPK):
                    pool.indirect_dma_start(
                        out=table, out_offset=bass.IndirectOffsetOnAxis(ap=slot[:, n, j:j + 1], axis=0),
                        in_=pair[:, n, j, :], in_offset=None).then_inc(s["scattered"], 16)
            pool.wait_ge(s["scattered"], 16 * NT * TOPK)

        @block.tensor
        def _(pe):
            pe.wait_ge(s["tri_made"], 2)
            pe.wait_ge(s["linked"], 3)
            flat = mask[:].rearrange("p n e -> p (n e)")
            for j in range(2):
                half = flat[:, j * 512:(j + 1) * 512]
                pe.matmul(ps[:, j, :], prefix[:], half, start=True, stop=True)
                last = pe.matmul(ps[:, 2 + j, :], ones[:], half, start=True, stop=True)
            last.then_inc(s["counted"], 1)
            pe.wait_ge(s["sw_split"], 3)
            pe.wait_ge(s["slots_ready"], 1)

            def body(i, v, last):
                n = i * 2 + v
                pe.wait_ge(s["xs_split"], n + 1)
                for hc in range(C):
                    if hc >= 2:
                        pe.wait_ge(s["g_split"], n * C + hc - 1)
                    for m in range(2):
                        for e in range(C):
                            mm = matmul(pe, ps[:, 4 + 2 * (hc % 2) + m, :],
                                        tuple(w[:, e, hc * P:(hc + 1) * P] for w in W[m]),
                                        tuple(x[:, e, :] for x in xTs), e == 0, e == C - 1)
                    mm.then_inc(s["sh_made"], 1)
                pe.wait_ge(s["g_split"], n * C + C)
                pe.wait_ge(s["y_ready"], n + 1)
                for t in range(GT):
                    for hc in range(C):
                        mm = matmul(pe, ps[:, t, :], tuple(g[:, hc, t * P:(t + 1) * P] for g in gs),
                                    tuple(w[:, hc, :] for w in W[2]), hc == 0, hc == C - 1)
                mm.then_inc(s["z_made"], 1)

            pairs(pe, body)

        @block.scalar
        def _(act):
            for m in range(3):
                act.wait_ge(s["sw_loaded"], 16 * (m + 1))
                act.copy(W[m][0][:], wraw[:]).then_inc(s["sw_hi"], 1)
            act.wait_ge(xT_loaded[0], 16)
            act.copy(xTs[0][:], xT[0][:]).then_inc(s["xs_hi"], 1)

            def body(i, v, last):
                n = i * 2 + v
                for hc in range(C):
                    act.wait_ge(s["sh_made"], n * C + hc + 1)
                    act.activation(sil[:, hc % 2, :], ps[:, 4 + 2 * (hc % 2), :], ACT.Silu
                                   ).then_inc(s["silu_made"], 1)
                    act.wait_ge(s["gated"], n * C + hc + 1)
                    act.copy(gs[0][:, hc, :], gate[:, hc % 2, :]).then_inc(s["gate_hi"], 1)
                if not (last and v):
                    act.wait_ge(xT_loaded[1 - v], (i + v) * 16 + 16)
                    act.copy(xTs[0][:], xT[1 - v][:]).then_inc(s["xs_hi"], 1)
                act.wait_ge(s["y_ready"], n + 2)
                act.dma_start(y_v[bass.ds(n, 1)].rearrange("g p t d -> (g p) t d"), yt[:]
                              ).then_inc(s["y_stored"], 16)

            pairs(act, body)

        @block.vector
        def _(dve):
            chain = Tally(s["linked"])

            def link(ins):
                chain.inc(ins)
                chain.wait(dve)

            def split_weight(m):
                dve.wait_ge(s["sw_hi"], m + 1)
                dve.tensor_tensor(W[m][1][:], wraw[:], W[m][0][:].bitcast(F32), ALU.subtract
                                  ).then_inc(s["sw_split"], 1)

            def spread(tile, n):
                return tile.rearrange("p (a b) -> p a b", b=1).to_broadcast([P, tile.shape[1], n])

            nj = "p n j -> p (n j)"
            link(dve.tensor_tensor(hot[:].rearrange("p n j e -> p (n j) e"), spread(k["expert"][:].rearrange(nj), E),
                                   k["iota"][:].rearrange("p (a e) -> p a e", a=1).to_broadcast([P, NT * TOPK, E]),
                                   ALU.is_equal))
            link(dve.memset(prior[:, 0, :], 0.0))
            link(dve.tensor_reduce(mask[:], hot[:].rearrange("p n j e -> p n e j"), AX.X, ALU.add))
            dve.wait_ge(s["iotas_made"], 2)
            dve.tensor_copy(r["spare"][:], spare_i[:])
            link(dve.tensor_reduce(wsum[:], k["score"][:], AX.X, ALU.add))
            link(dve.tensor_scalar(wsum[:], wsum[:], 1e-9, None, ALU.add))
            link(dve.reciprocal(winv[:], wsum[:]))
            link(dve.tensor_tensor(pair[:, :, :, 1].bitcast(F32), k["score"][:], spread(winv[:], TOPK), ALU.mult))
            split_weight(0)
            dve.wait_ge(s["counted"], 1)
            total = ps[:, 2:4, :].rearrange("p k (n e) -> p (k n) e", e=E)
            for n in range(1, NT):
                link(dve.tensor_tensor(prior[:, n, :], prior[:, n - 1, :], total[:, n - 1, :], ALU.add))
            link(dve.tensor_tensor(count[:], prior[:, NT - 1, :], total[:, NT - 1, :], ALU.add))
            link(dve.tensor_tensor(pos[:].rearrange("p n e -> p (n e)"),
                                   ps[:, 0:2, :].rearrange("p k m -> p (k m)"),
                                   prior[:].rearrange("p n e -> p (n e)"), ALU.add))
            for j in range(TOPK):
                last = dve.tensor_tensor(hot[:, :, j, :], hot[:, :, j, :], pos[:], ALU.mult)
            link(last)
            link(dve.tensor_reduce(r["pos"][:], hot[:], AX.X, ALU.add))
            dve.tensor_scalar(r["keep"][:], r["pos"][:], float(CAP), None, ALU.is_lt)
            link(dve.tensor_scalar(r["tile"][:], r["pos"][:], float(P), None, ALU.is_ge))
            for t in range(2, ST):
                link(dve.scalar_tensor_tensor(out=r["tile"][:], in0=r["pos"][:], scalar=float(t * P),
                                              in1=r["tile"][:], op0=ALU.is_ge, op1=ALU.add))
            link(dve.tensor_scalar(r["scaled"][:], r["pos"][:], float(ST), None, ALU.mult))
            link(dve.scalar_tensor_tensor(out=r["scaled"][:], in0=r["tile"][:], scalar=1.0 - P * ST,
                                          in1=r["scaled"][:], op0=ALU.mult, op1=ALU.add))
            link(dve.scalar_tensor_tensor(out=r["slot"][:], in0=k["expert"][:], scalar=float(CAP), in1=r["scaled"][:],
                                          op0=ALU.mult, op1=ALU.add))
            link(dve.tensor_tensor(r["away"][:], r["slot"][:], r["spare"][:], ALU.subtract))
            link(dve.tensor_tensor(r["away"][:], r["away"][:], r["keep"][:], ALU.mult))
            link(dve.tensor_tensor(r["slot"][:], r["away"][:], r["spare"][:], ALU.add))
            dve.tensor_copy(slot[:], r["slot"][:]).then_inc(s["slots_ready"], 2)
            for m in range(2):
                last = dve.tensor_scalar(more[:, m, :], count[:], float((ST - 2 + m) * P), None, ALU.is_gt)
            link(last)
            dve.wait_ge(s["bits_made"], E // 2)
            for m in range(2):
                last = dve.tensor_tensor(more[:, m, :], more[:, m, :], bit[:], ALU.mult)
            link(last)
            link(dve.tensor_reduce(words[:], more[:].rearrange("p m (i u) -> p m u i", u=2), AX.X, ALU.add))
            link(dve.tensor_copy(k["fuller"][:], words[:]))
            split_weight(1)
            split_weight(2)
            dve.sem_inc(s["y_ready"], 1)
            dve.sem_inc(s["y_stored"], 16)

            def split_x(n, v):
                dve.wait_ge(s["xs_hi"], n + 1)
                dve.tensor_tensor(xTs[1][:], xT[v][:], xTs[0][:].bitcast(F32), ALU.subtract
                                  ).then_inc(s["xs_split"], 1)

            split_x(0, 0)

            def body(i, v, last):
                n = i * 2 + v
                for hc in range(C):
                    dve.wait_ge(s["silu_made"], n * C + hc + 1)
                    dve.tensor_tensor(gate[:, hc % 2, :], ps[:, 5 + 2 * (hc % 2), :], sil[:, hc % 2, :],
                                      ALU.mult).then_inc(s["gated"], 1)
                    dve.wait_ge(s["gate_hi"], n * C + hc + 1)
                    dve.tensor_tensor(gs[1][:, hc, :], gate[:, hc % 2, :], gs[0][:, hc, :].bitcast(F32),
                                      ALU.subtract).then_inc(s["g_split"], 1)
                if not (last and v):
                    split_x(n + 1, 1 - v)
                dve.wait_ge(s["z_made"], n + 1)
                dve.wait_ge(s["x1_loaded"], n * 16 + 16)
                dve.wait_ge(s["y_stored"], n * 16 + 16)
                dve.tensor_tensor(yt[:], ps[:, 0:4, :], x1t[:], ALU.add).then_inc(s["y_ready"], 1)

            pairs(dve, body)


def experts(nc, k, w1, w2, w3, xn_dram, y_dram, table, out):
    ident = k["ident"]
    with ExitStack() as ctx:
        def sb(name, shape, dt=F32):
            return ctx.enter_context(nc.sbuf_tensor(name, shape, dt))

        def sem(name):
            return ctx.enter_context(nc.semaphore(name))

        parts = ("hi", "lo")
        raw = [sb(f"w_raw{m}", [P, C, D]) for m in range(3)]
        W = [[tuple(sb(f"w{m}_{part}{u}", [P, C, D], F32R) for part in parts) for m in range(2)] for u in range(2)]
        W2 = tuple(sb(f"w2_{part}", [P, C, D], F32R) for part in parts)
        slots = sb("slots", [P, E, ST, 2], I32)
        gather_ids = [sb(f"gather_ids{u}", [P, ST], I32) for u in range(2)]
        add_ids, weight = sb("add_ids", [P, ST], I32), sb("weight", [P, ST])
        xe = sb("xe", [P, ST, D])
        xT = tuple(sb(f"xeT_{part}", [P, C, CAP], F32R) for part in parts)
        sil = sb("sil_e", [P, CAP])
        gate = sb("gate_e", [P, 2, CAP])
        gs = tuple(sb(f"ge_{part}", [P, C, CAP], F32R) for part in parts)
        o = sb("o_e", [P, ST, D])
        ps = ctx.enter_context(nc.psum_tensor("ps_exp", [P, 8, 512], F32))
        names = ("slots_loaded raw_hi raw_split ids_ready gathered turned xT_hi xT_split h_made silu_made gated "
                 "gate_hi g_split o_made o_ready added o_free weight_ready sp_passed dve_passed pool_passed out_stored").split()
        s = {n: sem(n + "_e") for n in names}
        raw_loaded = [sem(f"raw_loaded{m}") for m in range(3)]
        block = ctx.enter_context(nc.Block())
        src = (w1, w3, w2)

        def pairs(eng, body):
            with eng.Fori(0, E // 2 - 1) as i:
                for u in range(2):
                    body(i, u, False)
            for u in range(2):
                body(E // 2 - 1, u, True)

        def load_fuller(eng):
            return [[eng.value_load(k["fuller"][0:1, m, u:u + 1], min_val=0, max_val=2 ** (E // 2) - 1)
                     for u in range(2)] for m in range(2)]

        def by_tiles(eng, fuller, i, u, body):
            with eng.If(((fuller[1][u] >> i) & 1) == 1):
                body(ST)
            with eng.Else():
                with eng.If(((fuller[0][u] >> i) & 1) == 1):
                    body(ST - 1)
                with eng.Else():
                    body(ST - 2)

        def pieces(tiles):
            n = tiles * P
            cuts = 1 if n <= 512 else 2
            return [slice(h * n // cuts, (h + 1) * n // cuts) for h in range(cuts)]

        @block.sync
        def _(sp):
            def load(e, m):
                sp.dma_start(raw[m][:], src[m][bass.ds(e, 1)].rearrange("e (c p) n -> (e p) c n", p=P)
                             ).then_inc(raw_loaded[m], 16)

            sp.dma_start(slots[:], table[0:E * CAP, :].rearrange("(e p t) w -> p e (t w)", p=P, t=ST)
                         ).then_inc(s["slots_loaded"], 16)
            for m in range(3):
                load(0, m)
            for m in range(2):
                sp.wait_ge(s["raw_split"], m + 1)
                load(1, m)

            def body(i, u, last):
                e = i * 2 + u
                for m in range(3):
                    ahead = 2 if m < 2 else 1
                    if not (last and u + ahead > 1):
                        wait_alone(sp, s["raw_split"], e * 3 + 2 + m + 1, s["sp_passed"])
                        load(e + ahead, m)

            pairs(sp, body)
            sp.wait_ge(s["added"], 16 * ST * E)
            for g in range(8):
                rows = slice(g * N // 8, (g + 1) * N // 8)
                sp.dma_start(out[rows, :], y_dram[rows, :]).then_inc(s["out_stored"], 16)
            sp.wait_ge(s["out_stored"], 16 * 8)

        @block.gpsimd
        def _(pool):
            pool.memset(o[:], 0.0).then_inc(s["o_free"], 1)

            def gather(e, u):
                wait_alone(pool, s["ids_ready"], e + 1, s["pool_passed"])
                for t in range(ST):
                    pool.indirect_dma_start(
                        out=xe[:, t, :], out_offset=None, in_=xn_dram,
                        in_offset=bass.IndirectOffsetOnAxis(ap=gather_ids[u][:, t:t + 1], axis=0)
                    ).then_inc(s["gathered"], 16)

            gather(0, 0)

            def body(i, u, last):
                e = i * 2 + u
                if not (last and u):
                    wait_alone(pool, s["turned"], e * C + C, s["pool_passed"])
                    gather(e + 1, 1 - u)
                for t in range(ST):
                    wait_alone(pool, s["o_ready"], e * ST + ST + t + 1, s["pool_passed"])
                    pool.indirect_dma_start(
                        out=y_dram, out_offset=bass.IndirectOffsetOnAxis(ap=add_ids[:, t:t + 1], axis=0),
                        in_=o[:, t, :], in_offset=None, compute_op=ALU.add).then_inc(s["added"], 16)
                wait_alone(pool, s["added"], e * (16 * ST) + 16 * ST, s["pool_passed"])
                pool.sem_inc(s["o_free"], 1)

            pairs(pool, body)

        @block.tensor
        def _(pe):
            def turn(e):
                pe.wait_ge(s["gathered"], e * (16 * ST) + 16 * ST)
                for c in range(C):
                    for t in range(ST):
                        mm = pe.transpose(ps[:, 2 * c + t // GT, (t % GT) * P:(t % GT + 1) * P],
                                          xe[:, t, c * P:(c + 1) * P], ident[:])
                    mm.then_inc(s["turned"], 1)
                    yield c

            for c in turn(0):
                pass

            fuller = load_fuller(pe)

            def body(i, u, last):
                e = i * 2 + u

                def expert(tiles):
                    for hc in range(C):
                        if hc == 0:
                            pe.wait_ge(s["raw_split"], e * 3 + 2)
                            pe.wait_ge(s["xT_split"], e * C + C)
                            pe.wait_ge(s["o_ready"], e * ST + GT)
                        elif hc == 1:
                            pe.wait_ge(s["o_ready"], e * ST + ST)
                        else:
                            pe.wait_ge(s["gated"], e * (2 * C) + 2 * (hc - 1))
                        for m in range(2):
                            for h, cut in enumerate(pieces(tiles)):
                                for d in range(C):
                                    mm = matmul(pe, ps[:, 4 * (hc % 2) + 2 * m + h, 0:cut.stop - cut.start],
                                                tuple(w[:, d, hc * P:(hc + 1) * P] for w in W[u][m]),
                                                tuple(x[:, d, cut] for x in xT), d == 0, d == C - 1)
                        mm.then_inc(s["h_made"], 1)
                    if not (last and u):
                        steps = turn(e + 1)
                        pe.wait_ge(s["gated"], e * (2 * C) + 2 * C - 2)
                        next(steps)
                        next(steps)
                        pe.wait_ge(s["gated"], e * (2 * C) + 2 * C)
                        for _ in steps:
                            pass
                    pe.wait_ge(s["g_split"], e * (2 * C) + 2 * C)
                    pe.wait_ge(s["raw_split"], e * 3 + (5 if not (last and u) else 3))
                    for t in range(tiles):
                        if not (last and u) and t % 2 == 0:
                            pe.wait_ge(s["xT_split"], e * C + C + t // 2 + 1)
                        for hc in range(C):
                            mm = matmul(pe, ps[:, t, :], tuple(g[:, hc, t * P:(t + 1) * P] for g in gs),
                                        tuple(w[:, hc, :] for w in W2), hc == 0, hc == C - 1)
                        mm.then_inc(s["o_made"], 1 if t < tiles - 1 else ST - t)

                by_tiles(pe, fuller, i, u, expert)

            pairs(pe, body)

        @block.scalar
        def _(act):
            def split_weight(m, dst, value):
                act.wait_ge(raw_loaded[m], value)
                act.copy(dst[0][:], raw[m][:]).then_inc(s["raw_hi"], 1)

            def turn_copy(e):
                for c in range(C):
                    act.wait_ge(s["turned"], e * C + c + 1)
                    act.copy(xT[0][:, c, :], ps[:, 2 * c:2 * c + 2, :].rearrange("p k n -> p (k n)")[:, 0:CAP]
                             ).then_inc(s["xT_hi"], 1)

            for m in range(2):
                split_weight(m, W[0][m], 16)
            turn_copy(0)
            fuller = load_fuller(act)

            def body(i, u, last):
                e = i * 2 + u

                def expert(tiles):
                    cuts = pieces(tiles)
                    by = 2 // len(cuts)
                    for hc in range(C):
                        act.wait_ge(s["h_made"], e * C + hc + 1)
                        for h, cut in enumerate(cuts):
                            act.activation(sil[:, cut], ps[:, 4 * (hc % 2) + h, 0:cut.stop - cut.start], ACT.Silu
                                           ).then_inc(s["silu_made"], by)
                        for h, cut in enumerate(cuts):
                            act.wait_ge(s["gated"], e * (2 * C) + 2 * hc + (h + 1) * by)
                            act.copy(gs[0][:, hc, cut], gate[:, hc % 2, cut]).then_inc(s["gate_hi"], by)
                        if hc < 2 and not (last and u):
                            split_weight(hc, W[1 - u][hc], e * 16 + 32)
                        elif hc == 2:
                            split_weight(2, W2, e * 16 + 16)
                    if not (last and u):
                        turn_copy(e + 1)

                by_tiles(act, fuller, i, u, expert)

            pairs(act, body)

        @block.vector
        def _(dve):
            def split_weight(m, dst, count):
                dve.wait_ge(s["raw_hi"], count)
                dve.tensor_tensor(dst[1][:], raw[m][:], dst[0][:].bitcast(F32), ALU.subtract
                                  ).then_inc(s["raw_split"], 1)

            def turn_split(e):
                for c in range(C):
                    dve.wait_ge(s["xT_hi"], e * C + c + 1)
                    dve.tensor_tensor(xT[1][:, c, :], ps[:, 2 * c:2 * c + 2, :].rearrange("p k n -> p (k n)")[:, 0:CAP],
                                      xT[0][:, c, :].bitcast(F32), ALU.subtract).then_inc(s["xT_split"], 1)

            def ids(e, u):
                dve.tensor_copy(gather_ids[u][:], slots[:, bass.ds(e, 1), :, 0].rearrange("p e t -> p (e t)")
                                ).then_inc(s["ids_ready"], 1)

            dve.wait_ge(s["slots_loaded"], 16)
            ids(0, 0)
            for m in range(2):
                split_weight(m, W[0][m], m + 1)
            turn_split(0)
            dve.sem_inc(s["o_ready"], ST)
            fuller = load_fuller(dve)

            def body(i, u, last):
                e = i * 2 + u

                def expert(tiles):
                    cuts = pieces(tiles)
                    by = 2 // len(cuts)
                    if not (last and u):
                        ids(e + 1, 1 - u)
                    for hc in range(C):
                        if hc >= 2:
                            dve.wait_ge(s["g_split"], e * (2 * C) + 2 * (hc - 1))
                        for h, cut in enumerate(cuts):
                            dve.wait_ge(s["silu_made"], e * (2 * C) + 2 * hc + (h + 1) * by)
                            dve.tensor_tensor(gate[:, hc % 2, cut], ps[:, 4 * (hc % 2) + 2 + h, 0:cut.stop - cut.start],
                                              sil[:, cut], ALU.mult).then_inc(s["gated"], by)
                        for h, cut in enumerate(cuts):
                            dve.wait_ge(s["gate_hi"], e * (2 * C) + 2 * hc + (h + 1) * by)
                            dve.tensor_tensor(gs[1][:, hc, cut], gate[:, hc % 2, cut], gs[0][:, hc, cut].bitcast(F32),
                                              ALU.subtract).then_inc(s["g_split"], by)
                        if hc < 2 and not (last and u):
                            split_weight(hc, W[1 - u][hc], e * 3 + 2 + hc + 1)
                        elif hc == 2:
                            split_weight(2, W2, e * 3 + (5 if not (last and u) else 3))
                    if not (last and u):
                        turn_split(e + 1)
                    wait_alone(dve, s["o_free"], e + 1, s["dve_passed"])
                    dve.tensor_copy(add_ids[:], slots[:, bass.ds(e, 1), :, 0].rearrange("p e t -> p (e t)"))
                    dve.tensor_copy(weight[:], slots[:, bass.ds(e, 1), :, 1].bitcast(F32).rearrange("p e t -> p (e t)")
                                    ).then_inc(s["weight_ready"], 1)
                    dve.wait_ge(s["weight_ready"], e + 1)
                    for t in range(tiles):
                        dve.wait_ge(s["o_made"], e * ST + t + 1)
                        dve.tensor_scalar(o[:, t, :], ps[:, t, :], weight[:, t:t + 1], None, ALU.mult
                                          ).then_inc(s["o_ready"], 1 if t < tiles - 1 else ST - t)

                by_tiles(dve, fuller, i, u, expert)

            pairs(dve, body)


_INS = ["x", "ctx_1024", "L0_xattn_Wq", "L0_xattn_Wk", "L0_xattn_Wv", "L0_xattn_Wcq", "L0_xattn_Wck", "L0_xattn_Wcv",
        "L0_xattn_gamma", "L0_xattn_beta", "L0_xattn_W1", "L0_xattn_b1", "L0_ffn_wg", "L0_ffn_w1", "L0_ffn_w2",
        "L0_ffn_w3", "L0_ffn_sw1", "L0_ffn_sw2", "L0_ffn_sw3"]


def kernel(**inputs):
    import concourse.bacc as bacc
    from concourse.bass_utils import run_bass_kernel_spmd

    nc = bacc.Bacc("TRN2", target_bir_lowering=False, num_devices=1)
    arrays, args = {}, []
    for name in _INS:
        a = np.ascontiguousarray(inputs[name])
        arrays[f"in_{name}"] = a
        args.append(nc.dram_tensor(f"in_{name}", a.shape, mybir.dt.from_np(a.dtype), kind="ExternalInput").ap())
    out = nc.dram_tensor("out_0", (N, D), F32, kind="ExternalOutput").ap()
    kernel_program(nc, *args, out)
    r = run_bass_kernel_spmd(nc, [arrays], core_ids=[0])
    return r.results[0]["out_0"].reshape(B, S, D)
```

```python
from contextlib import ExitStack

import numpy as np
import concourse.bass as bass
from concourse import mybir

F32 = mybir.dt.float32
F32R = mybir.dt.float32r
I32 = mybir.dt.int32
U32 = mybir.dt.uint32
ALU = mybir.AluOpType
ACT = mybir.ActivationFunctionType
AX = mybir.AxisListType

P = 128
B, S, D = 2, 2048, 512
C = D // P
NT = B * S // P
GT = 4
GN = GT * P
G = S // GN
QT = S // P
KC = 128
E, TOPK, NG, KEEP_G = 32, 4, 8, 4
CAP = int(1.25 * B * S * TOPK / E)
ST = CAP // P
WIDTHS = [CAP - i * P // 2 for i in range(4, -1, -1)]
NW = len(WIDTHS) - 1
N = B * S
MASKED = -3.0e38
SCALE = float(D) ** -0.5
EPS_X, EPS_H = 1e-5, 1e-3
DVE_LAG = 0.5
DVE_SHARE = 0.9
HOP = 1.0
SCATTER_EVERY = 3.0


class Tally:

    def __init__(self, sem, base=0):
        self.sem, self.base, self.n = sem, base, 0

    def inc(self, ins, by=1):
        ins.then_inc(self.sem, by)
        self.n += by
        return self.n

    def wait(self, eng, n=None):
        eng.wait_ge(self.sem, self.base + (self.n if n is None else n))


def matmul(pe, out, lhsT, rhs, start, stop):
    if not isinstance(lhsT, tuple):
        return pe.matmul(out, lhsT, rhs, start=start, stop=stop)
    pe.matmul(out, lhsT[0], rhs[0], start=start, stop=False)
    pe.matmul(out, lhsT[0], rhs[1], start=False, stop=False)
    return pe.matmul(out, lhsT[1], rhs[0], start=False, stop=stop)


def kernel_program(nc, x, ctx_1024, Wq, Wk, Wv, Wcq, Wck, Wcv, gamma, beta, W1, b1,
                   wg, w1, w2, w3, sw1, sw2, sw3, out):
    xn_dram = nc.dram_tensor("xn2", (N + CAP, D), F32, kind="Internal").ap()
    y_dram = nc.dram_tensor("y0", (N + CAP, D), F32, kind="Internal").ap()
    x1_dram = nc.dram_tensor("x1", (N, D), F32, kind="Internal").ap()
    xnT_dram = nc.dram_tensor("xn2T", (NT // GT, P, C, GN), F32, kind="Internal").ap()
    table = nc.dram_tensor("slot_table", (E * CAP + N * TOPK, 2), I32, kind="Internal").ap()
    with ExitStack() as keep:
        def sb(name, shape, dt=F32, stack=keep):
            return stack.enter_context(nc.sbuf_tensor(name, shape, dt))

        k = {}
        k["ident"] = sb("ident", [P, P])
        k["iota"] = sb("iota_f", [P, E])
        k["fuller"] = sb("fuller", [P, NW, 2], I32)
        with ExitStack() as first:
            k["A"] = [sb(f"A{u}", [P, GT, D], stack=first) for u in range(3)]
            k["H"] = sb("H", [P, GT, D], stack=first)
            k["T"] = sb("T", [P, C, GN], stack=first)
        ahead = FirstExpert(nc, keep, (w1, w3, w2), xn_dram, table)
        rest_of_T = 2 * GT * D - ST * D - E * ST * 2 - 2 * ST + 16
        with ExitStack() as first:
            sb("rest_of_T0", [P, rest_of_T], stack=first)
            ahead.W2 = tuple(sb(f"w2_{part}", [P, C, D], F32R, stack=first) for part in ("hi", "lo"))
            w1_hi, w3_lo, w1_lo, w3_hi = (sb(n, [P, C, D], F32R, stack=first) for n in ("w1_hi0", "w3_lo0", "w1_lo0", "w3_hi0"))
            ahead.W = [(w1_hi, w1_lo), (w3_hi, w3_lo)]
        ahead.size = rest_of_T + 6 * C * D
        with ExitStack() as early:
            sb("rest_of_T", [P, rest_of_T], stack=early)
            with ExitStack() as first:
                k["XN"] = [sb(f"XN{i}", [P, GT, D], stack=first) for i in range(3)]
                k["xnT"] = sb("xnT", [P, C, S], stack=first)
                k["V"] = sb("V", [P, QT, D], stack=first)
                k["QM"] = sb("QM", [P, C, GN], stack=first)
                k["probs"] = sb("probs", [P, 2, S], stack=first)
                k["probsT"] = sb("probsT", [P, 2, 512], stack=first)
                k["M"] = sb("M_qk", [P, C, D], stack=first)
                k["Wv"] = sb("Wv_sb", [P, C, D], stack=first)
            shared = SharedExpert(nc, early, x1_dram, xnT_dram, y_dram)
            norm_x = XNorm(nc, early, k["XN"], x)
            k["neg_half"] = sb("neg_half", [P, GT], stack=early)
            k["G"] = sb("G_ctx", [P, C, B * KC], stack=early)
            k["Vc"] = sb("V_ctx", [P, B, D], stack=early)
            k["wgT"] = sb("wgT", [P, C, E], stack=early)
            k["causal"] = sb("causal", [P, P], stack=early)
            prepare(nc, k, norm_x, ctx_1024, Wq, Wk, Wv, Wcq, Wck, Wcv, wg)
            attend_and_tokens(nc, k, ahead, norm_x, shared, (sw1, sw3, sw2), x, W1, gamma, beta, b1, x1_dram, xn_dram, xnT_dram,
                              y_dram, table)
        experts(nc, k, ahead, w1, w2, w3, xn_dram, y_dram, table, out)


def prepare(nc, k, norm_x, ctx_in, Wq, Wk, Wv, Wcq, Wck, Wcv, wg):
    ident, causal, M, Gc, Vc, wgT = (k[n] for n in ("ident", "causal", "M", "G", "Vc", "wgT"))
    with ExitStack() as ctx:
        def sb(name, shape, dt=F32):
            return ctx.enter_context(nc.sbuf_tensor(name, shape, dt))

        def sem(name):
            return ctx.enter_context(nc.semaphore(name))

        raw = {n: k["V"][:, 4 * i:4 * i + 4, :] for i, n in enumerate(("Wq", "Wk", "Wcq", "Wck"))}
        raw["Wcv"], WqT, WkT, WcqT = (k["xnT"][:, c, :].rearrange("p (c n) -> p c n", c=C) for c in range(C))
        cx = sb("cx", [P, B, D])
        cxT = sb("cxT", [P, C, B * KC])
        KcT = sb("KcT", [P, C, B * KC])
        wg_sb = sb("wg_sb", [E, D])
        ps = ctx.enter_context(nc.psum_tensor("ps_prep", [P, 8, 512], F32))
        loaded = {n: sem(f"loaded_{n}") for n in ("Wq", "Wk", "Wv", "Wcq", "Wck", "Wcv", "cx", "wg")}
        iota_i = sb("iota_i", [P, E], I32)
        zeroed, const_ready = sem("zeroed"), sem("const_ready")
        filled, copied = sem("prep_filled"), sem("prep_copied")
        block = ctx.enter_context(nc.Block())

        @block.sync
        def _(sp):
            for n, w in (("Wq", Wq), ("Wk", Wk), ("Wcq", Wcq)):
                sp.dma_start(raw[n], w.rearrange("(c p) n -> p c n", p=P)).then_inc(loaded[n], 16)
            sp.dma_start(cx[:], ctx_in.rearrange("b p n -> p b n")).then_inc(loaded["cx"], 16)
            for n, w in (("Wck", Wck), ("Wcv", Wcv)):
                sp.dma_start(raw[n], w.rearrange("(c p) n -> p c n", p=P)).then_inc(loaded[n], 16)
            sp.dma_start(wg_sb[:], wg).then_inc(loaded["wg"], 16)
            sp.dma_start(k["Wv"][:], Wv.rearrange("(c p) n -> p c n", p=P)).then_inc(loaded["Wv"], 16)
            for g in range(2):
                norm_x.load(sp, g)
            sp.wait_ge(loaded["Wv"], 16)

        @block.gpsimd
        def _(pool):
            pool.memset(ident[:], 0.0).then_inc(zeroed, 1)
            pool.memset(causal[:], 0.0).then_inc(zeroed, 1)
            pool.memset(k["neg_half"][:], -0.5).then_inc(const_ready, 1)
            pool.iota(iota_i[:], [[1, E]], base=0, channel_multiplier=0).then_inc(const_ready, 1)
            pool.wait_ge(zeroed, 2)
            pool.affine_select(out=ident[:], in_=ident[:], compare_op=ALU.not_equal, fill=1.0, base=0,
                               pattern=[[-1, P]], channel_multiplier=1).then_inc(const_ready, 1)
            pool.affine_select(out=causal[:], in_=causal[:], compare_op=ALU.is_ge, fill=MASKED, base=0,
                               pattern=[[-1, P]], channel_multiplier=1).then_inc(const_ready, 1)
            pool.wait_ge(const_ready, 4)
            norm_x.rstd(pool, 0, k["neg_half"])

        def bank(step, j):
            return ps[:, 4 * (step % 2) + j, :]

        @block.tensor
        def _(pe):
            pe.wait_ge(const_ready, 4)

            def turn(step, src, tiles):
                for c in range(C):
                    for r in range(tiles):
                        last = pe.transpose(bank(step, c)[:, r * P:(r + 1) * P],
                                            src[:, r, c * P:(c + 1) * P], ident[:])
                last.then_inc(filled, 1)

            pe.wait_ge(loaded["Wq"], 16)
            turn(0, raw["Wq"], C)
            pe.wait_ge(loaded["Wk"], 16)
            turn(1, raw["Wk"], C)
            pe.wait_ge(loaded["Wcq"], 16)
            pe.wait_ge(copied, 1)
            turn(2, raw["Wcq"], C)
            pe.wait_ge(loaded["cx"], 16)
            pe.wait_ge(copied, 2)
            turn(3, cx, B)
            pe.wait_ge(copied, 3)
            for r in range(C):
                for d in range(C):
                    last = pe.matmul(bank(4, r), WqT[:, d, r * P:(r + 1) * P], WkT[:, d, :],
                                     start=(d == 0), stop=(d == C - 1))
            last.then_inc(filled, 1)
            pe.wait_ge(loaded["Wck"], 16)
            pe.wait_ge(copied, 4)
            for r in range(C):
                for e in range(C):
                    last = pe.matmul(bank(5, r)[:, 0:B * KC], raw["Wck"][:, e, r * P:(r + 1) * P], cxT[:, e, :],
                                     start=(e == 0), stop=(e == C - 1))
            last.then_inc(filled, 1)
            pe.wait_ge(copied, 6)
            for r in range(C):
                for d in range(C):
                    last = pe.matmul(bank(6, r)[:, 0:B * KC], WcqT[:, d, r * P:(r + 1) * P], KcT[:, d, :],
                                     start=(d == 0), stop=(d == C - 1))
            last.then_inc(filled, 1)
            pe.wait_ge(loaded["Wcv"], 16)
            pe.wait_ge(loaded["wg"], 16)
            for b in range(B):
                for e in range(C):
                    pe.matmul(bank(7, b), cxT[:, e, b * KC:(b + 1) * KC], raw["Wcv"][:, e, :],
                              start=(e == 0), stop=(e == C - 1))
            for c in range(C):
                last = pe.transpose(bank(7, 2)[:, c * E:(c + 1) * E], wg_sb[:, c * P:(c + 1) * P],
                                    ident[0:E, 0:E])
            last.then_inc(filled, 1)

        @block.vector
        def _(dve):
            dve.wait_ge(const_ready, 4)
            dve.tensor_copy(k["iota"][:], iota_i[:])
            copies = [(WqT, 512), (WkT, 512), (WcqT, 512), (cxT[:], B * KC), (M[:], 512),
                      (KcT[:], B * KC), (Gc[:], B * KC)]
            for step, (dst, n) in enumerate(copies):
                dve.wait_ge(filled, step + 1)
                lo = 4 * (step % 2)
                dve.tensor_copy(dst, ps[:, lo:lo + 4, 0:n]).then_inc(copied, 1)
                if step == 5:
                    norm_x.stats(dve, 0)
            dve.wait_ge(filled, 8)
            dve.tensor_copy(Vc[:], ps[:, 4:6, :]).then_inc(copied, 1)
            dve.tensor_copy(wgT[:], ps[:, 6, 0:C * E].rearrange("p (c e) -> p c e", c=C)).then_inc(copied, 1)
            norm_x.norm(dve, 0)


def wait_alone(eng, sem, value, passed):
    eng.wait_ge(sem, value)
    eng.sem_inc(passed, 1)


def ln_rstd(pool, rstd, veps, neg_half, mv, eps, eps_added, rstd_ready):
    pool.tensor_scalar(veps, mv[:, :, 1], eps, None, ALU.add).then_inc(eps_added.sem, 1)
    eps_added.n += 1
    eps_added.wait(pool)
    pool.tensor_tensor(rstd, veps, neg_half, ALU.pow).then_inc(rstd_ready, 1)


def ln_stats(dve, made, tiles, stats, mv, var_ready):
    for t, tile in enumerate(tiles):
        last = dve.bn_stats(stats[:, t, :], tile)
    made.inc(last)
    made.wait(dve)
    for t in range(len(tiles)):
        last = dve.bn_aggr(mv[:, t, :], stats[:, t, :])
    last.then_inc(var_ready, 1)


class FirstExpert:

    def __init__(self, nc, stack, weights, xn_dram, table):
        def sb(name, shape, dt=F32):
            return stack.enter_context(nc.sbuf_tensor(name, shape, dt))

        self.weights, self.xn_dram, self.table = weights, xn_dram, table
        self.raw = [sb(f"w_raw{m}", [P, C, D]) for m in range(3)]
        self.xe = sb("xe", [P, ST, D])
        self.slots = sb("slots", [P, E, ST, 2], I32)
        self.gather_ids = [sb(f"gather_ids{u}", [P, ST], I32) for u in range(2)]
        self.s = {n: stack.enter_context(nc.semaphore(n + "_e")) for n in
                  ("slots_loaded", "ids_ready", "gathered", "raw_hi", "raw_split")}
        self.raw_loaded = [stack.enter_context(nc.semaphore(f"raw_loaded{m}")) for m in range(3)]

    def load_slots(self, sp):
        sp.dma_start(self.slots[:], self.table[0:E * CAP, :].rearrange("(e p t) w -> p e (t w)", p=P, t=ST)
                     ).then_inc(self.s["slots_loaded"], 16)

    def load(self, sp, e, m):
        sp.dma_start(self.raw[m][:], self.weights[m][bass.ds(e, 1)].rearrange("e (c p) n -> (e p) c n", p=P)
                     ).then_inc(self.raw_loaded[m], 16)

    def split_hi(self, act, m):
        act.wait_ge(self.raw_loaded[m], 16)
        act.copy(self.W[m][0][:], self.raw[m][:]).then_inc(self.s["raw_hi"], 1)

    def split_lo(self, dve, m):
        dve.wait_ge(self.s["raw_hi"], m + 1)
        dve.tensor_tensor(self.W[m][1][:], self.raw[m][:], self.W[m][0][:].bitcast(F32), ALU.subtract
                          ).then_inc(self.s["raw_split"], 1)

    def ids(self, dve, e, u):
        dve.tensor_copy(self.gather_ids[u][:], self.slots[:, bass.ds(e, 1), :, 0].rearrange("p e t -> p (e t)")
                        ).then_inc(self.s["ids_ready"], 1)

    def gather(self, pool, e, u, passed):
        wait_alone(pool, self.s["ids_ready"], e + 1, passed)
        for t in range(ST):
            pool.indirect_dma_start(
                out=self.xe[:, t, :], out_offset=None, in_=self.xn_dram,
                in_offset=bass.IndirectOffsetOnAxis(ap=self.gather_ids[u][:, t:t + 1], axis=0)
            ).then_inc(self.s["gathered"], 16)


class XNorm:

    def __init__(self, nc, stack, XN, x):
        self.XN, self.x_v = XN, x.rearrange("b (g t p) d -> (b g) p t d", p=P, t=GT)
        self.m = {n: stack.enter_context(nc.sbuf_tensor(f"x_{n}", shape, F32))
                  for n, shape in (("stats", [P, GT, 6]), ("mv", [P, GT, 2]), ("rstd", [P, GT]), ("veps", [P, GT]))}
        self.s = {n: stack.enter_context(nc.semaphore(n + "_x")) for n in ("made", "var", "eps", "rstd_ready", "xn_ready")}
        self.loaded = [stack.enter_context(nc.semaphore(f"x_loaded{i}")) for i in range(3)]

    def load(self, sp, g):
        sp.dma_start(self.XN[g % 3][:], self.x_v[g]).then_inc(self.loaded[g % 3], 16)

    def stats(self, dve, g):
        dve.wait_ge(self.loaded[g % 3], 16 * (g // 3 + 1))
        for t in range(GT):
            last = dve.bn_stats(self.m["stats"][:, t, :], self.XN[g % 3][:, t, :])
        last.then_inc(self.s["made"], 1)
        dve.wait_ge(self.s["made"], g + 1)
        for t in range(GT):
            last = dve.bn_aggr(self.m["mv"][:, t, :], self.m["stats"][:, t, :])
        last.then_inc(self.s["var"], 1)

    def rstd(self, pool, g, neg_half):
        pool.wait_ge(self.s["var"], g + 1)
        pool.tensor_scalar(self.m["veps"][:], self.m["mv"][:, :, 1], EPS_X, None, ALU.add).then_inc(self.s["eps"], 1)
        pool.wait_ge(self.s["eps"], g + 1)
        pool.tensor_tensor(self.m["rstd"][:], self.m["veps"][:], neg_half[:], ALU.pow).then_inc(self.s["rstd_ready"], 1)

    def norm(self, dve, g):
        dve.wait_ge(self.s["rstd_ready"], g + 1)
        for t in range(GT):
            last = dve.tensor_scalar(self.XN[g % 3][:, t, :], self.XN[g % 3][:, t, :], self.m["mv"][:, t, 0:1],
                                     self.m["rstd"][:, t:t + 1], ALU.subtract, ALU.mult)
        last.then_inc(self.s["xn_ready"], 1)


def attention_order():
    order, waiting = [], None

    def products(a):
        return [("p", a, j) for j in range(a % QT // GT + 1)]

    for s in range(B * G):
        if s % G == 0 and waiting is not None:
            order += products(waiting)
            waiting = None
        order += [("x", s)] + [("q", s, c) for c in range(C)] + [("v", s, t) for t in range(GT)]
        for a in range(s * GT, (s + 1) * GT):
            order += [("s", a, j) for j in range(a % QT // GT + 1)]
            if waiting is not None:
                order += products(waiting)
            waiting = a
    return order + products(waiting)


TOKEN_STEPS = [
    ("stats1", "dve", 2.8), ("norm1a", "dve", 2.6), ("norm1b", "dve", 2.6), ("turn1a", "pe", 0), ("turn1b", "pe", 0),
    ("cscore", "pe", 0), ("cmax", "dve", 1.0), ("cturn", "pe", 0), ("cprod0", "pe", 0), ("c0", "dve", 1.4),
    ("cprod1", "pe", 0), ("c1", "dve", 1.4), ("stats2", "dve", 2.8), ("norm2a", "dve", 2.6), ("norm2b", "dve", 2.6),
    ("turn2a", "pe", 0), ("turn2b", "pe", 0), ("f0", "pe", 0), ("g0", "dve", 2.6), ("f1", "pe", 0),
    ("g1", "dve", 2.6), ("stats3", "dve", 2.8), ("norm3a", "dve", 2.6), ("norm3b", "dve", 2.6), ("x1", "dve", 2.6),
    ("stats4", "dve", 2.8), ("xn", "dve", 1.6), ("turn3a", "pe", 0), ("turn3b", "pe", 0), ("logits", "pe", 0),
    ("lmax", "dve", 0.5), ("groups", "dve", 2.5), ("keep", "dve", 2.0), ("choose", "dve", 2.5),
    ("hot", "dve", 2.5), ("rank", "pe", 0), ("place", "dve", 3.0), ("reach", "dve", 1.5),
    ("slots", "dve", 2.5)]
SCATTER_STEPS = 16


def shared_order(first, end):
    order = []
    for n in range(first, end):
        order += [("h", n, hc) for hc in range(C)] + [("z", n, half) for half in range(2)]
    return order


class SharedExpert:

    def __init__(self, nc, stack, x1_dram, xnT_dram, y_dram):
        def sb(name, shape, dt=F32):
            return stack.enter_context(nc.sbuf_tensor(name, shape, dt))

        self.x1_v = x1_dram.rearrange("(g t p) d -> g p t d", p=P, t=GT)
        self.y_v = y_dram[0:N, :].rearrange("(g t p) d -> g p t d", p=P, t=GT)
        self.xnT_dram = xnT_dram
        sw3_hi = sb("sw3_hi", [P, C, D], F32R)
        self.gate = sb("gate", [P, 4, GN])
        self.raw = sb("sw_raw", [P, C, D])
        sw3_lo = sb("sw3_lo", [P, C, D], F32R)
        self.xT = [sb(f"xT{i}", [P, C, GN]) for i in range(2)]
        xTs_hi = sb("xTs_hi", [P, C, GN], F32R)
        sw2 = tuple(sb(f"sw2_{part}", [P, C, D], F32R) for part in ("hi", "lo"))
        self.x1t, self.yt = sb("x1t", [P, GT, D]), sb("yt", [P, GT, D])
        self.xTs = (xTs_hi, sb("xTs_lo", [P, C, GN], F32R))
        self.gs = tuple(sb(f"gs_{part}", [P, C, GN], F32R) for part in ("hi", "lo"))
        self.sil = sb("sil", [P, 2, GN])
        sw1 = tuple(sb(f"sw1_{part}", [P, C, D], F32R) for part in ("hi", "lo"))
        self.W = [sw1, (sw3_hi, sw3_lo), sw2]
        names = ("sw_loaded sw_hi sw_split x1_loaded y_stored xs_hi xs_split sh_made silu_made gated gate_hi "
                 "g_split z_made y_ready").split()
        self.s = {n: stack.enter_context(nc.semaphore(n + "_s")) for n in names}
        self.xT_loaded = [stack.enter_context(nc.semaphore(f"xT_loaded{i}")) for i in range(2)]

    def load_weight(self, sp, m, w):
        if m:
            sp.wait_ge(self.s["sw_split"], m)
        sp.dma_start(self.raw[:], w.rearrange("(c p) n -> p c n", p=P)).then_inc(self.s["sw_loaded"], 16)

    def weight_hi(self, act, m):
        act.wait_ge(self.s["sw_loaded"], 16 * (m + 1))
        act.copy(self.W[m][0][:], self.raw[:]).then_inc(self.s["sw_hi"], 1)

    def weight_lo(self, dve, m):
        dve.wait_ge(self.s["sw_hi"], m + 1)
        dve.tensor_tensor(self.W[m][1][:], self.raw[:], self.W[m][0][:].bitcast(F32), ALU.subtract
                          ).then_inc(self.s["sw_split"], 1)

    def load_x(self, sp, n):
        if n >= 2:
            sp.wait_ge(self.s["xs_split"], n - 1)
        sp.dma_start(self.xT[n % 2][:], self.xnT_dram[n]).then_inc(self.xT_loaded[n % 2], 16)

    def x_hi(self, act, n):
        act.wait_ge(self.xT_loaded[n % 2], 16 * (n // 2 + 1))
        if n:
            act.wait_ge(self.s["sh_made"], n * C)
        act.copy(self.xTs[0][:], self.xT[n % 2][:]).then_inc(self.s["xs_hi"], 1)

    def x_lo(self, dve, n):
        dve.wait_ge(self.s["xs_hi"], n + 1)
        dve.tensor_tensor(self.xTs[1][:], self.xT[n % 2][:], self.xTs[0][:].bitcast(F32), ALU.subtract
                          ).then_inc(self.s["xs_split"], 1)

    def load_x1(self, sp, n):
        if n:
            sp.wait_ge(self.s["y_ready"], 2 * n)
        sp.dma_start(self.x1t[:], self.x1_v[n]).then_inc(self.s["x1_loaded"], 16)

    def pe_step(self, pe, ps, kind, n, j):
        s = self.s
        if kind == "h":
            if j == 0:
                if n == 0:
                    pe.wait_ge(s["sw_split"], 2)
                else:
                    pe.wait_ge(s["gated"], n * C)
                pe.wait_ge(s["xs_split"], n + 1)
            elif j < 3:
                if n:
                    pe.wait_ge(s["y_ready"], 2 * n - 2 + j)
            else:
                pe.wait_ge(s["gated"], n * C + 1)
            for m in range(2):
                for e in range(C):
                    mm = matmul(pe, ps[:, 2 * (j % 3) + m, :],
                                tuple(w[:, e, j * P:(j + 1) * P] for w in self.W[m]),
                                tuple(x[:, e, :] for x in self.xTs), e == 0, e == C - 1)
            mm.then_inc(s["sh_made"], 1)
        else:
            if n == 0:
                pe.wait_ge(s["sw_split"], 3)
            pe.wait_ge(s["gated"], n * C + 2 + j)
            for hc in range(C):
                if j == 0:
                    pe.wait_ge(s["g_split"], n * C + hc + 1)
                for i in range(2):
                    t = 2 * j + i
                    mm = matmul(pe, ps[:, 2 + 2 * j + i, :], tuple(g[:, hc, t * P:(t + 1) * P] for g in self.gs),
                                tuple(w[:, hc, :] for w in self.W[2]), hc == 0, hc == C - 1)
            mm.then_inc(s["z_made"], 1)

    def act_step(self, act, ps, kind, n, j):
        s = self.s
        if kind == "h":
            act.wait_ge(s["sh_made"], n * C + j + 1)
            if n * C + j >= 2:
                act.wait_ge(s["gated"], n * C + j - 1)
            act.activation(self.sil[:, j % 2, :], ps[:, 2 * (j % 3), :], ACT.Silu).then_inc(s["silu_made"], 1)
            act.wait_ge(s["gated"], n * C + j + 1)
            act.copy(self.gs[0][:, j, :], self.gate[:, j % 2, :]).then_inc(s["gate_hi"], 1)
        elif j == 0 and n + 1 < NT // GT:
            self.x_hi(act, n + 1)

    def dve_step(self, dve, ps, kind, n, j):
        s = self.s
        if kind == "h":
            dve.wait_ge(s["silu_made"], n * C + j + 1)
            if n * C + j >= 2:
                dve.wait_ge(s["g_split"], n * C + j - 1)
            dve.tensor_tensor(self.gate[:, j % 2, :], ps[:, 2 * (j % 3) + 1, :], self.sil[:, j % 2, :],
                              ALU.mult).then_inc(s["gated"], 1)
            dve.wait_ge(s["gate_hi"], n * C + j + 1)
            dve.tensor_tensor(self.gs[1][:, j, :], self.gate[:, j % 2, :], self.gs[0][:, j, :].bitcast(F32),
                              ALU.subtract).then_inc(s["g_split"], 1)
        else:
            if j == 0:
                if n + 1 < NT // GT:
                    self.x_lo(dve, n + 1)
                dve.wait_ge(s["x1_loaded"], 16 * (n + 1))
                if n:
                    dve.wait_ge(s["y_stored"], 16 * n)
            dve.wait_ge(s["z_made"], 2 * n + j + 1)
            dve.tensor_tensor(self.yt[:, 2 * j:2 * j + 2, :], ps[:, 2 + 2 * j:4 + 2 * j, :],
                              self.x1t[:, 2 * j:2 * j + 2, :], ALU.add).then_inc(s["y_ready"], 1)

    def sp_step(self, sp, kind, n, j):
        if kind == "h" and j == 0 and 2 <= n + 1 < NT // GT:
            self.load_x(sp, n + 1)
        if kind == "z" and j == 1:
            if n + 1 < NT // GT:
                self.load_x1(sp, n + 1)
            sp.wait_ge(self.s["y_ready"], 2 * n + 2)
            sp.dma_start(self.y_v[n], self.yt[:]).then_inc(self.s["y_stored"], 16)


def token_places(order):
    def takes_dve(step):
        kind, a, j = (*step, 0)[:3]
        return kind in "hz" or kind in "sp" and j == a % QT // GT

    product = 0.85
    start, now, done_at = [], 0.0, {}
    for kind, a, *j in order:
        start.append(now)
        tiles = min(4, a % QT + 1 - 4 * j[0]) if kind in "sp" else 4
        now += 6 * product if kind in "hz" else tiles * product
        if kind == "p":
            done_at[a // GT] = now
    start.append(now)
    places = [[] for _ in order]
    free, by_pe, p = 0.0, False, 0
    for s in range(B * G):
        at = max(free, done_at[s] + HOP)
        for name, who, cost in TOKEN_STEPS:
            if who == "pe":
                at += HOP
                p = max(p, int(np.searchsorted(start, at)) - 1)
                if p < len(order):
                    at = max(at, start[p + 1])
            else:
                if by_pe:
                    at += HOP
                p = max(p, int(np.searchsorted(start, at, side="right")) - 2)
                if p + 1 < len(order) and takes_dve(order[p + 1]) and at + cost / 2 > start[p + 2]:
                    p, at = p + 1, start[p + 2] + DVE_LAG
            by_pe = who == "pe"
            while p >= len(places):
                places.append([])
            places[p].append((name, s))
            at += cost * DVE_SHARE if who != "pe" else 0.0
        free = at
        for i in range(SCATTER_STEPS):
            q = max(p, int(np.searchsorted(start, at + i * SCATTER_EVERY, side="right")) - 1)
            while q >= len(places):
                places.append([])
            places[q].append((f"scatter{i}", s))
    return places


def attend_and_tokens(nc, k, ahead, norm_x, shared, shared_weights, x, W1, gamma, beta, b1, x1_dram, xn_dram, xnT_dram, y_dram, table):
    ident, causal, M, Wv, Gc, Vc, wgT = (k[n] for n in ("ident", "causal", "M", "Wv", "G", "Vc", "wgT"))
    order = attention_order() + shared_order(0, B * G)
    places = token_places(order)
    plan = [(order[p] if p < len(order) else None, places[p]) for p in range(len(places))]
    place_of = {token: p for p, (_, tokens) in enumerate(plan) for token in tokens}
    assert all(place_of["turn3b", g] < order.index(("h", g - 1, 0)) for g in range(1, B * G))
    groups_of = [a % QT // GT + 1 for a in range(B * QT)]
    first_bank = [{1: a % 4, 2: a % 2 * 2}.get(groups_of[a], 0) for a in range(B * QT)]
    first_group = [sum(groups_of[:a]) for a in range(B * QT)]
    x_stats_at = {("s", (s - 1) * GT + 1, groups_of[(s - 1) * GT + 1] - 1): s for s in range(1, B * G)}
    x_norm_at = {("s", (s - 1) * GT + 2, groups_of[(s - 1) * GT + 2] - 1): s for s in range(1, B * G)}
    last_tile = B * QT - 1
    shared_split_at = [("s", last_tile - 2, 0), ("p", last_tile - 1, 0), ("h", 0, 0)]
    x_v = x.rearrange("b (g t p) d -> (b g) p t d", p=P, t=GT)
    x1_v = x1_dram.rearrange("(g t p) d -> g p t d", p=P, t=GT)
    xn_v = xn_dram[0:N, :].rearrange("(g t p) d -> g p t d", p=P, t=GT)
    with ExitStack() as ctx:
        def sb(name, shape, dt=F32):
            return ctx.enter_context(nc.sbuf_tensor(name, shape, dt))

        def sem(name):
            return ctx.enter_context(nc.semaphore(name))

        XN, xnT, V, QM, probs, probsT = (k[n] for n in ("XN", "xnT", "V", "QM", "probs", "probsT"))
        A, H, T = k["A"], k["H"], k["T"]
        Tx = T[:]
        W1_sb = sb("W1_sb", [P, C, D])
        gam, bet, b1_sb = sb("gam", [P, D]), sb("bet", [P, D]), sb("b1_sb", [P, D])
        zero = sb("zero", [P, D])
        hot = zero[:].rearrange("p (t j e) -> p t j e", t=GT, j=TOPK)
        spare = sb("spare_slots", [P, ST, 2], I32)
        cprobs, cprobsT = (T[:, i, :].rearrange("p (t n) -> p t n", t=GT) for i in range(2))
        nmax, rsum, rinv = sb("nmax", [P, B * QT]), sb("rsum", [P, B * QT]), sb("rinv", [P, B * QT])
        m = {}
        for n, shape in (("stats", [P, GT, 6]), ("mv", [P, GT, 2]), ("rstd", [P, GT]), ("veps", [P, GT]),
                         ("cmax", [P, GT]), ("csum", [P, GT]), ("cinv", [P, GT]), ("lmax", [P, GT]),
                         ("lsum", [P, GT]), ("linv", [P, GT]), ("lexp", [P, GT, E]), ("score", [P, GT, E]),
                         ("gmax", [P, GT, NG]), ("gtop", [P, GT, 8]), ("gidf", [P, GT, 8]),
                         ("hot", [P, GT, NG, KEEP_G]), ("keep", [P, GT, NG]), ("drop", [P, GT, NG]),
                         ("kept", [P, GT, E]), ("masked", [P, GT, E]), ("etop", [P, GT, 8]),
                         ("eidf", [P, GT, TOPK]), ("wsum", [P, GT]), ("winv", [P, GT]), ("prefix", [P, P]),
                         ("ones", [P, P]), ("bit", [P, E]), ("run", [P, E]), ("more", [P, NW, E]), ("words", [P, NW, 2]),
                         ("spare0", [P, GT, TOPK]), ("token0", [P, GT, TOPK]), ("r_pos", [P, GT, TOPK]),
                         ("r_tile", [P, GT, TOPK]), ("r_scaled", [P, GT, TOPK]), ("r_keep", [P, GT, TOPK]),
                         ("r_slot", [P, GT, TOPK]), ("r_spare", [P, GT, TOPK]), ("r_away", [P, GT, TOPK])):
            m[n] = sb(n, shape)
        for n in ("gid", "eid"):
            m[n] = sb(n, [P, GT, 8], U32)
        m["mask"], m["prior"], m["pos"] = m["kept"], m["masked"], m["score"]
        spare_i, token_i = sb("spare_i", [P, GT, TOPK], I32), sb("token_i", [P, GT, TOPK], I32)
        slot, pair = sb("slot", [P, GT, TOPK], I32), sb("pair", [P, GT, TOPK, 2], I32)
        ps = ctx.enter_context(nc.psum_tensor("ps_att", [P, 8, 512], F32))
        PT, O, TK = 4, 5, 6

        names = ("w_loaded zeros_made spare_stored xn_turned xnT_copied "
                 "q_made q_copied v_made v_copied scored max_linked max_ready exped p_turned p_copied pv_used "
                 "rinv_ready a_ready linked stats_made var_ready eps_added rstd_ready h_ready turned T_copied cscored "
                 "cmax_ready cexped cturned cp_copied c_made c_copied f_made f_copied x1_ready xn2_ready logits_made "
                 "lmax_ready lexped x1_stored xn_stored xnT_stored x_again hot_made counted tri_zero tri_made iotas_made "
                 "bits_made ranks_read slots_ready scattered pool_passed").split()
        s = {n: sem(n + "_a") for n in names}
        block = ctx.enter_context(nc.Block())

        @block.sync
        def _(sp):
            sp.dma_start(W1_sb[:], W1.rearrange("(c p) n -> p c n", p=P)).then_inc(s["w_loaded"], 16)
            for dst, v in ((gam, gamma), (bet, beta), (b1_sb, b1)):
                sp.dma_start(dst[:], v.rearrange("(a n) -> a n", a=1).to_broadcast([P, D])
                             ).then_inc(s["w_loaded"], 16)
            for step, tokens in plan:
                if step and step[0] == "p" and step[1] % GT == GT - 1 and step[2] == groups_of[step[1]] - 1:
                    g = step[1] // GT + 3
                    if g < B * G:
                        sp.wait_ge(s["a_ready"], step[1] + 1)
                        norm_x.load(sp, g)
                    elif g == B * G:
                        sp.wait_ge(s["a_ready"], step[1] + 1)
                        shared.load_weight(sp, 0, shared_weights[0])
                if step == shared_split_at[0]:
                    shared.load_weight(sp, 1, shared_weights[1])
                if step == shared_split_at[1]:
                    sp.wait_ge(s["scored"], B * QT)
                    for n in range(2):
                        sp.wait_ge(s["xnT_stored"], 16 * (n + 1))
                        shared.load_x(sp, n)
                    shared.load_weight(sp, 2, shared_weights[2])
                if step == ("h", 0, 0):
                    sp.wait_ge(s["pv_used"], first_group[-1] + groups_of[-1])
                    sp.wait_ge(s["x1_stored"], 16)
                    shared.load_x1(sp, 0)
                if step and step[0] in "hz":
                    if step[1] + 1 < B * G and step[0] == "h" and step[2] == 0:
                        sp.wait_ge(s["xnT_stored"], 16 * (step[1] + 2))
                    if step[1] + 1 < B * G and step[0] == "z" and step[2] == 1:
                        sp.wait_ge(s["x1_stored"], 16 * (step[1] + 2))
                    shared.sp_step(sp, *step)
                if step == ("z", B * G - 2, 0):
                    sp.wait_ge(s["xn2_ready"], B * G)
                    sp.wait_ge(s["x1_stored"], 16 * B * G)
                    for i in range(3):
                        ahead.load(sp, 0, i)
                if step == ("h", B * G - 1, 2):
                    for n, value in (("scattered", NT * TOPK), ("xn_stored", B * G), ("xnT_stored", B * G)):
                        sp.wait_ge(s[n], 16 * value)
                    ahead.load_slots(sp)
                if step == ("x", 0):
                    norm_x.load(sp, 2)
                for name, g in tokens:
                    if name == "f1":
                        sp.wait_ge(s["f_made"], 2 * g + 2)
                        sp.dma_start(Tx, x_v[g]).then_inc(s["x_again"], 16)
                    if name == "x1":
                        sp.wait_ge(s["x1_ready"], g + 1)
                        sp.dma_start(x1_v[g], A[g % 3][:]).then_inc(s["x1_stored"], 16)
                    if name == "xn":
                        sp.wait_ge(s["xn2_ready"], g + 1)
                        sp.dma_start(xn_v[g], H[:]).then_inc(s["xn_stored"], 16)
                    if name == "turn3b":
                        sp.wait_ge(s["T_copied"], 6 * g + 6)
                        sp.dma_start(xnT_dram[g], T[:]).then_inc(s["xnT_stored"], 16)
            for n in ("x1_stored", "xn_stored", "xnT_stored"):
                sp.wait_ge(s[n], 16 * B * G)
            sp.wait_ge(shared.s["y_stored"], 16 * B * G)

        @block.gpsimd
        def _(pool):
            pool.memset(zero[:], 0.0).then_inc(s["zeros_made"], 1)
            pool.iota(spare[:, :, 0], [[1, ST]], base=N, channel_multiplier=ST).then_inc(s["zeros_made"], 1)
            pool.memset(spare[:, :, 1], 0).then_inc(s["zeros_made"], 1)

            pool.memset(m["prefix"][:], 1.0).then_inc(s["tri_zero"], 1)
            pool.memset(m["ones"][:], 1.0).then_inc(s["tri_made"], 1)
            pool.memset(m["run"][:], 0.0).then_inc(s["tri_made"], 1)
            for i in range(E // 2):
                pool.memset(m["bit"][:, 2 * i:2 * i + 2], float(2 ** i)).then_inc(s["bits_made"], 1)
            pool.iota(spare_i[:], [[P * TOPK, GT], [1, TOPK]], base=E * CAP,
                      channel_multiplier=TOPK).then_inc(s["iotas_made"], 1)
            pool.iota(token_i[:], [[P, GT], [0, TOPK]], base=0, channel_multiplier=1).then_inc(s["iotas_made"], 1)

            in_tok = Tally(s["eps_added"])
            pool.wait_ge(s["tri_zero"], 1)
            pool.affine_select(out=m["prefix"][:], in_=m["prefix"][:], compare_op=ALU.is_gt, fill=0.0, base=0,
                               pattern=[[1, P]], channel_multiplier=-1).then_inc(s["tri_made"], 1)
            pool.wait_ge(s["zeros_made"], 3)
            for dst in (xn_dram, y_dram):
                for t in range(ST):
                    pool.dma_start(dst[N + t * P:N + (t + 1) * P, :], zero[:]).then_inc(s["spare_stored"], 16)
            for e in range(E):
                pool.dma_start(table[e * CAP:(e + 1) * CAP, :].rearrange("(p t) w -> p (t w)", p=P),
                               spare[:].rearrange("p t w -> p (t w)")).then_inc(s["spare_stored"], 16)
            for step, tokens in plan:
                if step in x_stats_at:
                    norm_x.rstd(pool, x_stats_at[step], k["neg_half"])
                for name, g in tokens:
                    if name.startswith("stats"):
                        n = int(name[5]) - 1
                        pool.wait_ge(s["var_ready"], 4 * g + n + 1)
                        ln_rstd(pool, m["rstd"][:], m["veps"][:], k["neg_half"][:], m["mv"],
                                EPS_X if n == 3 else EPS_H, in_tok, s["rstd_ready"])
                    if name.startswith("scatter"):
                        if name == "scatter0":
                            pool.wait_ge(s["slots_ready"], g + 1)
                            if g == 0:
                                pool.wait_ge(s["spare_stored"], 16 * (2 * ST + E))
                        each = GT * TOPK // SCATTER_STEPS
                        for i in range(int(name[7:]) * each, (int(name[7:]) + 1) * each):
                            t, j = divmod(i, TOPK)
                            pool.indirect_dma_start(
                                out=table, out_offset=bass.IndirectOffsetOnAxis(ap=slot[:, t, j:j + 1], axis=0),
                                in_=pair[:, t, j, :], in_offset=None).then_inc(s["scattered"], 16)
            ahead.gather(pool, 0, 0, s["pool_passed"])
            pool.wait_ge(s["scattered"], 16 * NT * TOPK)
            pool.wait_ge(ahead.s["gathered"], 16 * ST)

        @block.tensor
        def _(pe):
            def turn_probs(a, j):
                i = first_group[a] + j
                pe.wait_ge(s["exped"], a + 1)
                if i:
                    pe.wait_ge(s["p_copied"], i)
                for t in range(4 * j, min(4 * j + 4, a % QT + 1)):
                    mm = pe.transpose(ps[:, PT, (t % 4) * P:(t % 4 + 1) * P],
                                      probs[:, a % 2, t * P:(t + 1) * P], ident[:])
                mm.then_inc(s["p_turned"], 1)

            def attend(kind, a, j=0):
                if kind == "x":
                    pe.wait_ge(norm_x.s["xn_ready"], a + 1)
                    if a:
                        pe.wait_ge(s["exped"], a * GT)
                    for c in range(C):
                        for t in range(GT):
                            mm = pe.transpose(ps[:, c, t * P:(t + 1) * P],
                                              XN[a % 3][:, t, c * P:(c + 1) * P], ident[:])
                    mm.then_inc(s["xn_turned"], 1)
                elif kind == "q":
                    pe.wait_ge(s["xnT_copied"], 2 * a + 2)
                    for e in range(C):
                        mm = pe.matmul(ps[:, j, :], M[:, e, j * P:(j + 1) * P],
                                       xnT[:, e, a % G * GN:(a % G + 1) * GN], start=(e == 0), stop=(e == C - 1))
                    mm.then_inc(s["q_made"], 1)
                elif kind == "v":
                    pe.wait_ge(s["q_copied"], a * C + j + 1)
                    at = (a % G * GT + j) * P
                    for e in range(C):
                        mm = pe.matmul(ps[:, j, :], xnT[:, e, at:at + P], Wv[:, e, :],
                                       start=(e == 0), stop=(e == C - 1))
                    mm.then_inc(s["v_made"], 1)
                elif kind == "s":
                    g, n = a // GT, (a % QT + 1) * P
                    bank = first_bank[a] + j
                    before = 4 // groups_of[a]
                    if a % GT == 0:
                        pe.wait_ge(s["q_copied"], g * C + C)
                    if a % GT < before:
                        pe.wait_ge(s["v_copied"], g * GT + bank + 1)
                    else:
                        pe.wait_ge(s["exped"], a - before + 1)
                    if j == 0 and a % QT and before == 1:
                        turn_probs(a - 1, 0)
                    w = min(512, n - 512 * j)
                    for c in range(C):
                        mm = pe.matmul(ps[:, bank, 0:w], QM[:, c, a % GT * P:(a % GT + 1) * P],
                                       xnT[:, c, 512 * j:512 * j + w], start=(c == 0), stop=(c == C - 1))
                    if j == groups_of[a] - 1:
                        mm.then_inc(s["scored"], 1)
                    if j == 0 and a % QT and before > 1:
                        turn_probs(a - 1, 0)
                else:
                    i = first_group[a] + j
                    if j == 0:
                        if a % QT == QT - 1:
                            turn_probs(a, 0)
                        if a:
                            pe.wait_ge(s["a_ready"], a)
                    pe.wait_ge(s["p_copied"], i + 1)
                    if j + 1 < groups_of[a]:
                        turn_probs(a, j + 1)
                    if j == 0 and a % GT == 0:
                        pe.wait_ge(s["v_copied"], (a // GT + 1) * GT)
                    for t in range(4 * j, min(4 * j + 4, a % QT + 1)):
                        mm = pe.matmul(ps[:, O, :], probsT[:, i % 2, (t % 4) * P:(t % 4 + 1) * P],
                                       V[:, t, :], start=(t == 0), stop=(t == a % QT))
                    mm.then_inc(s["pv_used"], 1)

            def token(name, g):
                if name[:4] == "turn":
                    n, half = int(name[4]) - 1, "ab".index(name[5])
                    if half:
                        pe.wait_ge(s["T_copied"], 6 * g + 2 * n + 1)
                    elif n < 2:
                        pe.wait_ge(s["h_ready"], 2 * g + n + 1)
                    else:
                        pe.wait_ge(s["xn2_ready"], g + 1)
                    if n == 0 and half == 0 and g:
                        pe.wait_ge(s["lexped"], g)
                        pe.wait_ge(s["ranks_read"], g)
                    for i in range(2):
                        c = 2 * half + i
                        for t in range(GT):
                            mm = pe.transpose(ps[:, TK + i, t * P:(t + 1) * P], H[:, t, c * P:(c + 1) * P], ident[:])
                    mm.then_inc(s["turned"], 1)
                elif name == "cscore":
                    pe.wait_ge(s["T_copied"], 6 * g + 2)
                    for t in range(GT):
                        for e in range(C):
                            mm = pe.matmul(ps[:, TK, t * KC:(t + 1) * KC], T[:, e, t * P:(t + 1) * P],
                                           Gc[:, e, g // G * KC:(g // G + 1) * KC], start=(e == 0), stop=(e == C - 1))
                    mm.then_inc(s["cscored"], 1)
                elif name == "cturn":
                    pe.wait_ge(s["cexped"], g + 1)
                    for t in range(GT):
                        mm = pe.transpose(ps[:, TK + 1, t * P:(t + 1) * P], cprobs[:, t, :], ident[:])
                    mm.then_inc(s["cturned"], 1)
                elif name[:5] == "cprod":
                    half = int(name[5])
                    pe.wait_ge(s["cp_copied"], g + 1)
                    if half:
                        pe.wait_ge(s["c_copied"], 2 * g + 1)
                    for i in range(2):
                        mm = pe.matmul(ps[:, TK + i, :], cprobsT[:, 2 * half + i, :], Vc[:, g // G, :],
                                       start=True, stop=True)
                    mm.then_inc(s["c_made"], 1)
                elif name in ("f0", "f1"):
                    half = int(name[1])
                    pe.wait_ge(s["T_copied"], 6 * g + 4)
                    if g == 0:
                        pe.wait_ge(s["w_loaded"], 64)
                    if half:
                        pe.wait_ge(s["f_copied"], 2 * g + 1)
                    for i in range(2):
                        t = 2 * half + i
                        for e in range(C):
                            mm = pe.matmul(ps[:, TK + i, :], T[:, e, t * P:(t + 1) * P], W1_sb[:, e, :],
                                           start=(e == 0), stop=(e == C - 1))
                    mm.then_inc(s["f_made"], 1)
                elif name == "logits":
                    pe.wait_ge(s["T_copied"], 6 * g + 6)
                    for t in range(GT):
                        for e in range(C):
                            mm = pe.matmul(ps[:, TK, t * E:(t + 1) * E], T[:, e, t * P:(t + 1) * P],
                                           wgT[:, e, :], start=(e == 0), stop=(e == C - 1))
                    mm.then_inc(s["logits_made"], 1)
                elif name == "rank":
                    pe.wait_ge(s["tri_made"], 3)
                    pe.wait_ge(s["hot_made"], g + 1)
                    for i, ones in enumerate(("prefix", "ones")):
                        mm = pe.matmul(ps[:, TK + 1, i * GT * E:(i + 1) * GT * E], m[ones][:],
                                       m["mask"][:].rearrange("p t e -> p (t e)"), start=True, stop=True)
                    mm.then_inc(s["counted"], 1)

            for step, tokens in plan:
                if step and step[0] in "hz":
                    if step == ("h", 0, 0):
                        pe.wait_ge(s["exped"], B * QT)
                        pe.wait_ge(s["p_copied"], first_group[-1] + groups_of[-1])
                        pe.wait_ge(s["a_ready"], B * QT)
                    shared.pe_step(pe, ps, *step)
                elif step:
                    attend(*step)
                for name, g in tokens:
                    token(name, g)

        @block.scalar
        def _(act):
            def copy_probs(a, j):
                i = first_group[a] + j
                act.wait_ge(s["p_turned"], i + 1)
                if i >= 2:
                    act.wait_ge(s["pv_used"], i - 1)
                w = min(512, (a % QT + 1) * P - 512 * j)
                act.copy(probsT[:, i % 2, 0:w], ps[:, PT, 0:w]).then_inc(s["p_copied"], 1)

            def attend(kind, a, j=0):
                if kind == "x":
                    act.wait_ge(s["xn_turned"], a + 1)
                    for h in range(2):
                        act.copy(xnT[:, 2 * h:2 * h + 2, a % G * GN:(a % G + 1) * GN], ps[:, 2 * h:2 * h + 2, :]
                                 ).then_inc(s["xnT_copied"], 1)
                elif kind == "q":
                    act.wait_ge(s["q_made"], a * C + j + 1)
                    act.copy(QM[:, j, :], ps[:, j, :]).then_inc(s["q_copied"], 1)
                elif kind == "v":
                    act.wait_ge(s["v_made"], a * GT + j + 1)
                    act.copy(V[:, a % G * GT + j, :], ps[:, j, :]).then_inc(s["v_copied"], 1)
                elif kind == "s":
                    if j == 0 and a % QT:
                        copy_probs(a - 1, 0)
                    if j == groups_of[a] - 1:
                        act.wait_ge(s["max_ready"], a + 1)
                        flat = ps[:, first_bank[a]:4, :].rearrange("p k n -> p (k n)")[:, 0:(a % QT + 1) * P]
                        act.activation(probs[:, a % 2, 0:(a % QT + 1) * P], flat, ACT.Exp, bias=nmax[:, a:a + 1],
                                       scale=SCALE, accum_out=rsum[:, a:a + 1]).then_inc(s["exped"], 1)
                else:
                    if j == 0 and a % QT == QT - 1:
                        copy_probs(a, 0)
                    if j + 1 < groups_of[a]:
                        copy_probs(a, j + 1)

            def token(name, g):
                if name[:4] == "turn":
                    n, half = int(name[4]) - 1, "ab".index(name[5])
                    act.wait_ge(s["turned"], 6 * g + 2 * n + half + 1)
                    if n == 0 and half == 0 and g:
                        act.wait_ge(s["xnT_stored"], 16 * g)
                    act.copy(T[:, 2 * half:2 * half + 2, :], ps[:, TK:TK + 2, :]).then_inc(s["T_copied"], 1)
                elif name == "cmax":
                    act.wait_ge(s["cmax_ready"], g + 1)
                    for t in range(GT):
                        last = act.activation(cprobs[:, t, :], ps[:, TK, t * KC:(t + 1) * KC], ACT.Exp,
                                              bias=m["cmax"][:, t:t + 1], scale=SCALE,
                                              accum_out=m["csum"][:, t:t + 1])
                    last.then_inc(s["cexped"], 1)
                elif name == "cturn":
                    act.wait_ge(s["cturned"], g + 1)
                    act.copy(T[:, 1, :], ps[:, TK + 1, :]).then_inc(s["cp_copied"], 1)
                elif name == "lmax":
                    act.wait_ge(s["lmax_ready"], g + 1)
                    for t in range(GT):
                        last = act.activation(m["lexp"][:, t, :], ps[:, TK, t * E:(t + 1) * E], ACT.Exp,
                                              bias=m["lmax"][:, t:t + 1], scale=1.0,
                                              accum_out=m["lsum"][:, t:t + 1])
                    last.then_inc(s["lexped"], 1)

            for step, tokens in plan:
                if step == ("z", B * G - 1, 0):
                    act.wait_ge(shared.s["sw_split"], 3)
                    ahead.split_hi(act, 0)
                    act.wait_ge(shared.s["xs_split"], B * G)
                    ahead.split_hi(act, 1)
                if step and step[0] in "hz":
                    shared.act_step(act, ps, *step)
                elif step:
                    attend(*step)
                if step == shared_split_at[0]:
                    act.wait_ge(s["q_made"], B * G * C)
                    shared.weight_hi(act, 0)
                if step == shared_split_at[1]:
                    act.wait_ge(s["a_ready"], (B * G - 1) * GT)
                    shared.weight_hi(act, 1)
                    act.wait_ge(s["scored"], B * QT)
                    shared.x_hi(act, 0)
                if step == shared_split_at[2]:
                    act.wait_ge(s["pv_used"], first_group[-1] + groups_of[-1])
                    shared.weight_hi(act, 2)
                for name, g in tokens:
                    token(name, g)

        @block.vector
        def _(dve):
            chain, in_tok, in_max = (Tally(s[n]) for n in ("linked", "stats_made", "max_linked"))

            def link(ins, tally=chain):
                tally.inc(ins)
                tally.wait(dve)

            def attend(kind, a, j=0):
                if kind == "s" and j == groups_of[a] - 1:
                    dve.wait_ge(s["scored"], a + 1)
                    col = a % QT * P
                    diag = ps[:, first_bank[a] + col // 512, col % 512:col % 512 + P]
                    link(dve.tensor_tensor(diag, diag, causal[:], ALU.add), in_max)
                    flat = ps[:, first_bank[a]:4, :].rearrange("p k n -> p (k n)")[:, 0:col + P]
                    link(dve.tensor_reduce(nmax[:, a:a + 1], flat, AX.X, ALU.max), in_max)
                    dve.tensor_scalar(nmax[:, a:a + 1], nmax[:, a:a + 1], -SCALE, None,
                                      ALU.mult).then_inc(s["max_ready"], 1)
                if kind == "p" and j == groups_of[a] - 1:
                    dve.wait_ge(s["exped"], a + 1)
                    dve.reciprocal(rinv[:, a:a + 1], rsum[:, a:a + 1]).then_inc(s["rinv_ready"], 1)
                    dve.wait_ge(s["rinv_ready"], a + 1)
                    dve.wait_ge(s["pv_used"], first_group[a] + groups_of[a])
                    g = a // GT
                    if g >= 3 and a % GT == 0:
                        dve.wait_ge(s["x1_stored"], 16 * (g - 2))
                    dve.scalar_tensor_tensor(out=A[g % 3][:, a % GT], in0=ps[:, O, :], scalar=rinv[:, a:a + 1],
                                             in1=XN[g % 3][:, a % GT], op0=ALU.mult, op1=ALU.add
                                             ).then_inc(s["a_ready"], 1)

            def token(name, g):
                At = A[g % 3]
                if name[:5] == "stats":
                    if name == "stats1":
                        dve.wait_ge(s["a_ready"], (g + 1) * GT)
                    ln_stats(dve, in_tok, [At[:, t, :] for t in range(GT)], m["stats"], m["mv"], s["var_ready"])
                elif name[:4] == "norm":
                    n, dst = int(name[4]) - 1, (At if name[4] == "3" else H)
                    if name[5] == "a":
                        dve.wait_ge(s["var_ready"], 4 * g + n + 1)
                        if g == 0:
                            dve.wait_ge(s["w_loaded"], 64)
                        if n == 0 and g:
                            dve.wait_ge(s["xn_stored"], 16 * g)
                        for t in range(GT):
                            last = dve.scalar_tensor_tensor(out=dst[:, t, :], in0=At[:, t, :],
                                                            scalar=m["mv"][:, t, 0:1], in1=gam[:],
                                                            op0=ALU.subtract, op1=ALU.mult)
                        link(last)
                    else:
                        dve.wait_ge(s["rstd_ready"], 4 * g + n + 1)
                        for t in range(GT):
                            last = dve.scalar_tensor_tensor(out=dst[:, t, :], in0=dst[:, t, :],
                                                            scalar=m["rstd"][:, t:t + 1], in1=bet[:],
                                                            op0=ALU.mult, op1=ALU.add)
                        if n < 2:
                            last.then_inc(s["h_ready"], 1)
                        else:
                            link(last)
                elif name == "cmax":
                    dve.wait_ge(s["cscored"], g + 1)
                    link(dve.tensor_reduce(m["cmax"][:], ps[:, TK, :].rearrange("p (t n) -> p t n", t=GT),
                                           AX.X, ALU.max))
                    dve.tensor_scalar(m["cmax"][:], m["cmax"][:], -SCALE, None, ALU.mult).then_inc(s["cmax_ready"], 1)
                elif name in ("c0", "c1"):
                    half = int(name[1])
                    if not half:
                        dve.wait_ge(s["cexped"], g + 1)
                        link(dve.reciprocal(m["cinv"][:], m["csum"][:]))
                    dve.wait_ge(s["c_made"], 2 * g + half + 1)
                    for i in range(2):
                        t = 2 * half + i
                        last = dve.scalar_tensor_tensor(out=At[:, t, :], in0=ps[:, TK + i, :],
                                                        scalar=m["cinv"][:, t:t + 1], in1=H[:, t, :],
                                                        op0=ALU.mult, op1=ALU.add)
                    last.then_inc(s["c_copied"], 1)
                    dve.wait_ge(s["c_copied"], 2 * g + half + 1)
                elif name in ("g0", "g1"):
                    half = int(name[1])
                    dve.wait_ge(s["f_made"], 2 * g + half + 1)
                    for i in range(2):
                        t = 2 * half + i
                        last = dve.tensor_tensor(At[:, t, :], ps[:, TK + i, :], b1_sb[:], ALU.add)
                    last.then_inc(s["f_copied"], 1)
                    dve.wait_ge(s["f_copied"], 2 * g + half + 1)
                    for i in range(2):
                        t = 2 * half + i
                        last = dve.scalar_tensor_tensor(out=At[:, t, :], in0=At[:, t, :], scalar=0.0,
                                                        in1=H[:, t, :], op0=ALU.max, op1=ALU.add)
                    link(last)
                elif name == "x1":
                    dve.wait_ge(s["x_again"], 16 * (g + 1))
                    for t in range(GT):
                        last = dve.scalar_tensor_tensor(out=At[:, t, :], in0=At[:, t, :], scalar=0.0,
                                                        in1=T[:, t, :], op0=ALU.max, op1=ALU.add)
                    last.then_inc(s["x1_ready"], 1)
                    dve.wait_ge(s["x1_ready"], g + 1)
                elif name == "xn":
                    dve.wait_ge(s["rstd_ready"], 4 * g + 4)
                    for t in range(GT):
                        last = dve.tensor_scalar(H[:, t, :], At[:, t, :], m["mv"][:, t, 0:1],
                                                 m["rstd"][:, t:t + 1], ALU.subtract, ALU.mult)
                    last.then_inc(s["xn2_ready"], 1)
                elif name == "lmax":
                    dve.wait_ge(s["logits_made"], g + 1)
                    lg = ps[:, TK, 0:GT * E].rearrange("p (t e) -> p t e", t=GT)
                    link(dve.tensor_reduce(m["lmax"][:], lg, AX.X, ALU.max))
                    dve.tensor_scalar(m["lmax"][:], m["lmax"][:], -1.0, None, ALU.mult).then_inc(s["lmax_ready"], 1)
                elif name == "groups":
                    dve.wait_ge(s["lexped"], g + 1)
                    link(dve.reciprocal(m["linv"][:], m["lsum"][:]))
                    link(dve.tensor_tensor(m["score"][:], m["lexp"][:],
                                           m["linv"][:].rearrange("p (t a) -> p t a", a=1).to_broadcast([P, GT, E]),
                                           ALU.mult))
                    link(dve.tensor_reduce(m["gmax"][:].rearrange("p t g -> p (t g)"),
                                           m["score"][:].rearrange("p t (g a) -> p (t g) a", g=NG), AX.X, ALU.max))
                    for t in range(GT):
                        last = dve.max(m["gtop"][:, t, :], m["gmax"][:, t, :])
                    link(last)
                    for t in range(GT):
                        last = dve.max_index(m["gid"][:, t, :], m["gtop"][:, t, :], m["gmax"][:, t, :])
                    link(last)
                elif name == "keep":
                    link(dve.tensor_copy(m["gidf"][:], m["gid"][:]))
                    for t in range(GT):
                        last = dve.tensor_tensor(
                            m["hot"][:, t, :, :],
                            m["gidf"][:, t, 0:KEEP_G].rearrange("p (a j) -> p a j", a=1).to_broadcast([P, NG, KEEP_G]),
                            k["iota"][:, 0:NG].rearrange("p (g a) -> p g a", a=1).to_broadcast([P, NG, KEEP_G]),
                            ALU.is_equal)
                    link(last)
                    link(dve.tensor_reduce(m["keep"][:], m["hot"][:], AX.X, ALU.add))
                    link(dve.tensor_scalar(m["drop"][:], m["keep"][:], -1.0, None, ALU.add))
                elif name == "choose":
                    def of_group(tile):
                        return tile[:].rearrange("p t (g a) -> p (t g) a", a=1).to_broadcast([P, GT * NG, E // NG])

                    link(dve.tensor_tensor(m["kept"][:].rearrange("p t (g a) -> p (t g) a", g=NG),
                                           m["score"][:].rearrange("p t (g a) -> p (t g) a", g=NG),
                                           of_group(m["keep"]), ALU.mult))
                    link(dve.tensor_tensor(m["masked"][:].rearrange("p t (g a) -> p (t g) a", g=NG),
                                           m["kept"][:].rearrange("p t (g a) -> p (t g) a", g=NG),
                                           of_group(m["drop"]), ALU.add))
                    for t in range(GT):
                        last = dve.max(m["etop"][:, t, :], m["masked"][:, t, :])
                    link(last)
                    for t in range(GT):
                        last = dve.max_index(m["eid"][:, t, :], m["etop"][:, t, :], m["masked"][:, t, :])
                    link(last)
                    link(dve.tensor_copy(m["eidf"][:], m["eid"][:, :, 0:TOPK]))
                elif name == "hot":
                    if g == 0:
                        dve.wait_ge(s["spare_stored"], 16 * (2 * ST + E))
                    link(dve.tensor_tensor(hot.rearrange("p t j e -> p (t j) e"),
                                           m["eidf"][:].rearrange("p t (j a) -> p (t j) a", a=1).to_broadcast([P, GT * TOPK, E]),
                                           k["iota"][:].rearrange("p (a e) -> p a e", a=1).to_broadcast([P, GT * TOPK, E]),
                                           ALU.is_equal))
                    dve.tensor_reduce(m["mask"][:], hot.rearrange("p t j e -> p t e j"), AX.X, ALU.add
                                      ).then_inc(s["hot_made"], 1)
                    link(dve.tensor_reduce(m["wsum"][:], m["etop"][:, :, 0:TOPK], AX.X, ALU.add))
                    link(dve.tensor_scalar(m["wsum"][:], m["wsum"][:], 1e-9, None, ALU.add))
                    link(dve.reciprocal(m["winv"][:], m["wsum"][:]))
                    if g:
                        dve.wait_ge(s["scattered"], 16 * GT * TOPK * g)
                    link(dve.tensor_tensor(pair[:, :, :, 1].bitcast(F32), m["etop"][:, :, 0:TOPK],
                                           m["winv"][:].rearrange("p (t a) -> p t a", a=1).to_broadcast([P, GT, TOPK]),
                                           ALU.mult))
                elif name == "place":
                    if g == 0:
                        dve.wait_ge(s["iotas_made"], 2)
                        dve.tensor_copy(m["spare0"][:], spare_i[:])
                        link(dve.tensor_copy(m["token0"][:], token_i[:]))
                    dve.wait_ge(s["counted"], g + 1)
                    if g == 0:
                        dve.wait_ge(s["tri_made"], 3)
                    rank, total = (ps[:, TK + 1, i * GT * E:(i + 1) * GT * E].rearrange("p (t e) -> p t e", t=GT)
                                   for i in range(2))
                    dve.tensor_scalar(pair[:, :, :, 0], m["token0"][:], float(g * GN), None, ALU.add)
                    dve.tensor_scalar(m["r_spare"][:], m["spare0"][:], float(g * GN * TOPK), None, ALU.add)
                    link(dve.tensor_copy(m["prior"][:, 0, :], m["run"][:]))
                    for t in range(1, GT):
                        link(dve.tensor_tensor(m["prior"][:, t, :], m["prior"][:, t - 1, :], total[:, t - 1, :], ALU.add))
                    dve.tensor_tensor(m["run"][:], m["prior"][:, GT - 1, :], total[:, GT - 1, :], ALU.add)
                    last = dve.tensor_tensor(m["pos"][:], rank, m["prior"][:], ALU.add)
                    last.then_inc(s["ranks_read"], 1)
                    dve.wait_ge(s["ranks_read"], g + 1)
                elif name == "reach":
                    for j in range(TOPK):
                        last = dve.tensor_tensor(hot[:, :, j, :], hot[:, :, j, :], m["pos"][:], ALU.mult)
                    link(last)
                    link(dve.tensor_reduce(m["r_pos"][:], hot, AX.X, ALU.add))
                elif name == "slots":
                    dve.tensor_scalar(m["r_keep"][:], m["r_pos"][:], float(CAP), None, ALU.is_lt)
                    dve.tensor_scalar(m["r_scaled"][:], m["r_pos"][:], float(ST), None, ALU.mult)
                    link(dve.tensor_scalar(m["r_tile"][:], m["r_pos"][:], float(P), None, ALU.is_ge))
                    for t in range(2, ST):
                        link(dve.scalar_tensor_tensor(out=m["r_tile"][:], in0=m["r_pos"][:], scalar=float(t * P),
                                                      in1=m["r_tile"][:], op0=ALU.is_ge, op1=ALU.add))
                    link(dve.scalar_tensor_tensor(out=m["r_scaled"][:], in0=m["r_tile"][:], scalar=1.0 - P * ST,
                                                  in1=m["r_scaled"][:], op0=ALU.mult, op1=ALU.add))
                    link(dve.scalar_tensor_tensor(out=m["r_slot"][:], in0=m["eidf"][:], scalar=float(CAP),
                                                  in1=m["r_scaled"][:], op0=ALU.mult, op1=ALU.add))
                    link(dve.tensor_tensor(m["r_away"][:], m["r_slot"][:], m["r_spare"][:], ALU.subtract))
                    link(dve.tensor_tensor(m["r_away"][:], m["r_away"][:], m["r_keep"][:], ALU.mult))
                    link(dve.tensor_tensor(m["r_slot"][:], m["r_away"][:], m["r_spare"][:], ALU.add))
                    dve.tensor_copy(slot[:], m["r_slot"][:]).then_inc(s["slots_ready"], 1)
                    if g == B * G - 1:
                        dve.wait_ge(s["bits_made"], E // 2)
                        for i in range(NW):
                            last = dve.tensor_scalar(m["more"][:, i, :], m["run"][:], float(WIDTHS[i]), None,
                                                     ALU.is_gt)
                        link(last)
                        for i in range(NW):
                            last = dve.tensor_tensor(m["more"][:, i, :], m["more"][:, i, :], m["bit"][:], ALU.mult)
                        link(last)
                        link(dve.tensor_reduce(m["words"][:], m["more"][:].rearrange("p m (i u) -> p m u i", u=2),
                                               AX.X, ALU.add))
                        link(dve.tensor_copy(k["fuller"][:], m["words"][:]))

            for step, tokens in plan:
                if step == ("z", B * G - 1, 0):
                    dve.wait_ge(ahead.s["slots_loaded"], 16)
                    ahead.ids(dve, 0, 0)
                    ahead.split_lo(dve, 0)
                    dve.wait_ge(shared.s["sh_made"], B * G * C)
                    ahead.split_lo(dve, 1)
                if step and step[0] in "hz":
                    shared.dve_step(dve, ps, *step)
                elif step:
                    attend(*step)
                    if step in x_stats_at:
                        norm_x.stats(dve, x_stats_at[step])
                    if step in x_norm_at:
                        norm_x.norm(dve, x_norm_at[step])
                if step == shared_split_at[0]:
                    dve.wait_ge(s["v_made"], B * G * GT)
                    shared.weight_lo(dve, 0)
                if step == shared_split_at[1]:
                    dve.wait_ge(s["scored"], B * QT)
                    shared.weight_lo(dve, 1)
                    shared.x_lo(dve, 0)
                if step == shared_split_at[2]:
                    shared.weight_lo(dve, 2)
                for name, g in tokens:
                    token(name, g)


def experts(nc, k, ahead, w1, w2, w3, xn_dram, y_dram, table, out):
    ident = k["ident"]
    with ExitStack() as ctx:
        def sb(name, shape, dt=F32):
            return ctx.enter_context(nc.sbuf_tensor(name, shape, dt))

        def sem(name):
            return ctx.enter_context(nc.semaphore(name))

        parts = ("hi", "lo")
        raw, slots, xe = ahead.raw, ahead.slots, ahead.xe
        sb("allocated_ahead", [P, ahead.size])
        W = [ahead.W, [tuple(sb(f"w{m}_{part}", [P, C, D], F32R) for part in parts) for m in (1, 3)]]
        W2 = ahead.W2
        add_ids, weight = sb("add_ids", [P, ST], I32), sb("weight", [P, ST])
        xT = tuple(sb(f"xeT_{part}", [P, C, CAP], F32R) for part in parts)
        sil = sb("sil_e", [P, CAP])
        gate = sb("gate_e", [P, 2, CAP])
        gs = tuple(sb(f"ge_{part}", [P, C, CAP], F32R) for part in parts)
        o = sb("o_e", [P, ST, D])
        ps = ctx.enter_context(nc.psum_tensor("ps_exp", [P, 8, 512], F32))
        names = ("turned xT_hi xT_split h_made silu_made gated "
                 "gate_hi g_split o_made o_ready added o_free weight_ready sp_passed dve_passed pool_passed out_stored").split()
        s = {n: sem(n + "_e") for n in names}
        s.update(ahead.s)
        raw_loaded = ahead.raw_loaded
        block = ctx.enter_context(nc.Block())

        def pairs(eng, body):
            with eng.Fori(0, E // 2 - 1) as i:
                for u in range(2):
                    body(i, u, False)
            for u in range(2):
                body(E // 2 - 1, u, True)

        def load_fuller(eng):
            regs = [eng.alloc_register(f"fuller{i}") for i in range(2 * NW)]
            eng.load(regs, k["fuller"][0:1, :, :].rearrange("p m u -> p (m u)"))
            words = [eng.snap(r, min_val=0, max_val=2 ** (E // 2) - 1) for r in regs]
            return [words[2 * m:2 * m + 2] for m in range(NW)]

        def by_width(eng, fuller, i, u, body, low=0, high=NW):
            if low == high:
                body(WIDTHS[low])
                return
            mid = (low + high) // 2
            with eng.If(((fuller[mid][u] >> i) & 1) == 1):
                by_width(eng, fuller, i, u, body, mid + 1, high)
            with eng.Else():
                by_width(eng, fuller, i, u, body, low, mid)

        o_bank = [0, 4, 5, 6, 7]
        turned_before = {0: 1, 1: 3, 3: 4}

        def pieces(width):
            cuts = 1 if width <= 512 else 2
            return [slice(h * width // cuts, (h + 1) * width // cuts) for h in range(cuts)]

        def tiles_of(width):
            tiles = -(-width // P)
            return [(t, min(P, width - t * P), 1 if t < tiles - 1 else ST - t) for t in range(tiles)]

        @block.sync
        def _(sp):
            for m in range(2):
                sp.wait_ge(s["raw_split"], m + 1)
                ahead.load(sp, 1, m)

            def body(i, u, last):
                e = i * 2 + u
                for n, m in enumerate((0, 2, 1)):
                    further = 2 if m < 2 else 1
                    if not (last and u + further > 1):
                        wait_alone(sp, s["raw_split"], e * 3 + 2 + n + 1, s["sp_passed"])
                        ahead.load(sp, e + further, m)

            pairs(sp, body)
            sp.wait_ge(s["added"], 16 * ST * E)
            for g in range(8):
                rows = slice(g * N // 8, (g + 1) * N // 8)
                sp.dma_start(out[rows, :], y_dram[rows, :]).then_inc(s["out_stored"], 16)
            sp.wait_ge(s["out_stored"], 16 * 8)

        @block.gpsimd
        def _(pool):
            pool.memset(o[:], 0.0).then_inc(s["o_free"], 1)

            def body(i, u, last):
                e = i * 2 + u
                if not (last and u):
                    wait_alone(pool, s["turned"], e * C + C, s["pool_passed"])
                    ahead.gather(pool, e + 1, 1 - u, s["pool_passed"])
                for t in range(ST):
                    wait_alone(pool, s["o_ready"], e * ST + ST + t + 1, s["pool_passed"])
                    pool.indirect_dma_start(
                        out=y_dram, out_offset=bass.IndirectOffsetOnAxis(ap=add_ids[:, t:t + 1], axis=0),
                        in_=o[:, t, :], in_offset=None, compute_op=ALU.add).then_inc(s["added"], 16)
                wait_alone(pool, s["added"], e * (16 * ST) + 16 * ST, s["pool_passed"])
                pool.sem_inc(s["o_free"], 1)

            pairs(pool, body)

        @block.tensor
        def _(pe):
            def turn(e):
                pe.wait_ge(s["gathered"], e * (16 * ST) + 16 * ST)
                for c in range(C):
                    for t in range(ST):
                        mm = pe.transpose(ps[:, 2 * c + t // GT, (t % GT) * P:(t % GT + 1) * P],
                                          xe[:, t, c * P:(c + 1) * P], ident[:])
                    mm.then_inc(s["turned"], 1)
                    yield c

            for c in turn(0):
                pass

            fuller = load_fuller(pe)

            def body(i, u, last):
                e = i * 2 + u

                def expert(width):
                    for hc in range(C):
                        if hc == 0:
                            pe.wait_ge(s["raw_split"], e * 3 + 2)
                            pe.wait_ge(s["xT_split"], e * C + C)
                            pe.wait_ge(s["o_ready"], e * ST + 1)
                        elif hc == 1:
                            pe.wait_ge(s["o_ready"], e * ST + ST)
                        else:
                            pe.wait_ge(s["gated"], e * (2 * C) + 2 * (hc - 1))
                        for m in range(2):
                            for h, cut in enumerate(pieces(width)):
                                for d in range(C):
                                    mm = matmul(pe, ps[:, 4 * (hc % 2) + 2 * m + h, 0:cut.stop - cut.start],
                                                tuple(w[:, d, hc * P:(hc + 1) * P] for w in W[u][m]),
                                                tuple(x[:, d, cut] for x in xT), d == 0, d == C - 1)
                        mm.then_inc(s["h_made"], 1)
                    if not (last and u):
                        steps = turn(e + 1)
                        pe.wait_ge(s["gated"], e * (2 * C) + 2 * C - 2)
                        next(steps)
                        next(steps)
                        pe.wait_ge(s["gated"], e * (2 * C) + 2 * C)
                        for _ in steps:
                            pass
                    else:
                        pe.wait_ge(s["gated"], e * (2 * C) + 2 * C - 2)
                    pe.wait_ge(s["raw_split"], e * 3 + (4 if not (last and u) else 3))
                    for t, rows, stands_for in tiles_of(width):
                        if not (last and u) and t in turned_before:
                            pe.wait_ge(s["xT_split"], e * C + C + turned_before[t])
                        for hc in range(C):
                            if t == 0:
                                pe.wait_ge(s["g_split"], e * (2 * C) + 2 * hc + 2)
                            mm = matmul(pe, ps[0:rows, o_bank[t], :], tuple(g[:, hc, t * P:t * P + rows] for g in gs),
                                        tuple(w[:, hc, :] for w in W2), hc == 0, hc == C - 1)
                        mm.then_inc(s["o_made"], stands_for)

                by_width(pe, fuller, i, u, expert)

            pairs(pe, body)

        @block.scalar
        def _(act):
            def split_weight(m, dst, value):
                act.wait_ge(raw_loaded[m], value)
                act.copy(dst[0][:], raw[m][:]).then_inc(s["raw_hi"], 1)

            def turn_copy(e, chunks):
                for c in chunks:
                    act.wait_ge(s["turned"], e * C + c + 1)
                    act.copy(xT[0][:, c, :], ps[:, 2 * c:2 * c + 2, :].rearrange("p k n -> p (k n)")[:, 0:CAP]
                             ).then_inc(s["xT_hi"], 1)

            turn_copy(0, range(C))
            fuller = load_fuller(act)

            def body(i, u, last):
                e = i * 2 + u

                def expert(width):
                    cuts = pieces(width)
                    by = 2 // len(cuts)
                    for hc in range(C):
                        act.wait_ge(s["h_made"], e * C + hc + 1)
                        for h, cut in enumerate(cuts):
                            act.activation(sil[:, cut], ps[:, 4 * (hc % 2) + h, 0:cut.stop - cut.start], ACT.Silu
                                           ).then_inc(s["silu_made"], by)
                        if hc == C - 1 and not (last and u):
                            turn_copy(e + 1, [0])
                        for h, cut in enumerate(cuts):
                            act.wait_ge(s["gated"], e * (2 * C) + 2 * hc + (h + 1) * by)
                            act.copy(gs[0][:, hc, cut], gate[:, hc % 2, cut]).then_inc(s["gate_hi"], by)
                        if hc == 1:
                            split_weight(2, W2, e * 16 + 16)
                        elif hc < 3 and not (last and u):
                            split_weight(hc // 2, W[1 - u][hc // 2], e * 16 + 32)
                    if not (last and u):
                        turn_copy(e + 1, range(1, C))

                by_width(act, fuller, i, u, expert)

            pairs(act, body)

        @block.vector
        def _(dve):
            def split_weight(m, dst, count):
                dve.wait_ge(s["raw_hi"], count)
                dve.tensor_tensor(dst[1][:], raw[m][:], dst[0][:].bitcast(F32), ALU.subtract
                                  ).then_inc(s["raw_split"], 1)

            def turn_split(e, chunks):
                for c in chunks:
                    dve.wait_ge(s["xT_hi"], e * C + c + 1)
                    dve.tensor_tensor(xT[1][:, c, :], ps[:, 2 * c:2 * c + 2, :].rearrange("p k n -> p (k n)")[:, 0:CAP],
                                      xT[0][:, c, :].bitcast(F32), ALU.subtract).then_inc(s["xT_split"], 1)

            turn_split(0, range(C))
            dve.sem_inc(s["o_ready"], ST)
            fuller = load_fuller(dve)

            def body(i, u, last):
                e = i * 2 + u

                def expert(width):
                    cuts = pieces(width)
                    by = 2 // len(cuts)
                    if not (last and u):
                        ahead.ids(dve, e + 1, 1 - u)
                    for hc in range(C):
                        if hc >= 2:
                            dve.wait_ge(s["g_split"], e * (2 * C) + 2 * (hc - 1))
                        for h, cut in enumerate(cuts):
                            dve.wait_ge(s["silu_made"], e * (2 * C) + 2 * hc + (h + 1) * by)
                            dve.tensor_tensor(gate[:, hc % 2, cut], ps[:, 4 * (hc % 2) + 2 + h, 0:cut.stop - cut.start],
                                              sil[:, cut], ALU.mult).then_inc(s["gated"], by)
                        if hc == C - 1 and not (last and u):
                            turn_split(e + 1, [0])
                        for h, cut in enumerate(cuts):
                            dve.wait_ge(s["gate_hi"], e * (2 * C) + 2 * hc + (h + 1) * by)
                            dve.tensor_tensor(gs[1][:, hc, cut], gate[:, hc % 2, cut], gs[0][:, hc, cut].bitcast(F32),
                                              ALU.subtract).then_inc(s["g_split"], by)
                        if hc == 0 and not (last and u):
                            split_weight(0, W[1 - u][0], e * 3 + 3)
                        elif hc == 1:
                            split_weight(2, W2, e * 3 + (4 if not (last and u) else 3))
                    if not (last and u):
                        turn_split(e + 1, range(1, C))
                        split_weight(1, W[1 - u][1], e * 3 + 5)
                    wait_alone(dve, s["o_free"], e + 1, s["dve_passed"])
                    dve.tensor_copy(add_ids[:], slots[:, bass.ds(e, 1), :, 0].rearrange("p e t -> p (e t)"))
                    dve.tensor_copy(weight[:], slots[:, bass.ds(e, 1), :, 1].bitcast(F32).rearrange("p e t -> p (e t)")
                                    ).then_inc(s["weight_ready"], 1)
                    dve.wait_ge(s["weight_ready"], e + 1)
                    for t, rows, stands_for in tiles_of(width):
                        dve.wait_ge(s["o_made"], e * ST + t + 1)
                        dve.tensor_scalar(o[0:rows, t, :], ps[0:rows, o_bank[t], :], weight[0:rows, t:t + 1], None, ALU.mult
                                          ).then_inc(s["o_ready"], stands_for)

                by_width(dve, fuller, i, u, expert)

            pairs(dve, body)


_INS = ["x", "ctx_1024", "L0_xattn_Wq", "L0_xattn_Wk", "L0_xattn_Wv", "L0_xattn_Wcq", "L0_xattn_Wck", "L0_xattn_Wcv",
        "L0_xattn_gamma", "L0_xattn_beta", "L0_xattn_W1", "L0_xattn_b1", "L0_ffn_wg", "L0_ffn_w1", "L0_ffn_w2",
        "L0_ffn_w3", "L0_ffn_sw1", "L0_ffn_sw2", "L0_ffn_sw3"]


def kernel(**inputs):
    import concourse.bacc as bacc
    from concourse.bass_utils import run_bass_kernel_spmd

    nc = bacc.Bacc("TRN2", target_bir_lowering=False, num_devices=1)
    arrays, args = {}, []
    for name in _INS:
        a = np.ascontiguousarray(inputs[name])
        arrays[f"in_{name}"] = a
        args.append(nc.dram_tensor(f"in_{name}", a.shape, mybir.dt.from_np(a.dtype), kind="ExternalInput").ap())
    out = nc.dram_tensor("out_0", (N, D), F32, kind="ExternalOutput").ap()
    kernel_program(nc, *args, out)
    r = run_bass_kernel_spmd(nc, [arrays], core_ids=[0])
    return r.results[0]["out_0"].reshape(B, S, D)
```
